# Optimizing a Trainium2 kernel written in Bass

```python
import numpy as np
import jax
import jax.numpy as jnp

def _softmax(x, axis=-1):
    return jax.nn.softmax(x, axis=axis)

def _gelu(x):
    return jax.nn.gelu(x, approximate=True)

def _silu(x):
    return jax.nn.silu(x)

def _sigmoid(x):
    return jax.nn.sigmoid(x)

def _layernorm(x, axis=-1, eps=1e-05):
    m = jnp.mean(x, axis=axis, keepdims=True)
    v = jnp.var(x, axis=axis, keepdims=True)
    return (x - m) / jnp.sqrt(v + eps)

def _scatter_add(tgt, idx, src, axis=0):
    return tgt.at[idx].add(src)

def _segment_sum(src, seg, n):
    return jax.ops.segment_sum(src, seg, n)
kernel_name = 'mk_decoder_postln_d2_seqx_r4_36948b'

def setup_inputs(seed: int=0):
    np.random.seed(seed)
    _w = jnp.asarray

    def _rec_inputs():
        import jax
        import jax.numpy as jnp
        _rk = jax.random.key(seed)
        x = 7.22e-05 + 1 * jax.random.normal(jax.random.fold_in(_rk, 1), (8, 112, 256), jnp.float32)
        _lenS = 112 - jax.random.randint(jax.random.fold_in(_rk, 7), (8,), 0, max(1, 112 // 4) + 1, jnp.int32)
        _lenS2 = 375 - jax.random.randint(jax.random.fold_in(_rk, 8), (8,), 0, max(1, 375 // 4) + 1, jnp.int32)
        _ctx_768P = jax.random.normal(jax.random.fold_in(_rk, 11), (8, 16, 192), jnp.float32)
        _ctx_768c = jax.random.dirichlet(jax.random.fold_in(_rk, 511), 0.3 * jnp.ones((16,), jnp.float32), (8, 375))
        _ctx_768t = jnp.einsum('bsk,bkd->bsd', _ctx_768c, _ctx_768P)
        _ctx_768t = _ctx_768t * jax.lax.rsqrt(jnp.mean(jnp.square(_ctx_768t)) + 1e-12) * 0.953939
        ctx_768 = 2.09791e-05 + 1.00001 * (_ctx_768t + 0.3 * jax.random.normal(jax.random.fold_in(_rk, 611), (8, 375, 192), jnp.float32))
        return (x, ctx_768)
    x, ctx_768 = _rec_inputs()

    def _L0_attn_setup():
        import jax, jax.numpy as jnp
        import numpy as np
        from jax import lax
        D_MODEL = 256
        D_STATE = 64
        HEADDIM = 64
        EXPAND = 2
        D_INNER = EXPAND * D_MODEL
        NHEADS = D_INNER // HEADDIM
        ROPE_FRACTION = min(0.5, HEADDIM / D_STATE)
        ROPE_DIM = int(ROPE_FRACTION * D_STATE)
        key = jax.random.key(seed)
        ks = jax.random.split(key, 8)
        B, L = (2, 512)
        d_in_proj = 2 * D_INNER + 2 * D_STATE + NHEADS
        x = jax.random.normal(ks[0], (B, L, D_MODEL), dtype=jnp.float32)
        W_in = jax.random.normal(ks[1], (D_MODEL, d_in_proj), dtype=jnp.float32) * 0.02
        W_out = jax.random.normal(ks[2], (D_INNER, D_MODEL), dtype=jnp.float32) * 0.02
        dt_bias = jax.random.normal(ks[3], (NHEADS,), dtype=jnp.float32) * 0.1
        A_log = jnp.log(jax.random.uniform(ks[4], (NHEADS,), minval=1.0, maxval=16.0, dtype=jnp.float32))
        D_skip = jnp.ones((NHEADS,), dtype=jnp.float32)
        norm_weight = jnp.ones((D_INNER,), dtype=jnp.float32)
        return {'x': x, 'W_in': W_in, 'W_out': W_out, 'dt_bias': dt_bias, 'A_log': A_log, 'D_skip': D_skip, 'norm_weight': norm_weight}
    _L0_attn_all = _L0_attn_setup()
    _L0_attn_in = {k: v for k, v in _L0_attn_all.items() if k in ('W_in', 'W_out', 'dt_bias', 'A_log', 'D_skip', 'norm_weight')}
    del _L0_attn_all

    def _L0_xattn_setup():
        import jax, jax.numpy as jnp
        import numpy as np
        HEADS = 16
        DIM_HEAD = 64
        key = jax.random.key(seed)
        ks = jax.random.split(key, 7)
        B, Nq, Dq = (4, 512, 256)
        Nk, Dc = (256, 192)
        inner = HEADS * DIM_HEAD
        sq = 1.0 / np.sqrt(Dq)
        sc = 1.0 / np.sqrt(Dc)
        si = 1.0 / np.sqrt(inner)
        return {'x': jax.random.normal(ks[0], (B, Nq, Dq), dtype=jnp.float32), 'context': jax.random.normal(ks[1], (B, Nk, Dc), dtype=jnp.float32), 'Wq': jax.random.normal(ks[2], (Dq, inner), dtype=jnp.float32) * sq, 'Wk': jax.random.normal(ks[3], (Dc, inner), dtype=jnp.float32) * sc, 'Wv': jax.random.normal(ks[4], (Dc, inner), dtype=jnp.float32) * sc, 'Wo': jax.random.normal(ks[5], (inner, Dq), dtype=jnp.float32) * si, 'bo': jax.random.normal(ks[6], (Dq,), dtype=jnp.float32) * 0.01}
    _L0_xattn_all = _L0_xattn_setup()
    _L0_xattn_in = {k: v for k, v in _L0_xattn_all.items() if k in ('Wq', 'Wk', 'Wv', 'Wo', 'bo')}
    del _L0_xattn_all

    def _L0_ffn_setup():
        import jax, jax.numpy as jnp
        import numpy as np
        TOP_K = 2
        key = jax.random.key(seed)
        kx, kg, k1, k2 = jax.random.split(key, 4)
        B, T, D, E, H = (4, 256, 256, 8, 512)
        x = jax.random.normal(kx, (B, T, D), dtype=jnp.float32)
        Wg = jax.random.normal(kg, (D, E), dtype=jnp.float32) * 0.02
        W1 = jax.random.normal(k1, (E, D, H), dtype=jnp.float32) * 0.02
        W2 = jax.random.normal(k2, (E, H, D), dtype=jnp.float32) * 0.02
        return {'x': x, 'Wg': Wg, 'W1': W1, 'W2': W2}
    _L0_ffn_all = _L0_ffn_setup()
    _L0_ffn_in = {k: v for k, v in _L0_ffn_all.items() if k in ('Wg', 'W1', 'W2')}
    del _L0_ffn_all

    def _L1_attn_setup():
        import jax, jax.numpy as jnp
        import numpy as np
        import math
        B, S, E = (2, 512, 256)
        H, DC, DR = (16, 64, 128)
        HD = E // H

        def _linear_params(key, din, dout):
            k1, k2 = jax.random.split(key)
            bound = 1.0 / math.sqrt(din)
            w = jax.random.uniform(k1, (din, dout), minval=-bound, maxval=bound, dtype=jnp.float32)
            b = jax.random.uniform(k2, (dout,), minval=-bound, maxval=bound, dtype=jnp.float32)
            return (w, b)

        def _gelu(x):
            return jax.nn.gelu(x, approximate=False)

        def _rope_cos_sin(seq_len, d_rope):
            inv_freq = 1.0 / 10000.0 ** (jnp.arange(0, d_rope, 2, dtype=jnp.float32) / d_rope)
            t = jnp.arange(seq_len, dtype=jnp.float32)
            freqs = t[:, None] * inv_freq[None, :]
            emb = jnp.concatenate([freqs, freqs], axis=-1)
            return (jnp.cos(emb), jnp.sin(emb))

        def _apply_rope(x, cos, sin):
            d = x.shape[-1]
            x1, x2 = (x[..., :d // 2], x[..., d // 2:])
            rot = jnp.concatenate([-x2, x1], axis=-1)
            return x * cos + rot * sin
        key = jax.random.key(seed)
        ks = jax.random.split(key, 10)
        x = jax.random.normal(ks[0], (B, S, E), dtype=jnp.float32)
        wq, bq = _linear_params(ks[1], E, DC)
        wqc, bqc = _linear_params(ks[2], DC, E - DR)
        wqr, bqr = _linear_params(ks[3], E, DR)
        wkv, bkv = _linear_params(ks[4], E, DC)
        wkr, bkr = _linear_params(ks[5], E, DR)
        wkc, bkc = _linear_params(ks[6], DC, E - DR)
        wv, bv = _linear_params(ks[7], DC, E)
        wo, bo = _linear_params(ks[8], E, E)
        return dict(x=x, wq=wq, bq=bq, wqc=wqc, bqc=bqc, wqr=wqr, bqr=bqr, wkv=wkv, bkv=bkv, wkr=wkr, bkr=bkr, wkc=wkc, bkc=bkc, wv=wv, bv=bv, wo=wo, bo=bo)
    _L1_attn_all = _L1_attn_setup()
    _L1_attn_in = {k: v for k, v in _L1_attn_all.items() if k in ('wq', 'bq', 'wqc', 'bqc', 'wqr', 'bqr', 'wkv', 'bkv', 'wkr', 'bkr', 'wkc', 'bkc', 'wv', 'bv', 'wo', 'bo')}
    del _L1_attn_all

    def _L1_xattn_setup():
        import jax, jax.numpy as jnp
        import numpy as np
        NUM_HEADS = 8
        DIM_HEAD = 128
        SCALE = DIM_HEAD ** (-0.25)
        key = jax.random.key(seed)
        ks = jax.random.split(key, 7)
        B, Tq, Dq = (8, 1024, 256)
        Tk, Dc = (256, 192)
        inner = NUM_HEADS * DIM_HEAD
        s = lambda d: 1.0 / np.sqrt(d)
        return {'x': jax.random.normal(ks[0], (B, Tq, Dq), jnp.float32), 'context': jax.random.normal(ks[1], (B, Tk, Dc), jnp.float32), 'Wq': jax.random.normal(ks[2], (Dq, inner), jnp.float32) * s(Dq), 'Wk': jax.random.normal(ks[3], (Dc, inner), jnp.float32) * s(Dc), 'Wv': jax.random.normal(ks[4], (Dc, inner), jnp.float32) * s(Dc), 'Wo': jax.random.normal(ks[5], (inner, Dq), jnp.float32) * s(inner), 'bo': jnp.zeros((Dq,), jnp.float32)}
    _L1_xattn_all = _L1_xattn_setup()
    _L1_xattn_in = {k: v for k, v in _L1_xattn_all.items() if k in ('Wq', 'Wk', 'Wv', 'Wo', 'bo')}
    del _L1_xattn_all

    def _L1_ffn_setup():
        import jax, jax.numpy as jnp
        import numpy as np
        B, S, IN, OUT, E, R = (8, 1024, 256, 256, 8, 8)
        LORA_ALPHA = 16
        SCALING = LORA_ALPHA / R
        key = jax.random.key(seed)
        k = jax.random.split(key, 6)
        x = jax.random.normal(k[0], (B, S, IN), dtype=jnp.float32)
        base_w = jax.random.normal(k[1], (OUT, IN), dtype=jnp.float32) * 0.02
        base_b = jnp.zeros((OUT,), dtype=jnp.float32)
        lora_A = jax.random.normal(k[2], (IN, R), dtype=jnp.float32) * 0.02
        lora_B = jax.random.normal(k[3], (E, R, OUT), dtype=jnp.float32) * 0.02
        router_w = jax.random.normal(k[4], (E, IN), dtype=jnp.float32) * 0.02
        router_b = jnp.zeros((E,), dtype=jnp.float32)
        return {'x': x, 'base_w': base_w, 'base_b': base_b, 'lora_A': lora_A, 'lora_B': lora_B, 'router_w': router_w, 'router_b': router_b}
    _L1_ffn_all = _L1_ffn_setup()
    _L1_ffn_in = {k: v for k, v in _L1_ffn_all.items() if k in ('base_w', 'base_b', 'lora_A', 'lora_B', 'router_w', 'router_b')}
    del _L1_ffn_all
    return {'x': x, 'ctx_768': ctx_768, 'L0_attn_W_in': _L0_attn_in['W_in'], 'L0_attn_W_out': _L0_attn_in['W_out'], 'L0_attn_dt_bias': _L0_attn_in['dt_bias'], 'L0_attn_A_log': _L0_attn_in['A_log'], 'L0_attn_D_skip': _L0_attn_in['D_skip'], 'L0_attn_norm_weight': _L0_attn_in['norm_weight'], 'L0_xattn_Wq': _L0_xattn_in['Wq'], 'L0_xattn_Wk': _L0_xattn_in['Wk'], 'L0_xattn_Wv': _L0_xattn_in['Wv'], 'L0_xattn_Wo': _L0_xattn_in['Wo'], 'L0_xattn_bo': _L0_xattn_in['bo'], 'L0_ffn_Wg': _L0_ffn_in['Wg'], 'L0_ffn_W1': _L0_ffn_in['W1'], 'L0_ffn_W2': _L0_ffn_in['W2'], 'L1_attn_wq': _L1_attn_in['wq'], 'L1_attn_bq': _L1_attn_in['bq'], 'L1_attn_wqc': _L1_attn_in['wqc'], 'L1_attn_bqc': _L1_attn_in['bqc'], 'L1_attn_wqr': _L1_attn_in['wqr'], 'L1_attn_bqr': _L1_attn_in['bqr'], 'L1_attn_wkv': _L1_attn_in['wkv'], 'L1_attn_bkv': _L1_attn_in['bkv'], 'L1_attn_wkr': _L1_attn_in['wkr'], 'L1_attn_bkr': _L1_attn_in['bkr'], 'L1_attn_wkc': _L1_attn_in['wkc'], 'L1_attn_bkc': _L1_attn_in['bkc'], 'L1_attn_wv': _L1_attn_in['wv'], 'L1_attn_bv': _L1_attn_in['bv'], 'L1_attn_wo': _L1_attn_in['wo'], 'L1_attn_bo': _L1_attn_in['bo'], 'L1_xattn_Wq': _L1_xattn_in['Wq'], 'L1_xattn_Wk': _L1_xattn_in['Wk'], 'L1_xattn_Wv': _L1_xattn_in['Wv'], 'L1_xattn_Wo': _L1_xattn_in['Wo'], 'L1_xattn_bo': _L1_xattn_in['bo'], 'L1_ffn_base_w': _L1_ffn_in['base_w'], 'L1_ffn_base_b': _L1_ffn_in['base_b'], 'L1_ffn_lora_A': _L1_ffn_in['lora_A'], 'L1_ffn_lora_B': _L1_ffn_in['lora_B'], 'L1_ffn_router_w': _L1_ffn_in['router_w'], 'L1_ffn_router_b': _L1_ffn_in['router_b']}

def reference(x, ctx_768, L0_attn_W_in, L0_attn_W_out, L0_attn_dt_bias, L0_attn_A_log, L0_attn_D_skip, L0_attn_norm_weight, L0_xattn_Wq, L0_xattn_Wk, L0_xattn_Wv, L0_xattn_Wo, L0_xattn_bo, L0_ffn_Wg, L0_ffn_W1, L0_ffn_W2, L1_attn_wq, L1_attn_bq, L1_attn_wqc, L1_attn_bqc, L1_attn_wqr, L1_attn_bqr, L1_attn_wkv, L1_attn_bkv, L1_attn_wkr, L1_attn_bkr, L1_attn_wkc, L1_attn_bkc, L1_attn_wv, L1_attn_bv, L1_attn_wo, L1_attn_bo, L1_xattn_Wq, L1_xattn_Wk, L1_xattn_Wv, L1_xattn_Wo, L1_xattn_bo, L1_ffn_base_w, L1_ffn_base_b, L1_ffn_lora_A, L1_ffn_lora_B, L1_ffn_router_w, L1_ffn_router_b):
    import jax
    import jax.numpy as jnp

    def _L0_attn_ref(x, W_in, W_out, dt_bias, A_log, D_skip, norm_weight):
        import jax, jax.numpy as jnp
        import numpy as np
        from jax import lax
        D_MODEL = 256
        D_STATE = 64
        HEADDIM = 64
        EXPAND = 2
        D_INNER = EXPAND * D_MODEL
        NHEADS = D_INNER // HEADDIM
        ROPE_FRACTION = min(0.5, HEADDIM / D_STATE)
        ROPE_DIM = int(ROPE_FRACTION * D_STATE)
        Bsz, L, _ = x.shape
        H, P, N = (NHEADS, HEADDIM, D_STATE)
        pairs = ROPE_DIM // 2
        zxbcdt = x @ W_in
        z = zxbcdt[..., :D_INNER]
        xs = zxbcdt[..., D_INNER:2 * D_INNER].reshape(Bsz, L, H, P)
        Bm = zxbcdt[..., 2 * D_INNER:2 * D_INNER + N]
        Cm = zxbcdt[..., 2 * D_INNER + N:2 * D_INNER + 2 * N]
        dt = jax.nn.softplus(zxbcdt[..., 2 * D_INNER + 2 * N:] + dt_bias)
        decay = jnp.exp(-jnp.exp(A_log) * dt)
        inv_freq = 1.0 / 10000.0 ** (jnp.arange(pairs, dtype=jnp.float32) / pairs)
        angle = dt[..., None] * inv_freq
        cos, sin = (jnp.cos(angle), jnp.sin(angle))

        def step(h, inp):
            dt_t, dec_t, B_t, C_t, x_t, cos_t, sin_t = inp
            hr = h[:, :, :ROPE_DIM, :].reshape(Bsz, H, pairs, 2, P)
            h1, h2 = (hr[..., 0, :], hr[..., 1, :])
            c, s = (cos_t[..., None], sin_t[..., None])
            rot = jnp.stack([c * h1 - s * h2, s * h1 + c * h2], axis=-2)
            h_rot = jnp.concatenate([rot.reshape(Bsz, H, ROPE_DIM, P), h[:, :, ROPE_DIM:, :]], axis=2)
            h_new = dec_t[..., None, None] * h_rot + dt_t[..., None, None] * B_t[:, None, :, None] * x_t[:, :, None, :]
            y_t = jnp.einsum('bhnp,bn->bhp', h_new, C_t)
            return (h_new, y_t)
        h0 = jnp.zeros((Bsz, H, N, P), x.dtype)
        lfirst = lambda a: jnp.moveaxis(a, 1, 0)
        inputs = (lfirst(dt), lfirst(decay), lfirst(Bm), lfirst(Cm), lfirst(xs), lfirst(cos), lfirst(sin))
        _, ys = lax.scan(step, h0, inputs)
        y = jnp.moveaxis(ys, 0, 1) + D_skip[None, None, :, None] * xs
        y = y.reshape(Bsz, L, D_INNER)
        y = y * jax.nn.silu(z)
        y = y * lax.rsqrt(jnp.mean(y * y, axis=-1, keepdims=True) + 1e-05) * norm_weight
        return y @ W_out

    def _L0_xattn_ref(x, context, Wq, Wk, Wv, Wo, bo):
        import jax, jax.numpy as jnp
        import numpy as np
        HEADS = 16
        DIM_HEAD = 64
        B, Nq, _ = x.shape
        Nk = context.shape[1]
        h, dh = (HEADS, DIM_HEAD)
        q = (x @ Wq).reshape(B, Nq, h, dh)
        k = (context @ Wk).reshape(B, Nk, h, dh)
        v = (context @ Wv).reshape(B, Nk, h, dh)
        scale = 1.0 / jnp.sqrt(jnp.asarray(dh, dtype=x.dtype))
        scores = jnp.einsum('bqhd,bkhd->bhqk', q, k) * scale
        attn = jax.nn.softmax(scores, axis=-1)
        out = jnp.einsum('bhqk,bkhd->bqhd', attn, v).reshape(B, Nq, h * dh)
        return out @ Wo + bo

    def _L0_ffn_ref(x, Wg, W1, W2):
        import jax, jax.numpy as jnp
        import numpy as np
        TOP_K = 2
        B, T, D = x.shape
        E = W1.shape[0]
        logits = jnp.einsum('btd,de->bte', x, Wg)
        probs = jax.nn.softmax(logits, axis=-1)
        top_w, top_i = jax.lax.top_k(probs, TOP_K)
        top_w = top_w / (jnp.sum(top_w, axis=-1, keepdims=True) + 1e-08)
        N = B * T
        oh = jax.nn.one_hot(top_i.reshape(N, TOP_K), E, dtype=x.dtype)
        combine = jnp.sum(oh * top_w.reshape(N, TOP_K)[..., None], axis=1)
        xt = x.reshape(N, D)
        h = jnp.einsum('td,edh->teh', xt, W1)
        h = jnp.square(jax.nn.relu(h))
        y = jnp.einsum('teh,ehd->ted', h, W2)
        out = jnp.einsum('te,ted->td', combine, y)
        return out.reshape(B, T, D)

    def _L1_attn_ref(x, wq, bq, wqc, bqc, wqr, bqr, wkv, bkv, wkr, bkr, wkc, bkc, wv, bv, wo, bo):
        import jax, jax.numpy as jnp
        import numpy as np
        import math
        B, S, E = (2, 512, 256)
        H, DC, DR = (16, 64, 128)
        HD = E // H

        def _linear_params(key, din, dout):
            k1, k2 = jax.random.split(key)
            bound = 1.0 / math.sqrt(din)
            w = jax.random.uniform(k1, (din, dout), minval=-bound, maxval=bound, dtype=jnp.float32)
            b = jax.random.uniform(k2, (dout,), minval=-bound, maxval=bound, dtype=jnp.float32)
            return (w, b)

        def _gelu(x):
            return jax.nn.gelu(x, approximate=False)

        def _rope_cos_sin(seq_len, d_rope):
            inv_freq = 1.0 / 10000.0 ** (jnp.arange(0, d_rope, 2, dtype=jnp.float32) / d_rope)
            t = jnp.arange(seq_len, dtype=jnp.float32)
            freqs = t[:, None] * inv_freq[None, :]
            emb = jnp.concatenate([freqs, freqs], axis=-1)
            return (jnp.cos(emb), jnp.sin(emb))

        def _apply_rope(x, cos, sin):
            d = x.shape[-1]
            x1, x2 = (x[..., :d // 2], x[..., d // 2:])
            rot = jnp.concatenate([-x2, x1], axis=-1)
            return x * cos + rot * sin
        b, s, _ = x.shape
        cq = _gelu(x @ wq + bq)
        q_c = cq @ wqc + bqc
        q_r = x @ wqr + bqr
        ckv = _gelu(x @ wkv + bkv)
        k_r = x @ wkr + bkr
        k_c = ckv @ wkc + bkc
        v = (ckv @ wv + bv).reshape(b, s, H, HD).transpose(0, 2, 1, 3)
        cos, sin = _rope_cos_sin(s, DR)
        q_r = _apply_rope(q_r, cos, sin)
        k_r = _apply_rope(k_r, cos, sin)
        q = _gelu(jnp.concatenate([q_c, q_r], axis=-1)).reshape(b, s, H, HD).transpose(0, 2, 1, 3)
        k = _gelu(jnp.concatenate([k_c, k_r], axis=-1)).reshape(b, s, H, HD).transpose(0, 2, 1, 3)
        scale = 1.0 / math.sqrt(HD)
        scores = jnp.einsum('bhqd,bhkd->bhqk', q, k) * scale
        causal = jnp.triu(jnp.ones((s, s), dtype=bool), k=1)
        scores = jnp.where(causal[None, None], -jnp.inf, scores)
        attn = jax.nn.softmax(scores, axis=-1)
        out = jnp.einsum('bhqk,bhkd->bhqd', attn, v)
        out = out.transpose(0, 2, 1, 3).reshape(b, s, E)
        return out @ wo + bo

    def _L1_xattn_ref(x, context, Wq, Wk, Wv, Wo, bo):
        import jax, jax.numpy as jnp
        import numpy as np
        NUM_HEADS = 8
        DIM_HEAD = 128
        SCALE = DIM_HEAD ** (-0.25)
        B, Tq, _ = x.shape
        Tk = context.shape[1]
        h, C = (NUM_HEADS, DIM_HEAD)
        q = (x @ Wq).reshape(B, Tq, h, C) * SCALE
        k = (context @ Wk).reshape(B, Tk, h, C) * SCALE
        v = (context @ Wv).reshape(B, Tk, h, C)
        attn = jax.nn.softmax(jnp.einsum('bqhc,bkhc->bhqk', q, k), axis=-1)
        out = jnp.einsum('bhqk,bkhc->bqhc', attn, v).reshape(B, Tq, h * C)
        return out @ Wo + bo

    def _L1_ffn_ref(x, base_w, base_b, lora_A, lora_B, router_w, router_b):
        import jax, jax.numpy as jnp
        import numpy as np
        B, S, IN, OUT, E, R = (8, 1024, 256, 256, 8, 8)
        LORA_ALPHA = 16
        SCALING = LORA_ALPHA / R
        result = jnp.einsum('bsd,od->bso', x, base_w) + base_b
        logits = jnp.einsum('bsd,ed->bse', x, router_w) + router_b
        gating = jax.nn.softmax(logits, axis=-1).astype(jnp.bfloat16)
        mid = jnp.einsum('bsd,dr->bsr', x, lora_A)
        lora_out = jnp.einsum('bsr,erd,bse->bsd', mid, lora_B, gating.astype(jnp.float32))
        return result + lora_out * SCALING
    x = _layernorm(x + _L0_attn_ref(x, L0_attn_W_in, L0_attn_W_out, L0_attn_dt_bias, L0_attn_A_log, L0_attn_D_skip, L0_attn_norm_weight), axis=-1)
    x = _layernorm(x + _L0_xattn_ref(x, ctx_768, L0_xattn_Wq, L0_xattn_Wk, L0_xattn_Wv, L0_xattn_Wo, L0_xattn_bo), axis=-1)
    x = _layernorm(x + _L0_ffn_ref(x, L0_ffn_Wg, L0_ffn_W1, L0_ffn_W2), axis=-1)
    x = _layernorm(x + _L1_attn_ref(x, L1_attn_wq, L1_attn_bq, L1_attn_wqc, L1_attn_bqc, L1_attn_wqr, L1_attn_bqr, L1_attn_wkv, L1_attn_bkv, L1_attn_wkr, L1_attn_bkr, L1_attn_wkc, L1_attn_bkc, L1_attn_wv, L1_attn_bv, L1_attn_wo, L1_attn_bo), axis=-1)
    x = _layernorm(x + _L1_xattn_ref(x, ctx_768, L1_xattn_Wq, L1_xattn_Wk, L1_xattn_Wv, L1_xattn_Wo, L1_xattn_bo), axis=-1)
    x = _layernorm(x + _L1_ffn_ref(x, L1_ffn_base_w, L1_ffn_base_b, L1_ffn_lora_A, L1_ffn_lora_B, L1_ffn_router_w, L1_ffn_router_b), axis=-1)
    return x

_drawn_inputs = setup_inputs


def setup_inputs(seed=0):
    import zlib

    import numpy as np

    out = dict(_drawn_inputs(seed))
    spreads = {'L0_attn_D_skip': (1.0, 0.2),
     'L0_attn_norm_weight': (1.0, 0.2),
     'L1_xattn_bo': (0.0, 0.1),
     'L1_ffn_base_b': (0.0, 0.1),
     'L1_ffn_router_b': (0.0, 0.8)}
    factors = {'L0_xattn_bo': 7.539,
     'L1_attn_wq': 8.0,
     'L1_attn_bq': 55.334,
     'L1_attn_wqc': 8.0,
     'L1_attn_bqc': 64.0,
     'L1_attn_wqr': 8.0,
     'L1_attn_bqr': 51.732,
     'L1_attn_bkv': 8.0,
     'L1_attn_wkr': 8.0,
     'L1_attn_bkr': 62.371,
     'L1_attn_wkc': 8.0,
     'L1_attn_bkc': 25.323,
     'L1_ffn_lora_A': 4.455,
     'L1_ffn_lora_B': 4.211,
     'L1_ffn_router_w': 8.0}
    for name, (base, spread) in spreads.items():
        noise = np.random.default_rng([zlib.crc32(name.encode()), seed]).standard_normal(out[name].shape)
        drawn = base * np.exp(spread * noise) if base else spread * noise
        out[name] = jnp.asarray(drawn.astype(out[name].dtype))
    for name, factor in factors.items():
        out[name] = (out[name] * factor).astype(out[name].dtype)
    return out
```

```python
from contextlib import ExitStack

import numpy as np

import concourse.bass as bass
from concourse import mybir

F32 = mybir.dt.float32
F32R = mybir.dt.float32r
BF16 = mybir.dt.bfloat16
ALU = mybir.AluOpType
ACT = mybir.ActivationFunctionType
AX_X = mybir.AxisListType.X
EXP_LN = "natural_log_exp_and_others"

B, T, D = 8, 112, 256
N = B * T
S, DC = 375, 192
KD = D // 128
ST, SP_ = 3, S // 3
SE = S + 1
CB = DC - 128
EPS = 1e-5
H0, P0, NS, PAIRS = 8, 64, 64, 16
DI = H0 * P0
W_IN = 2 * DI + 2 * NS + H0
ROUND = 1.5 * 2.0 ** 23
TURN = 6.2831850
INNER = 1024
E0, F0, FM = 8, 512, 4
H1, HD1, R1 = 16, 16, 128
E1, RK = 8, 8

C_ID = 0
C_TRI = C_ID + 128
C_AFTER = C_TRI + T
C_CAUSAL = C_AFTER + T
C_COS = C_CAUSAL + T
C_SIN = C_COS + T
C_FREQ = C_SIN + T
C_HEAD = C_FREQ + PAIRS
C_PRIO = C_HEAD + 8
C_ONE = C_PRIO + E0
C_EPS = C_ONE + 128
C_END = C_EPS + 1

R_DTB, R_ALOG, R_DSKIP = 0, H0, 2 * H0
R_END = 3 * H0


def constants():
    c = np.zeros((128, C_END), np.float32)
    r = np.arange(T)
    c[:, C_ID:C_ID + 128] = np.eye(128)
    c[:T, C_TRI:C_TRI + T] = r[:, None] <= r[None, :]
    c[:T, C_AFTER:C_AFTER + T] = r[:, None] > r[None, :]
    c[:T, C_CAUSAL:C_CAUSAL + T] = np.where(r[None, :] > r[:, None], -1e30, 0.0)
    freq = (1.0 / np.float32(10000.0) ** (np.arange(0, R1, 2, dtype=np.float32) / np.float32(R1))).astype(np.float32)
    angle = (r.astype(np.float32)[None, :] * np.concatenate([freq, freq])[:, None]).astype(np.float32)
    c[:, C_COS:C_COS + T] = np.cos(angle)
    sign = np.where(np.arange(R1) < R1 // 2, -1.0, 1.0)
    c[:, C_SIN:C_SIN + T] = np.sin(angle) * sign[:, None]
    inv = 1.0 / np.float32(10000.0) ** (np.arange(PAIRS, dtype=np.float32) / np.float32(PAIRS))
    c[:, C_FREQ:C_FREQ + PAIRS] = inv.astype(np.float64) / (2 * np.pi)
    c[:, C_HEAD:C_HEAD + 8] = (np.arange(128) // HD1)[:, None] == np.arange(8)[None, :]
    c[:, C_PRIO:C_PRIO + E0] = E0 - np.arange(E0)
    c[:, C_ONE:C_ONE + 128] = 1.0
    c[:, C_EPS] = EPS
    return c


def accumulate(pe, out, pairs):
    last = None
    for k, (lhs, rhs) in enumerate(pairs):
        last = pe.matmul(out, lhs, rhs, start=(k == 0), stop=(k == len(pairs) - 1))
    return last


def split_products(lhs_high, lhs_low, rhs_high, rhs_low):
    return [(lhs_high, rhs_high), (lhs_high, rhs_low), (lhs_low, rhs_high)]


def exact_products(lhs, rhs):
    return [(lhs["high"], rhs["high"]), (lhs["high"], rhs["low"]), (lhs["low"], rhs["high"]),
            (lhs["rest"], rhs["rest"]), (lhs["last"], rhs["last"])]


def wait_past(eng, sem, value):
    if not isinstance(value, int) or value > 0:
        eng.wait_ge(sem, value)


class Chain:

    def __init__(self, eng, sem, links):
        self.eng, self.sem, self.links, self.item, self.done = eng, sem, links, 0, links

    def start(self, item):
        assert self.done == self.links, f"{self.sem.name}: {self.done} links"
        self.item, self.done = item, 0

    def link(self, ins):
        self.done += 1
        ins.then_inc(self.sem, 1)
        self.eng.wait_ge(self.sem, self.item * self.links + self.done)


def skewed(eng, front, back):
    front(0, 0)
    front(1, 1)
    back(0, 0)
    with eng.Fori(0, B // 2 - 1) as j:
        front(2 * j + 2, 0)
        back(2 * j + 1, 1)
        front(2 * j + 3, 1)
        back(2 * j + 2, 0)
    back(B - 1, 1)


def nothing(item, p):
    pass


class Core:

    def __init__(self, nc, ctx):
        self.nc = nc
        self.phase_sems = []
        sb = lambda name, shape: ctx.enter_context(nc.sbuf_tensor(name, shape, F32))
        self.x = sb("x", [T, B, D])
        self.xt = sb("xt", [128, KD, N])
        self.const = sb("const", [128, C_END])
        self.rows = sb("rows", [T, R_END])
        self.bank = [ctx.enter_context(nc.psum_tensor(f"bank{k}", [128, 512], F32)) for k in range(8)]
        self.loaded = ctx.enter_context(nc.semaphore("const_loaded"))
        self.wq, self.wk, self.wv = sb("wq", [128, KD, INNER]), sb("wk", [128, 2, INNER]), sb("wv", [128, 2, INNER])
        self.wo, self.bo = sb("wo", [128, INNER // 128, D]), sb("bo", [1, D])
        self.xw_loaded = ctx.enter_context(nc.semaphore("cross_weights_loaded"))

    def sem(self, name):
        self.phase_sems.append(self.nc.alloc_semaphore(name=name))
        return self.phase_sems[-1]

    def free_semaphores(self):
        self.nc.clear_and_free_semaphores(self.phase_sems)
        self.phase_sems = []
        self.nc.all_engine_barrier()

    def load_cross_weights(self, sp, d, layer):
        name = f"L{layer}_xattn_W"
        sp.dma_start(self.wk[:, :, :], d[name + "k"].rearrange("(c p) n -> p c n", p=128)).then_inc(self.xw_loaded, 16)
        sp.dma_start(self.wv[:, :, :], d[name + "v"].rearrange("(c p) n -> p c n", p=128)).then_inc(self.xw_loaded, 16)
        sp.dma_start(self.wq[:, :, :], d[name + "q"].rearrange("(c p) n -> p c n", p=128)).then_inc(self.xw_loaded, 16)
        sp.dma_start(self.wo[:, :, :], d[name + "o"].rearrange("(c p) n -> p c n", p=128)).then_inc(self.xw_loaded, 16)
        sp.dma_start(self.bo[:, :], d[f"L{layer}_bo"]).then_inc(self.xw_loaded, 16)

    def c(self, rows, start, width):
        return self.const[0:rows, start:start + width]


def project_time_and_gate(core, d, zs, dt, dta, cosine, sine):
    nc = core.nc
    bank = core.bank
    with ExitStack() as ctx:
        sb = lambda name, shape: ctx.enter_context(nc.sbuf_tensor(name, shape, F32))
        raw = sb("dt_raw", [T, B, H0])
        mag = sb("dt_mag", [T, B, H0])
        soft = sb("dt_soft", [T, B, H0])
        rate = sb("rate", [T, H0])
        turns = sb("turns", [T, B * H0, PAIRS])
        whole = sb("whole", [T, B * H0, PAIRS])
        sin_in = sb("sin_in", [T, B * H0, PAIRS])
        cos_in = sb("cos_in", [T, B * H0, PAIRS])
        x_loaded, w_loaded = core.sem("p1_x_loaded"), core.sem("p1_w_loaded")
        dt_ready, mag_ready, soft_ready = core.sem("dt_ready"), core.sem("dt_mag_ready"), core.sem("dt_soft_ready")
        rate_ready, steps_ready = core.sem("rate_ready"), core.sem("steps_ready")
        time_ready, z_ready, z_used = core.sem("time_ready"), core.sem("z_ready"), core.sem("z_used")
        angles_ready, act_chain, dve_chain = core.sem("angles_ready"), core.sem("p1_act"), core.sem("p1_dve")
        ZB = 4

        with nc.Block() as block:
            @block.sync
            def _(sp):
                sp.dma_start(core.xt[:, :, :], d["xt"].rearrange("(c p) n -> p c n", p=128)).then_inc(x_loaded, 16)
                sp.dma_start(core.w_in[:, :, :], d["L0_attn_W_in"].rearrange("(c p) n -> p c n", p=128)).then_inc(w_loaded, 16)
                sp.dma_start(core.const[:, :], d["const"]).then_inc(core.loaded, 16)
                sp.dma_start(core.rows[:, :], d["rows"]).then_inc(core.loaded, 16)

            @block.tensor
            def _(pe):
                def z(i):
                    if i >= ZB:
                        pe.wait_ge(z_used, i - ZB + 1)
                    accumulate(pe, bank[1 + i % ZB][0:T, :], [
                        (core.xt[:, c, i * T:(i + 1) * T], core.w_in[:, c, 0:DI]) for c in range(KD)]).then_inc(z_ready, 1)

                pe.wait_ge(x_loaded, 16)
                pe.wait_ge(w_loaded, 16)
                for i in range(B):
                    last = accumulate(pe, bank[0][0:T, i * H0:(i + 1) * H0], [
                        (core.xt[:, c, i * T:(i + 1) * T], core.w_in[:, c, W_IN - H0:W_IN]) for c in range(KD)])
                last.then_inc(dt_ready, 1)
                for i in range(ZB):
                    z(i)
                pe.wait_ge(core.loaded, 32)
                pe.wait_ge(steps_ready, 1)
                pe.matmul(bank[5][0:T, 0:B * H0], core.c(T, C_TRI, T), dt[:, :, :].rearrange("t b h -> t (b h)"),
                          start=True, stop=True).then_inc(time_ready, 1)
                for i in range(ZB, B):
                    z(i)

            @block.vector
            def _(dve):
                chain = Chain(dve, dve_chain, 6)
                chain.start(0)
                row = lambda k: core.rows[:, k:k + H0].unsqueeze(1).broadcast_to([T, B, H0])
                dve.wait_ge(core.loaded, 32)
                dve.wait_ge(dt_ready, 1)
                chain.link(dve.tensor_tensor(raw[:, :, :], bank[0][0:T, 0:B * H0].rearrange("t (b h) -> t b h", b=B),
                                             row(R_DTB), ALU.add))
                dve.scalar_tensor_tensor(mag[:, :, :], raw[:, :, :], -1.0, raw[:, :, :], ALU.mult, ALU.max).then_inc(mag_ready, 1)
                dve.wait_ge(soft_ready, 1)
                chain.link(dve.scalar_tensor_tensor(dt[:, :, :], raw[:, :, :], 0.0, soft[:, :, :], ALU.max, ALU.add))
                dve.wait_ge(rate_ready, 1)
                dve.scalar_tensor_tensor(dta[:, :, :], dt[:, :, :], -1.0, rate[:, :].unsqueeze(1).broadcast_to([T, B, H0]),
                                         ALU.mult, ALU.mult).then_inc(steps_ready, 1)
                dve.wait_ge(time_ready, 1)
                shape = [T, B * H0, PAIRS]
                chain.link(dve.tensor_tensor(turns[:, :, :], bank[5][0:T, 0:B * H0].unsqueeze(2).broadcast_to(shape),
                                             core.c(T, C_FREQ, PAIRS).unsqueeze(1).broadcast_to(shape), ALU.mult))
                chain.link(dve.tensor_scalar(whole[:, :, :], turns[:, :, :], ROUND, ROUND, ALU.add, ALU.subtract))
                chain.link(dve.tensor_tensor(sin_in[:, :, :], turns[:, :, :], whole[:, :, :], ALU.subtract))
                dve.tensor_scalar(cos_in[:, :, :], sin_in[:, :, :], 0.25, None, ALU.add)
                chain.link(dve.tensor_scalar(whole[:, :, :], sin_in[:, :, :], 0.25, 0.5, ALU.add, ALU.is_gt))
                dve.tensor_tensor(cos_in[:, :, :], cos_in[:, :, :], whole[:, :, :], ALU.subtract).then_inc(angles_ready, 1)

            @block.scalar
            def _(act):
                chain = Chain(act, act_chain, 1)
                chain.start(0)
                act.preload_act_table_set(EXP_LN)
                act.wait_ge(core.loaded, 32)
                act.activation(rate[:, :], core.rows[:, R_ALOG:R_ALOG + H0], ACT.Exp).then_inc(rate_ready, 1)
                act.wait_ge(mag_ready, 1)
                chain.link(act.activation(soft[:, :, :], mag[:, :, :], ACT.Exp, scale=-1.0))
                act.activation(soft[:, :, :], soft[:, :, :], ACT.Ln, bias=core.c(T, C_ONE, 1)).then_inc(soft_ready, 1)
                act.preload_act_table_set("silu_and_others")
                for i in range(B):
                    act.wait_ge(z_ready, i + 1)
                    act.activation(zs[:, i, :], bank[1 + i % ZB][0:T, :], ACT.Silu).then_inc(z_used, 1)
                act.wait_ge(angles_ready, 1)
                act.activation(sine[:, :, :], sin_in[:, :, :], ACT.Sin, scale=TURN)
                act.activation(cosine[:, :, :], cos_in[:, :, :], ACT.Sin, scale=TURN)


def state_space(core, d, zs, dt, dta, cosine, sine):
    nc = core.nc
    bank = core.bank
    with ExitStack() as ctx:
        sb = lambda name, shape: ctx.enter_context(nc.sbuf_tensor(name, shape, F32))
        pair = lambda name, shape: [sb(f"{name}{p}", shape) for p in range(2)]
        w_out = sb("w_out", [128, 4, D])
        w_norm = sb("w_norm", [128, 4])
        x_in, xt_in = pair("x_in", [T, D]), pair("xt_in", [128, KD, T])
        bc = sb("bc", [T, 2, NS])
        rot = pair("rot", [T, 2, H0, NS])
        prod = [sb(f"prod{k}", [T, 2, H0, PAIRS]) for k in range(4)]
        xs = sb("xs", [T, DI])
        xs_dt, xs_skip = pair("xs_dt", [T, DI]), pair("xs_skip", [T, DI])
        lower = sb("lower", [T, H0, T])
        decay = pair("decay", [T, H0, T])
        rot_t = sb("rot_t", [128, 2, 4, T])
        mix = sb("mix", [T, H0, T])
        y, y2, sq = sb("y", [T, DI]), sb("y2", [T, DI]), sb("sq", [T, DI])
        y_t = sb("y_t", [128, 4, T])
        ssq, rms = sb("ssq", [T, 1]), sb("rms", [T, 1])
        res, normed = sb("res", [T, D]), sb("normed", [T, D])
        stats, mv, rstd, pad = sb("stats", [T, 6]), sb("mv", [T, 2]), sb("rstd", [T, 1]), sb("pad", [T, 1])
        sem = lambda name: core.sem("ss_" + name)
        w_loaded, w_scaled = sem("w_loaded"), sem("w_scaled")
        x_loaded = [sem("x_loaded0"), sem("x_loaded1")]
        xs_ready, bc_ready, xs_copied, bc_copied = sem("xs_ready"), sem("bc_ready"), sem("xs_copied"), sem("bc_copied")
        lower_ready, logdecay_ready, exp_done, decay_ready = sem("lower_ready"), sem("logdecay_ready"), sem("exp_done"), sem("decay_ready")
        rot_copied, rot_ready, xdt_ready, skip_ready = sem("rot_copied"), sem("rot_ready"), sem("xdt_ready"), sem("skip_ready")
        turned, turned_copied = sem("turned"), sem("turned_copied")
        scores_ready, mix_ready, y_ready, y2_ready = sem("scores_ready"), sem("mix_ready"), sem("y_ready"), sem("y2_ready")
        yt_ready, yt_copied, rms_ready, out_ready = sem("yt_ready"), sem("yt_copied"), sem("rms_ready"), sem("out_ready")
        var_ready, rstd_ready, normed_ready, nt_ready, nt_copied = (
            sem("var_ready"), sem("rstd_ready"), sem("normed_ready"), sem("nt_ready"), sem("nt_copied"))
        front_chain, back_chain, act_chain = sem("dve_front"), sem("dve_back"), sem("act")

        with nc.Block() as block:
            @block.sync
            def _(sp):
                sp.dma_start(w_out[:, :, :], d["L0_attn_W_out"].rearrange("(c p) n -> p c n", p=128)).then_inc(w_loaded, 16)
                sp.dma_start(w_norm[:, :], d["norm_w"]).then_inc(w_loaded, 16)

                def load(i, p, k):
                    wait_past(sp, xs_ready, i - 1)
                    wait_past(sp, logdecay_ready, i - 1)
                    wait_past(sp, var_ready, i - 1)
                    sp.dma_start(xt_in[p][:, :, :], d["xt_items"][i].rearrange("(c p) n -> p c n", p=128)).then_inc(x_loaded[p], 16)
                    sp.dma_start(x_in[p][:, :], d["x"][i]).then_inc(x_loaded[p], 16)

                load(0, 0, 0)
                load(1, 1, 0)
                core.load_cross_weights(sp, d, 0)
                with sp.Fori(1, B // 2) as k:
                    load(2 * k, 0, k)
                    load(2 * k + 1, 1, k)

            @block.tensor
            def _(pe):
                ident = core.c(128, C_ID, 128)

                def front(i, p):
                    pe.wait_ge(x_loaded[p], 16 * i + 32 - 16 * p)
                    wait_past(pe, xs_copied, i)
                    accumulate(pe, bank[1][0:T, :], [
                        (xt_in[p][:, c, :], core.w_in[:, c, DI:2 * DI]) for c in range(KD)])
                    wait_past(pe, rot_copied, i)
                    accumulate(pe, bank[2][0:T, 0:2 * NS], [
                        (xt_in[p][:, c, :], core.w_in[:, c, 2 * DI:2 * DI + 2 * NS]) for c in range(KD)]).then_inc(xs_ready, 1)
                    pe.wait_ge(lower_ready, i + 1)
                    wait_past(pe, exp_done, i)
                    for h in range(H0):
                        last = pe.matmul(bank[3 + h // 4][0:T, h % 4 * T:(h % 4 + 1) * T], lower[:, h, :],
                                         core.c(T, C_TRI, T), start=True, stop=True)
                    last.then_inc(logdecay_ready, 1)

                def back(i, p):
                    pe.wait_ge(rot_ready, i + 1)
                    pe.wait_ge(rot_copied, i + 1)
                    for g in range(2):
                        for m in range(4):
                            last = pe.transpose(bank[5 + g][:, m * T:(m + 1) * T],
                                                rot[p][:, g, 2 * m:2 * m + 2, :].rearrange("t h n -> t (h n)"), ident[0:T, 0:T])
                    last.then_inc(turned, 1)
                    pe.wait_ge(turned_copied, 2 * i + 2)
                    wait_past(pe, nt_copied, i)
                    for h in range(H0):
                        half = slice(h % 2 * NS, (h % 2 + 1) * NS)
                        last = pe.matmul(bank[7 * (1 - h % 2)][0:T, h // 2 * T:(h // 2 + 1) * T], rot_t[half, 0, h // 2, :],
                                         rot_t[half, 1, h // 2, :], start=True, stop=True)
                    last.then_inc(scores_ready, 1)
                    pe.wait_ge(mix_ready, i + 1)
                    pe.wait_ge(xdt_ready, i + 1)
                    for h in range(H0):
                        last = pe.matmul(bank[5][0:T, h * P0:(h + 1) * P0], mix[:, h, :], xs_dt[p][:, h * P0:(h + 1) * P0],
                                         start=True, stop=True)
                    last.then_inc(y_ready, 1)
                    pe.wait_ge(y2_ready, i + 1)
                    for m in range(4):
                        last = pe.transpose(bank[6][:, m * T:(m + 1) * T], y2[:, m * 128:(m + 1) * 128], ident[0:T, 0:T])
                    last.then_inc(yt_ready, 1)
                    pe.wait_ge(yt_copied, i + 1)
                    pe.wait_ge(w_scaled, 1)
                    accumulate(pe, bank[7][0:T, 0:D], [(y_t[:, m, :], w_out[:, m, :]) for m in range(4)]).then_inc(out_ready, 1)
                    pe.wait_ge(normed_ready, i + 1)
                    for c in range(KD):
                        last = pe.transpose(bank[0][:, c * T:(c + 1) * T], normed[:, c * 128:(c + 1) * 128], ident[0:T, 0:T])
                    last.then_inc(nt_ready, 1)

                skewed(pe, front, back)

            @block.vector
            def _(dve):
                chain_f, chain_b = Chain(dve, front_chain, 1), Chain(dve, back_chain, 6)
                dve.wait_ge(w_loaded, 32)
                dve.tensor_tensor(w_out[:, :, :], w_out[:, :, :], w_norm[:, :].unsqueeze(2).broadcast_to([128, 4, D]),
                                  ALU.mult).then_inc(w_scaled, 1)

                def front(i, p):
                    chain_f.start(i)
                    wait_past(dve, logdecay_ready, i)
                    dve.tensor_tensor(lower[:, :, :], core.c(T, C_AFTER, T).unsqueeze(1).broadcast_to([T, H0, T]),
                                      dta[:, i, :].unsqueeze(2).broadcast_to([T, H0, T]), ALU.mult).then_inc(lower_ready, 1)
                    dve.wait_ge(bc_copied, i + 1)
                    wait_past(dve, turned, i - 1)
                    shape = [T, 2, H0, PAIRS]
                    c1 = cosine[:, bass.ts(i, H0), :].unsqueeze(1).broadcast_to(shape)
                    s1 = sine[:, bass.ts(i, H0), :].unsqueeze(1).broadcast_to(shape)
                    of = lambda e: bc[:, :, e:2 * PAIRS:2].unsqueeze(2).broadcast_to(shape)
                    dve.tensor_tensor(prod[0][:, :, :, :], of(0), c1, ALU.mult)
                    dve.tensor_tensor(prod[1][:, :, :, :], of(1), s1, ALU.mult)
                    dve.tensor_tensor(prod[2][:, :, :, :], of(1), c1, ALU.mult)
                    chain_f.link(dve.tensor_tensor(prod[3][:, :, :, :], of(0), s1, ALU.mult))
                    dve.tensor_tensor(rot[p][:, :, :, 0:2 * PAIRS:2], prod[0][:, :, :, :], prod[1][:, :, :, :], ALU.add)
                    dve.tensor_tensor(rot[p][:, :, :, 1:2 * PAIRS:2], prod[2][:, :, :, :], prod[3][:, :, :, :],
                                      ALU.subtract).then_inc(rot_ready, 1)
                    dve.wait_ge(xs_copied, i + 1)
                    wait_past(dve, y_ready, i - 1)
                    dve.tensor_tensor(xs_dt[p][:, :].rearrange("t (h p) -> t h p", h=H0),
                                      xs[:, :].rearrange("t (h p) -> t h p", h=H0),
                                      dt[:, i, :].unsqueeze(2).broadcast_to([T, H0, P0]), ALU.mult).then_inc(xdt_ready, 1)

                def back(i, p):
                    chain_b.start(i)
                    dve.wait_ge(turned, i + 1)
                    wait_past(dve, scores_ready, i)
                    dve.tensor_copy(rot_t[:, 1, :, :], bank[6][:, 0:4 * T].rearrange("n (m t) -> n m t", m=4)).then_inc(turned_copied, 1)
                    dve.wait_ge(scores_ready, i + 1)
                    dve.wait_ge(decay_ready, i + 1)
                    for g in range(2):
                        last = dve.tensor_tensor(mix[:, g:H0:2, :], bank[7 * (1 - g)][0:T, 0:4 * T].rearrange("s (h t) -> s h t", h=4),
                                                 decay[p][:, g:H0:2, :], ALU.mult)
                    last.then_inc(mix_ready, 1)
                    dve.wait_ge(y_ready, i + 1)
                    dve.wait_ge(skip_ready, i + 1)
                    chain_b.link(dve.tensor_tensor(y[:, :], bank[5][0:T, :], xs_skip[p][:, :], ALU.add))
                    dve.tensor_tensor(y2[:, :], y[:, :], zs[:, i, :], ALU.mult).then_inc(y2_ready, 1)
                    dve.wait_ge(out_ready, i + 1)
                    dve.wait_ge(rms_ready, i + 1)
                    dve.wait_ge(x_loaded[p], 16 * i + 32 - 16 * p)
                    chain_b.link(dve.scalar_tensor_tensor(res[:, :], bank[7][0:T, 0:D], rms[:, :], x_in[p][:, :], ALU.mult, ALU.add))
                    chain_b.link(dve.bn_stats(stats[:, :], res[:, :]))
                    dve.memset(pad[:, :], 0.0)
                    chain_b.link(dve.bn_aggr(mv[:, :], stats[:, :]))
                    dve.tensor_scalar(mv[:, 1:2], mv[:, 1:2], EPS, None, ALU.add).then_inc(var_ready, 1)
                    dve.wait_ge(rstd_ready, i + 1)
                    chain_b.link(dve.tensor_scalar(normed[:, :], res[:, :], mv[:, 0:1], rstd[:, :], ALU.subtract, ALU.mult))
                    dve.sem_inc(normed_ready, 1)
                    chain_b.link(dve.tensor_copy(core.x[:, i, :], normed[:, :]))

                skewed(dve, front, back)

            @block.scalar
            def _(act):
                chain = Chain(act, act_chain, 4)
                act.preload_act_table_set(EXP_LN)

                def front(i, p):
                    act.wait_ge(xs_ready, i + 1)
                    wait_past(act, xdt_ready, i)
                    wait_past(act, skip_ready, i)
                    act.copy(xs[:, :], bank[1][0:T, :]).then_inc(xs_copied, 1)
                    wait_past(act, rot_ready, i)
                    act.copy(bc[:, :, :], bank[2][0:T, 0:2 * NS].rearrange("t (g n) -> t g n", g=2)).then_inc(bc_copied, 1)
                    wait_past(act, turned, i - 1)
                    for g in range(2):
                        last = act.copy(rot[p][:, g, :, 2 * PAIRS:NS], bank[2][0:T, g * NS + 2 * PAIRS:(g + 1) * NS]
                                        .unsqueeze(1).broadcast_to([T, H0, NS - 2 * PAIRS]))
                    last.then_inc(rot_copied, 1)
                    act.wait_ge(logdecay_ready, i + 1)
                    wait_past(act, mix_ready, i - 1)
                    for g in range(2):
                        last = act.activation(decay[p][:, 4 * g:4 * g + 4, :],
                                              bank[3 + g][0:T, 0:4 * T].rearrange("s (h t) -> s h t", h=4), ACT.Exp)
                    last.then_inc(exp_done, 1)

                def back(i, p):
                    chain.start(i)
                    act.wait_ge(turned, i + 1)
                    wait_past(act, scores_ready, i)
                    act.copy(rot_t[:, 0, :, :], bank[5][:, 0:4 * T].rearrange("n (m t) -> n m t", m=4)).then_inc(turned_copied, 1)
                    act.wait_ge(yt_ready, i + 1)
                    wait_past(act, out_ready, i)
                    act.copy(y_t[:, :, :], bank[6][:, 0:4 * T].rearrange("n (m t) -> n m t", m=4)).then_inc(yt_copied, 1)
                    act.wait_ge(y2_ready, i + 1)
                    chain.link(act.activation(sq[:, :], y2[:, :], ACT.Square, accum_out=ssq[:, :]))
                    chain.link(act.activation(ssq[:, :], ssq[:, :], ACT.Ln, bias=core.c(T, C_EPS, 1), scale=1.0 / DI))
                    wait_past(act, var_ready, i)
                    act.activation(rms[:, :], ssq[:, :], ACT.Exp, scale=-0.5).then_inc(rms_ready, 1)
                    act.wait_ge(var_ready, i + 1)
                    chain.link(act.activation(rstd[:, :], mv[:, 1:2], ACT.Ln))
                    chain.link(act.activation(rstd[:, :], rstd[:, :], ACT.Exp, scale=-0.5))
                    act.sem_inc(rstd_ready, 1)
                    act.wait_ge(nt_ready, i + 1)
                    act.copy(core.xt[:, :, bass.ts(i, T)], bank[0][:, 0:2 * T].rearrange("n (c t) -> n c t", c=KD)).then_inc(nt_copied, 1)

                skewed(act, front, back)

            @block.gpsimd
            def _(pool):
                def front(i, p):
                    pool.wait_ge(xs_copied, i + 1)
                    wait_past(pool, y2_ready, i - 1)
                    pool.tensor_tensor(xs_skip[p][:, :].rearrange("t (h p) -> t h p", h=H0),
                                       xs[:, :].rearrange("t (h p) -> t h p", h=H0),
                                       core.rows[:, R_DSKIP:R_DSKIP + H0].unsqueeze(2).broadcast_to([T, H0, P0]),
                                       ALU.mult).then_inc(skip_ready, 1)
                    pool.wait_ge(exp_done, i + 1)
                    pool.tensor_tensor(decay[p][:, :, :], decay[p][:, :, :],
                                       core.c(T, C_TRI, T).unsqueeze(1).broadcast_to([T, H0, T]), ALU.mult).then_inc(decay_ready, 1)

                skewed(pool, front, nothing)


def cross_attention(core, d, layer):
    nc = core.nc
    G, DH = ((16, 64), (8, 128))[layer]
    PER = 128 // DH
    SCALE = DH ** -0.5
    M = INNER // 128
    bank = core.bank
    OT_A, OT_B, OUT, NT = "ot_a", "ot_b", "out", "nt"
    fronts = [("q", 0), ("q", 1)] + [("k", m) for m in range(M)] + [("v", n) for n in range(2 * ST)]
    NF = len(fronts)
    assert NF == 16 and 2 * NF % G == 0

    TAILS = {3: ((4, 0, OT_A), (5, 1, OT_B)), 6: ((9, 3, OUT),), 10: ((14, 2, NT),)}

    def order(front, tail):
        steps = [[] for _ in range(G)]
        n = 0
        for f in range(NF):
            if front:
                steps[f * G // NF].append((n, *fronts[f]))
                n += 1
            if tail:
                for among, alone, kind in TAILS.get(f, ()):
                    steps[f * G // NF].append((among if front else alone, kind, 0))
                    n += 1
        return steps

    RSTD = 6 * G // NF + 1

    def before(i):
        if isinstance(i, int):
            return NF // 2 * min(i + 1, B) + 2 * max(i - 1, 0)
        return (NF // 2 + 2) * i + (NF // 2 - 2)

    with ExitStack() as ctx:
        sb = lambda name, shape: ctx.enter_context(nc.sbuf_tensor(f"x{layer}_{name}", shape, F32))
        sbr = lambda name, shape: ctx.enter_context(nc.sbuf_tensor(f"x{layer}_{name}", shape, F32R))
        pair = lambda name, shape: [sb(f"{name}{p}", shape) for p in range(2)]
        pair_r = lambda name, shape: [sbr(f"{name}{p}", shape) for p in range(2)]
        ctx_t = pair("ctx_t", [128, 2, SE])
        rest_high = sbr("rest_high", [128, SE])
        ctx_high, ctx_low, ctx_rest = pair_r("ctx_high", [128, SE]), pair_r("ctx_low", [128, SE]), pair_r("ctx_rest", [128, SE])
        w_high, w_low, w_rest, w_rest_low = (
            {n: sbr(f"w{n}_{part}", [rows, INNER]) for n in "kv"}
            for part, rows in (("high", 128), ("low", 128), ("rest", 128), ("rest_low", CB)))
        kt, v, qt = pair("kt", [128, M, S]), pair("v", [SP_, ST, INNER]), pair("qt", [128, M, T])
        prob, prob_t = pair("prob", [T, S]), pair("prob_t", [SP_, ST, T])
        negmax, total, inv = sb("negmax", [T, G]), sb("total", [T, G]), sb("inv", [T, G])
        o, ot = sb("o", [T, INNER]), sb("ot", [128, M, T])
        res, normed = sb("res", [T, D]), sb("normed", [T, D])
        stats, mv, rstd, pad = sb("stats", [T, 6]), sb("mv", [T, 2]), sb("rstd", [T, 1]), sb("pad", [T, 1])
        sem = lambda name: core.sem(f"x{layer}_{name}")
        ctx_loaded = [sem("ctx_loaded0"), sem("ctx_loaded1")]
        chunk_ready, chunk_used = [sem("chunk_ready0"), sem("chunk_ready1")], [sem("chunk_used0"), sem("chunk_used1")]
        s_ready, max_ready, p_ready, pt_ready, pt_copied, pv_done = (
            sem("s_ready"), sem("max_ready"), sem("p_ready"), sem("pt_ready"), sem("pt_copied"), sem("pv_done"))
        o_ready, var_ready, rstd_ready, normed_ready = sem("o_ready"), sem("var_ready"), sem("rstd_ready"), sem("normed_ready")
        dve_chain, act_chain = sem("dve"), sem("act")
        split_chain, split_done, w_rounded, w_split = sem("split_chain"), sem("split_done"), sem("w_rounded"), sem("w_split")

        def rounds(eng, round_):
            round_(-1, 1)
            round_(0, 0)
            with eng.Fori(0, B // 2 - 1) as j:
                round_(2 * j + 1, 1)
                round_(2 * j + 2, 0)
            round_(B - 1, 1)
            round_(B, 0)

        def parts(i):
            if not isinstance(i, int):
                return True, True, True
            return 0 <= i < B, i + 1 < B, i > 0

        with nc.Block() as block:
            @block.sync
            def _(sp):
                for i in range(B):
                    if i >= 2:
                        sp.wait_ge(split_done, i - 1)
                    sp.dma_start(ctx_t[i % 2][:, :, :], d["ctx_t"][i].rearrange("(c p) n -> p c n", p=128)).then_inc(ctx_loaded[i % 2], 16)

            @block.gpsimd
            def _(pool):
                chain = Chain(pool, split_chain, 2)

                def split(i, p):
                    chain.start(i)
                    pool.wait_ge(ctx_loaded[p], 8 * i + 16 - 8 * p)
                    wait_past(pool, split_done, i)
                    for b in range(2):
                        wait_past(pool, chunk_ready[b], before(i - 2))
                    pool.tensor_copy(ctx_high[p][:, :], ctx_t[p][:, 0, :])
                    pool.tensor_copy(rest_high[:, :], ctx_t[p][:, 1, :])
                    chain.link(pool.tensor_copy(ctx_rest[p][0:CB, :], ctx_t[p][0:CB, 1, :]))
                    chain.link(pool.tensor_tensor(ctx_low[p][:, :], ctx_t[p][:, 0, :], ctx_high[p][:, :].bitcast(F32), ALU.subtract))
                    pool.tensor_tensor(ctx_rest[p][CB:128, :], ctx_t[p][CB:128, 1, :], rest_high[CB:128, :].bitcast(F32),
                                       ALU.subtract).then_inc(split_done, 1)

                for i in range(B):
                    split(i, i % 2)

            @block.tensor
            def _(pe):
                ident = core.c(128, C_ID, 128)
                context = lambda q, cols: dict(high=ctx_high[q][:, cols], low=ctx_low[q][:, cols], rest=ctx_rest[q][:, cols],
                                               last=ctx_rest[q][0:CB, cols])
                weights = lambda n, cols: dict(high=w_high[n][:, cols], low=w_low[n][:, cols], rest=w_rest[n][:, cols],
                                               last=w_rest_low[n][:, cols])

                def scores(i, g, p):
                    rows = slice(g % PER * DH, (g % PER + 1) * DH)
                    pe.matmul(bank[2 + g % 2][0:T, 0:S], qt[p][rows, g // PER, :], kt[p][rows, g // PER, :],
                              start=True, stop=True).then_inc(s_ready, 1)

                def weigh(i, g, p):
                    pe.wait_ge(pt_copied, i * G + g + 1)
                    if g == 0:
                        wait_past(pe, o_ready, i)
                    at = g % (G // 2) * DH
                    accumulate(pe, bank[6 + g // (G // 2)][0:T, at:at + DH], [
                        (prob_t[g % 2][:, k, :], v[p][:, k, g * DH:(g + 1) * DH]) for k in range(ST)]).then_inc(pv_done, 1)

                def chunk(i, p, n, kind, a):
                    b, q = n % 2, 1 - p
                    out = bank[b]
                    wait_past(pe, chunk_used[b], before(i) + n // 2)
                    if kind == "q":
                        for m in range(4):
                            last = accumulate(pe, out[:, m * T:(m + 1) * T], [
                                (core.wq[:, c, (4 * a + m) * 128:(4 * a + m + 1) * 128], core.xt[:, c, bass.ts(i + 1, T)])
                                for c in range(KD)])
                    elif kind == "k":
                        last = accumulate(pe, out[:, 0:SE], exact_products(
                            weights("k", slice(a * 128, (a + 1) * 128)), context(q, slice(0, SE))))
                    elif kind == "v":
                        last = accumulate(pe, out[0:SP_, :], exact_products(
                            context(q, slice(a // 2 * SP_, (a // 2 + 1) * SP_)), weights("v", slice(a % 2 * 512, (a % 2 + 1) * 512))))
                    elif kind in (OT_A, OT_B):
                        pe.wait_ge(o_ready, i)
                        for m in range(4):
                            mm = m + 4 * (kind == OT_B)
                            last = pe.transpose(out[:, m * T:(m + 1) * T], o[:, mm * 128:(mm + 1) * 128], ident[0:T, 0:T])
                    elif kind == OUT:
                        for half in range(2):
                            pe.wait_ge(chunk_used[half], before(i) + TAILS[3][half][0 if parts(i)[1] else 1] // 2 + 1)
                        last = accumulate(pe, out[0:T, 0:D], [(ot[:, m, :], core.wo[:, m, :]) for m in range(M)]
                                          + [(core.c(1, C_ONE, T), core.bo[:, :])])
                    else:
                        pe.wait_ge(normed_ready, i)
                        for c in range(KD):
                            last = pe.transpose(out[:, c * T:(c + 1) * T], normed[:, c * 128:(c + 1) * 128], ident[0:T, 0:T])
                    last.then_inc(chunk_ready[b], 1)

                def round_(i, p):
                    heads, front, tail = parts(i)
                    if heads:
                        for b in range(2):
                            pe.wait_ge(chunk_used[b], before(i))
                        scores(i, 0, p)
                        scores(i, 1, p)
                    if front:
                        pe.wait_ge(split_done, i + 2)
                    for g, chunks in enumerate(order(front, tail)):
                        for n, kind, a in chunks:
                            chunk(i, p, n, kind, a)
                        if not heads:
                            continue
                        pe.wait_ge(p_ready, i * G + g + 1)
                        wait_past(pe, pt_copied, i * G + g - 1)
                        for k in range(ST):
                            last = pe.transpose(bank[4 + g % 2][0:SP_, k * T:(k + 1) * T], prob[g % 2][:, k * SP_:(k + 1) * SP_],
                                                ident[0:T, 0:T])
                        last.then_inc(pt_ready, 1)
                        if g + 2 < G:
                            scores(i, g + 2, p)
                        if g > 0:
                            weigh(i, g - 1, p)
                    if heads:
                        weigh(i, G - 1, p)

                pe.wait_ge(core.xw_loaded, 80 * (layer + 1))
                pe.wait_ge(w_split, 2)
                rounds(pe, round_)

            def empty(eng, i, p, n, kind, a, copy):
                b, q = n % 2, 1 - p
                src = bank[b]
                eng.wait_ge(chunk_ready[b], before(i) + n // 2 + 1)
                if kind == "q":
                    return copy(qt[q][:, 4 * a:4 * a + 4, :], src[:, 0:4 * T].rearrange("d (m t) -> d m t", m=4), SCALE)
                if kind == "k":
                    return copy(kt[q][:, a, :], src[:, 0:S], None)
                if kind == "v":
                    return copy(v[q][:, a // 2, a % 2 * 512:(a % 2 + 1) * 512], src[0:SP_, :], None)
                if kind in (OT_A, OT_B):
                    half = 4 * (kind == OT_B)
                    return copy(ot[:, half:half + 4, :], src[:, 0:4 * T].rearrange("d (m t) -> d m t", m=4), None)
                assert kind == NT
                return copy(core.xt[:, :, bass.ts(i - 1, T)], src[:, 0:2 * T].rearrange("d (c t) -> d c t", c=KD), None)

            @block.vector
            def _(dve):
                chain = Chain(dve, dve_chain, 6)

                def copy(out, in_, scale):
                    if scale is None:
                        return dve.tensor_copy(out, in_)
                    return dve.tensor_scalar(out, in_, scale, None, ALU.mult)

                def row_max(i, g):
                    dve.wait_ge(s_ready, i * G + g + 1)
                    dve.tensor_reduce(negmax[:, g:g + 1], bank[2 + g % 2][0:T, 0:S], AX_X, ALU.max, negate=True).then_inc(max_ready, 1)

                def round_(i, p):
                    heads, front, tail = parts(i)
                    if heads:
                        row_max(i, 0)
                    if tail:
                        chain.start(i - 1)
                        dve.wait_ge(p_ready, i * G)
                        chain.link(dve.reciprocal(inv[:, :], total[:, :]))
                        dve.wait_ge(pv_done, i * G)
                        for half in range(2):
                            w = slice(half * G // 2, (half + 1) * G // 2)
                            last = dve.tensor_tensor(o[:, half * 512:(half + 1) * 512].rearrange("t (h e) -> t h e", e=DH),
                                                     bank[6 + half][0:T, :].rearrange("t (h e) -> t h e", e=DH),
                                                     inv[:, w].unsqueeze(2).broadcast_to([T, G // 2, DH]), ALU.mult)
                        last.then_inc(o_ready, 1)
                    for g, chunks in enumerate(order(front, tail)):
                        if heads and g + 1 < G:
                            row_max(i, g + 1)
                        for n, kind, a in chunks:
                            if n % 2 == 0:
                                continue
                            if kind != OUT:
                                empty(dve, i, p, n, kind, a, copy).then_inc(chunk_used[1], 1)
                                continue
                            dve.wait_ge(chunk_ready[1], before(i) + n // 2 + 1)
                            dve.tensor_tensor(res[:, :], bank[1][0:T, 0:D], core.x[:, i - 1, :], ALU.add).then_inc(chunk_used[1], 1)
                            dve.wait_ge(chunk_used[1], before(i) + n // 2 + 1)
                            chain.link(dve.bn_stats(stats[:, :], res[:, :]))
                            dve.memset(pad[:, :], 0.0)
                            chain.link(dve.bn_aggr(mv[:, :], stats[:, :]))
                            chain.link(dve.tensor_scalar(mv[:, 1:2], mv[:, 1:2], EPS, None, ALU.add))
                            dve.sem_inc(var_ready, 1)
                        if tail and g == RSTD:
                            dve.wait_ge(rstd_ready, i)
                            chain.link(dve.tensor_scalar(normed[:, :], res[:, :], mv[:, 0:1], rstd[:, :], ALU.subtract, ALU.mult))
                            dve.sem_inc(normed_ready, 1)
                            chain.link(dve.tensor_copy(core.x[:, i - 1, :], normed[:, :]))
                        if heads:
                            dve.wait_ge(pt_ready, i * G + g + 1)
                            wait_past(dve, pv_done, i * G + g - 1)
                            dve.tensor_copy(prob_t[g % 2][:, :, :], bank[4 + g % 2][0:SP_, 0:ST * T]
                                            .rearrange("s (k t) -> s k t", k=ST)).then_inc(pt_copied, 1)

                for n, (name, w) in enumerate((("k", core.wk), ("v", core.wv))):
                    dve.wait_ge(w_rounded, n + 1)
                    dve.tensor_tensor(w_low[name][:, :], w[:, 0, :], w_high[name][:, :].bitcast(F32), ALU.subtract)
                    dve.tensor_tensor(w_rest_low[name][:, :], w[0:CB, 1, :], w_rest[name][0:CB, :].bitcast(F32),
                                      ALU.subtract).then_inc(w_split, 1)
                rounds(dve, round_)

            @block.scalar
            def _(act):
                chain = Chain(act, act_chain, 1)

                def copy(out, in_, scale):
                    if scale is None:
                        return act.copy(out, in_)
                    return act.activation(out, in_, ACT.Copy, scale=scale)

                def round_(i, p):
                    heads, front, tail = parts(i)
                    for g, chunks in enumerate(order(front, tail)):
                        if heads:
                            act.wait_ge(max_ready, i * G + g + 1)
                            wait_past(act, pt_ready, i * G + g - 1)
                            if g == 0:
                                wait_past(act, o_ready, i)
                            act.activation(prob[g % 2][:, :], bank[2 + g % 2][0:T, 0:S], ACT.Exp, bias=negmax[:, g:g + 1],
                                           accum_out=total[:, g:g + 1]).then_inc(p_ready, 1)
                        if tail and g == RSTD:
                            chain.start(i - 1)
                            act.wait_ge(var_ready, i)
                            chain.link(act.activation(rstd[:, :], mv[:, 1:2], ACT.Ln))
                            act.activation(rstd[:, :], rstd[:, :], ACT.Exp, scale=-0.5).then_inc(rstd_ready, 1)
                        for n, kind, a in chunks:
                            if n % 2 == 0:
                                empty(act, i, p, n, kind, a, copy).then_inc(chunk_used[0], 1)

                act.preload_act_table_set(EXP_LN)
                act.wait_ge(core.xw_loaded, 80 * (layer + 1))
                for name, w in (("k", core.wk), ("v", core.wv)):
                    act.copy(w_high[name][:, :], w[:, 0, :])
                    act.copy(w_rest[name][:, :], w[:, 1, :]).then_inc(w_rounded, 1)
                rounds(act, round_)


def norm_statistics(dve, chain, core, mv, stats, pad, ready):
    for i in range(B):
        dve.bn_stats(stats[:, i, :], core.x[:, i, :])
    chain.link(dve.memset(pad[:, :], 0.0))
    for i in range(B):
        dve.bn_aggr(mv[:, i, :], stats[:, i, :])
    chain.link(dve.memset(pad[:, :], 0.0))
    dve.tensor_scalar(mv[:, :, 1:2], mv[:, :, 1:2], EPS, None, ALU.add).then_inc(ready, 1)


def mixture(core, d):
    nc = core.nc
    bank = core.bank
    HALF = N // 2
    HI = B // 2
    with ExitStack() as ctx:
        sb = lambda name, shape: ctx.enter_context(nc.sbuf_tensor("moe_" + name, shape, F32))
        sbr = lambda name, shape: ctx.enter_context(nc.sbuf_tensor("moe_" + name, shape, F32R))
        pair = lambda name, shape: [sb(f"{name}{p}", shape) for p in range(2)]
        pair_r = lambda name, shape: [sbr(f"{name}{p}", shape) for p in range(2)]
        wg = sb("wg", [128, KD, E0])
        w1, w2 = pair("w1", [128, KD, F0]), pair("w2", [128, FM, D])
        xt_high, xt_low = sbr("xt_high", [128, KD, N]), sbr("xt_low", [128, KD, N])
        w1_high, w1_low = pair_r("w1_high", [128, KD, F0]), pair_r("w1_low", [128, KD, F0])
        w2_high, w2_low = pair_r("w2_high", [128, FM, D]), pair_r("w2_low", [128, FM, D])
        h_high, h_low = pair_r("h_high", [128, FM, HALF]), pair_r("h_low", [128, FM, HALF])
        r, sq = pair("r", [128, HALF]), pair("sq", [128, HALF])
        gates = {n: sb(n, [T, B, E0]) for n in ("shifted", "e", "prob", "eq", "first", "rest", "second", "both", "kept", "weight")}
        per = {n: sb(n, [T, B]) for n in ("max", "sum", "inv", "best", "pick", "sum2", "inv2")}
        stats, mv, rstd, pad = sb("stats", [T, B, 6]), sb("mv", [T, B, 2]), sb("rstd", [T, B, 1]), sb("pad", [T, 1])
        sem = lambda name: core.sem("moe_" + name)
        wg_loaded, w_loaded = sem("wg_loaded"), [sem("w_loaded0"), sem("w_loaded1")]
        logits_ready, shifted_ready, e_ready = sem("logits_ready"), sem("shifted_ready"), sem("e_ready")
        h_ready, h_used, sq_done = sem("h_ready"), sem("h_used"), sem("sq_done")
        y_ready, y_used = sem("y_ready"), sem("y_used")
        high_done, low_done, w_rounded, w_split = sem("high_done"), sem("low_done"), sem("w_rounded"), sem("w_split")
        xt_rounded, xt_split = sem("xt_rounded"), sem("xt_split")
        var_ready, rstd_ready, normed_ready, nt_ready = sem("var_ready"), sem("rstd_ready"), sem("normed_ready"), sem("nt_ready")
        dve_chain, act_chain = sem("dve"), sem("act")

        def rounds(eng, round_):
            round_(0, 0)
            with eng.Fori(0, E0 // 2 - 1) as j:
                round_(2 * j + 1, 1)
                round_(2 * j + 2, 0)
            round_(E0 - 1, 1)
            round_(E0, 0)

        def parts(e):
            return (True, True) if not isinstance(e, int) else (e < E0, e > 0)

        more = lambda e: not isinstance(e, int) or e + 1 < E0

        with nc.Block() as block:
            @block.sync
            def _(sp):
                sp.dma_start(wg[:, :, :], d["L0_ffn_Wg"].rearrange("(c p) n -> p c n", p=128)).then_inc(wg_loaded, 16)

                def load(e, p):
                    wait_past(sp, w_split, e - 1)
                    sp.dma_start(w1[p][:, :, :], d["L0_ffn_W1"][e].rearrange("(c p) n -> p c n", p=128)).then_inc(w_loaded[p], 16)
                    sp.dma_start(w2[p][:, :, :], d["L0_ffn_W2"][e].rearrange("(m p) n -> p m n", p=128)).then_inc(w_loaded[p], 16)

                load(0, 0)
                load(1, 1)
                core.load_cross_weights(sp, d, 1)
                for e in range(2, E0):
                    load(e, e % 2)

            @block.tensor
            def _(pe):
                def hidden(e, p, half):
                    for m in range(FM):
                        c = 2 * FM * e + FM * half + m
                        wait_past(pe, h_used, c - FM + 1)
                        rows, cols = slice(m * 128, (m + 1) * 128), slice(half * HALF, (half + 1) * HALF)
                        accumulate(pe, bank[m][:, 0:HALF], [
                            pair for k in range(KD) for pair in split_products(
                                w1_high[p][:, k, rows], w1_low[p][:, k, rows], xt_high[:, k, cols], xt_low[:, k, cols])]
                        ).then_inc(h_ready, 1)

                def outputs(e, p, half):
                    pe.wait_ge(low_done, 2 * FM * e + FM * (half + 1))
                    for b in range(HI // 2):
                        pe.wait_ge(y_used, HI * e + HI // 2 * half + b + 1)
                        for u in range(2):
                            i = 2 * b + u
                            last = accumulate(pe, bank[4 + 2 * half + b][0:T, u * D:(u + 1) * D], [
                                pair for m in range(FM) for pair in split_products(
                                    h_high[half][:, m, i * T:(i + 1) * T], h_low[half][:, m, i * T:(i + 1) * T],
                                    w2_high[p][:, m, :], w2_low[p][:, m, :])])
                        last.then_inc(y_ready, 1)

                def round_(e, p):
                    own, before = parts(e)
                    if own:
                        pe.wait_ge(w_split, e + 1)
                        hidden(e, p, 0)
                    if before:
                        outputs(e - 1, 1 - p, 1)
                    if own:
                        hidden(e, p, 1)
                        outputs(e, p, 0)

                pe.wait_ge(wg_loaded, 16)
                for i in range(B):
                    last = accumulate(pe, bank[7][0:T, i * E0:(i + 1) * E0], [
                        (core.xt[:, c, i * T:(i + 1) * T], wg[:, c, :]) for c in range(KD)])
                last.then_inc(logits_ready, 1)
                pe.wait_ge(xt_split, 1)
                rounds(pe, round_)
                ident = core.c(128, C_ID, 128)
                pe.wait_ge(normed_ready, 1)
                for b in range(B // 2):
                    for u in range(2):
                        for c in range(KD):
                            at = (u * KD + c) * T
                            last = pe.transpose(bank[b][:, at:at + T], core.x[:, 2 * b + u, c * 128:(c + 1) * 128], ident[0:T, 0:T])
                    last.then_inc(nt_ready, 1)

            @block.vector
            def _(dve):
                chain = Chain(dve, dve_chain, 22)
                chain.start(0)
                link = chain.link
                g = {n: t[:, :, :] for n, t in gates.items()}
                s = {n: t[:, :] for n, t in per.items()}
                wide = lambda n: per[n][:, :].unsqueeze(2).broadcast_to([T, B, E0])
                logits = bank[7][0:T, 0:B * E0].rearrange("t (b e) -> t b e", b=B)
                prio = core.c(T, C_PRIO, E0).unsqueeze(1).broadcast_to([T, B, E0])
                tt = dve.tensor_tensor
                dve.wait_ge(xt_rounded, 1)
                dve.tensor_tensor(xt_low[:, :, :], core.xt[:, :, :], xt_high[:, :, :].bitcast(F32), ALU.subtract).then_inc(xt_split, 1)
                dve.wait_ge(w_rounded, 1)
                dve.tensor_tensor(w1_low[0][:, :, :], w1[0][:, :, :], w1_high[0][:, :, :].bitcast(F32), ALU.subtract)
                dve.tensor_tensor(w2_low[0][:, :, :], w2[0][:, :, :], w2_high[0][:, :, :].bitcast(F32), ALU.subtract).then_inc(w_split, 1)
                dve.wait_ge(logits_ready, 1)
                link(dve.tensor_reduce(s["max"], logits, AX_X, ALU.max))
                tt(g["shifted"], logits, wide("max"), ALU.subtract).then_inc(shifted_ready, 1)
                dve.wait_ge(e_ready, 1)
                link(dve.tensor_reduce(s["sum"], g["e"], AX_X, ALU.add))
                link(dve.reciprocal(s["inv"], s["sum"]))
                link(tt(g["prob"], g["e"], wide("inv"), ALU.mult))

                def pick(src, out):
                    link(dve.tensor_reduce(s["best"], g[src], AX_X, ALU.max))
                    link(tt(g["eq"], g[src], wide("best"), ALU.is_equal))
                    link(tt(g["eq"], g["eq"], prio, ALU.mult))
                    link(dve.tensor_reduce(s["pick"], g["eq"], AX_X, ALU.max))
                    link(tt(g[out], g["eq"], wide("pick"), ALU.is_equal))

                pick("prob", "first")
                link(dve.scalar_tensor_tensor(g["rest"], g["first"], -2.0, g["prob"], ALU.mult, ALU.add))
                pick("rest", "second")
                link(tt(g["both"], g["first"], g["second"], ALU.add))
                link(tt(g["kept"], g["prob"], g["both"], ALU.mult))
                link(dve.tensor_reduce(s["sum2"], g["kept"], AX_X, ALU.add))
                link(dve.tensor_scalar(s["sum2"], s["sum2"], 1e-8, None, ALU.add))
                link(dve.reciprocal(s["inv2"], s["sum2"]))
                link(tt(g["weight"], g["kept"], wide("inv2"), ALU.mult))

                def add(e, half):
                    for b in range(HI // 2):
                        n = HI * e + HI // 2 * half + b
                        dve.wait_ge(y_ready, n + 1)
                        dve.wait_ge(y_used, n + 1)
                        for u in range(2):
                            i = HI * half + 2 * b + u
                            last = dve.scalar_tensor_tensor(core.x[:, i, :], bank[4 + 2 * half + b][0:T, u * D:(u + 1) * D],
                                                            gates["weight"][:, i, bass.ds(e, 1)], core.x[:, i, :], ALU.mult, ALU.add)
                        last.then_inc(y_used, 1)

                def low(e, half):
                    for m in range(FM):
                        c = 2 * FM * e + FM * half + m
                        dve.wait_ge(sq_done, c + 1)
                        dve.wait_ge(high_done, c + 1)
                        dve.tensor_tensor(h_low[half][:, m, :], sq[m % 2][:, :], h_high[half][:, m, :].bitcast(F32),
                                          ALU.subtract).then_inc(low_done, 1)

                def split_low(e, p):
                    dve.wait_ge(w_rounded, e + 1)
                    dve.tensor_tensor(w1_low[p][:, :, :], w1[p][:, :, :], w1_high[p][:, :, :].bitcast(F32), ALU.subtract)
                    dve.tensor_tensor(w2_low[p][:, :, :], w2[p][:, :, :], w2_high[p][:, :, :].bitcast(F32),
                                      ALU.subtract).then_inc(w_split, 1)

                def round_(e, p):
                    own, before = parts(e)
                    if own:
                        low(e, 0)
                    if before:
                        add(e - 1, 1)
                    if own:
                        low(e, 1)
                        if more(e):
                            split_low(e + 1, 1 - p)
                        add(e, 0)

                dve.sem_inc(y_used, HI)
                rounds(dve, round_)
                dve.wait_ge(y_used, HI * (E0 + 1))
                norm_statistics(dve, chain, core, mv, stats, pad, var_ready)
                dve.wait_ge(rstd_ready, 1)
                for i in range(B):
                    last = dve.tensor_scalar(core.x[:, i, :], core.x[:, i, :], mv[:, i, 0:1], rstd[:, i, :], ALU.subtract, ALU.mult)
                last.then_inc(normed_ready, 1)
                for b in range(1, B // 2, 2):
                    dve.wait_ge(nt_ready, b + 1)
                    dve.tensor_copy(core.xt[:, :, 2 * b * T:2 * (b + 1) * T].rearrange("d c (u t) -> d u c t", u=2),
                                    bank[b][:, 0:4 * T].rearrange("d (u c t) -> d u c t", u=2, c=KD))

            @block.gpsimd
            def _(pool):
                def square(e, half):
                    for m in range(FM):
                        c = 2 * FM * e + FM * half + m
                        pool.wait_ge(h_used, c + 1)
                        wait_past(pool, low_done, c - 1)
                        pool.tensor_tensor(sq[m % 2][:, :], r[m % 2][:, :], r[m % 2][:, :], ALU.mult).then_inc(sq_done, 1)

                def round_(e, p):
                    if parts(e)[0]:
                        square(e, 0)
                        square(e, 1)

                rounds(pool, round_)

            @block.scalar
            def _(act):
                chain = Chain(act, act_chain, 1)
                chain.start(0)
                act.preload_act_table_set(EXP_LN)
                act.copy(xt_high[:, :, :], core.xt[:, :, :]).then_inc(xt_rounded, 1)
                act.wait_ge(w_loaded[0], 32)
                act.copy(w1_high[0][:, :, :], w1[0][:, :, :])
                act.copy(w2_high[0][:, :, :], w2[0][:, :, :]).then_inc(w_rounded, 1)
                act.wait_ge(shifted_ready, 1)
                act.activation(gates["e"][:, :, :], gates["shifted"][:, :, :], ACT.Exp).then_inc(e_ready, 1)

                def high(e, half, m):
                    c = 2 * FM * e + FM * half + m
                    act.wait_ge(h_used, c + 1)
                    act.activation(h_high[half][:, m, :], r[m % 2][:, :], ACT.Square).then_inc(high_done, 1)

                def relu(e, half):
                    for m in range(FM):
                        c = 2 * FM * e + FM * half + m
                        act.wait_ge(h_ready, c + 1)
                        wait_past(act, sq_done, c - 1)
                        wait_past(act, high_done, c - 1)
                        act.activation(r[m % 2][:, :], bank[m][:, 0:HALF], ACT.Relu).then_inc(h_used, 1)
                        if m == 0:
                            wait_past(act, y_ready, HI * (e - 1) + HI // 2 * (half + 1))
                        else:
                            high(e, half, m - 1)
                    high(e, half, FM - 1)

                def round_high(e, p):
                    act.wait_ge(w_loaded[p], 16 * e + 32 - 16 * p)
                    wait_past(act, y_ready, HI * (e - 1))
                    act.copy(w1_high[p][:, :, :], w1[p][:, :, :])
                    act.copy(w2_high[p][:, :, :], w2[p][:, :, :]).then_inc(w_rounded, 1)

                def round_(e, p):
                    if parts(e)[0]:
                        relu(e, 0)
                        relu(e, 1)
                        if more(e):
                            round_high(e + 1, 1 - p)

                rounds(act, round_)
                act.wait_ge(var_ready, 1)
                chain.link(act.activation(rstd[:, :, :], mv[:, :, 1:2], ACT.Ln))
                act.activation(rstd[:, :, :], rstd[:, :, :], ACT.Exp, scale=-0.5).then_inc(rstd_ready, 1)
                for b in range(0, B // 2, 2):
                    act.wait_ge(nt_ready, b + 1)
                    act.copy(core.xt[:, :, 2 * b * T:2 * (b + 1) * T].rearrange("d c (u t) -> d u c t", u=2),
                             bank[b][:, 0:4 * T].rearrange("d (u c t) -> d u c t", u=2, c=KD))


def low_rank_experts(core, d, out):
    nc = core.nc
    bank = core.bank
    W = D + E1 + RK
    with ExitStack() as ctx:
        sb = lambda name, shape, dt=F32: ctx.enter_context(nc.sbuf_tensor("lora_" + name, shape, dt))
        w, bias, lora_b = sb("w", [128, KD, W]), sb("bias", [1, W]), sb("b", [E1 * RK, D])
        small = sb("small", [T, B, E1 + RK])
        shifted, e, gate = sb("shifted", [T, B, E1]), sb("e", [T, B, E1]), sb("gate", [T, B, E1], BF16)
        mid2 = sb("mid2", [T, B, RK])
        top, total, inv = sb("top", [T, B]), sb("total", [T, B]), sb("inv", [T, B])
        gm, gm_t = sb("gm", [T, B, E1, RK]), sb("gm_t", [E1 * RK, B, T])
        stats, mv, rstd, pad = sb("stats", [T, B, 6]), sb("mv", [T, B, 2]), sb("rstd", [T, B, 1]), sb("pad", [T, 1])
        sem = lambda name: core.sem("lora_" + name)
        loaded, base_ready, shifted_ready, e_ready, gm_ready = (
            sem("loaded"), sem("base_ready"), sem("shifted_ready"), sem("e_ready"), sem("gm_ready"))
        base_used, gmt_ready, gmt_copied, low_ready = sem("base_used"), sem("gmt_ready"), sem("gmt_copied"), sem("low_ready")
        var_ready, rstd_ready, out_ready, stored = sem("var_ready"), sem("rstd_ready"), sem("out_ready"), sem("stored")
        dve_chain, act_chain = sem("dve"), sem("act")

        with nc.Block() as block:
            @block.sync
            def _(sp):
                sp.dma_start(w[:, :, 0:D], d["base_wt"].rearrange("(c p) n -> p c n", p=128)).then_inc(loaded, 16)
                sp.dma_start(w[:, :, D:D + E1], d["router_wt"].rearrange("(c p) n -> p c n", p=128)).then_inc(loaded, 16)
                sp.dma_start(w[:, :, D + E1:W], d["lora_a"].rearrange("(c p) n -> p c n", p=128)).then_inc(loaded, 16)
                sp.dma_start(bias[:, :], d["ffn_bias"]).then_inc(loaded, 16)
                sp.dma_start(lora_b[:, :], d["lora_b"]).then_inc(loaded, 16)
                for i in range(B):
                    sp.wait_ge(out_ready, i + 1)
                    sp.dma_start(out[i], core.x[:, i, :]).then_inc(stored, 16)
                sp.wait_ge(stored, 16 * B)

            @block.tensor
            def _(pe):
                ident = core.c(128, C_ID, 128)
                pe.wait_ge(loaded, 80)
                for i in range(B):
                    accumulate(pe, bank[i][0:T, 0:W], [(core.xt[:, c, i * T:(i + 1) * T], w[:, c, :]) for c in range(KD)]
                               + [(core.c(1, C_ONE, T), bias[:, :])]).then_inc(base_ready, 1)
                pe.wait_ge(gm_ready, 1)
                pe.wait_ge(base_used, B)
                for i in range(B):
                    last = pe.transpose(bank[i // 4][0:E1 * RK, i % 4 * T:(i % 4 + 1) * T],
                                        gm[:, i, :, :].rearrange("t e r -> t (e r)"), ident[0:T, 0:T])
                    if i % 4 == 3:
                        last.then_inc(gmt_ready, 1)
                for i in range(B):
                    if i % 4 == 0:
                        pe.wait_ge(gmt_copied, i // 4 + 1)
                    last = pe.matmul(bank[2 + i // 2][0:T, i % 2 * D:(i % 2 + 1) * D], gm_t[:, i, :], lora_b[:, :],
                                     start=True, stop=True)
                    if i % 2 == 1:
                        last.then_inc(low_ready, 1)

            @block.vector
            def _(dve):
                chain = Chain(dve, dve_chain, 9)
                chain.start(0)
                wide = lambda t: t[:, :].unsqueeze(2).broadcast_to([T, B, E1])
                logits = small[:, :, 0:E1]
                for i in range(B):
                    dve.wait_ge(base_ready, i + 1)
                    last = dve.tensor_copy(small[:, i, :], bank[i][0:T, D:W])
                chain.link(last)
                chain.link(dve.tensor_reduce(top[:, :], logits, AX_X, ALU.max))
                dve.tensor_tensor(shifted[:, :, :], logits, wide(top), ALU.subtract).then_inc(shifted_ready, 1)
                chain.link(dve.tensor_scalar(mid2[:, :, :], small[:, :, E1:E1 + RK], 2.0, None, ALU.mult))
                for i in range(B):
                    dve.tensor_tensor(core.x[:, i, :], bank[i][0:T, 0:D], core.x[:, i, :], ALU.add).then_inc(base_used, 1)
                dve.wait_ge(e_ready, 1)
                chain.link(dve.tensor_reduce(total[:, :], e[:, :, :], AX_X, ALU.add))
                chain.link(dve.reciprocal(inv[:, :], total[:, :]))
                chain.link(dve.tensor_tensor(gate[:, :, :], e[:, :, :], wide(inv), ALU.mult))
                shape = [T, B, E1, RK]
                dve.tensor_tensor(gm[:, :, :, :], gate[:, :, :].unsqueeze(3).broadcast_to(shape),
                                  mid2[:, :, :].unsqueeze(2).broadcast_to(shape), ALU.mult).then_inc(gm_ready, 1)
                for k in range(2):
                    dve.wait_ge(gmt_ready, k + 1)
                    dve.tensor_copy(gm_t[:, 4 * k:4 * k + 4, :], bank[k][0:E1 * RK, 0:4 * T].rearrange("r (i t) -> r i t", i=4)
                                    ).then_inc(gmt_copied, 1)
                for b in range(B // 2):
                    dve.wait_ge(low_ready, b + 1)
                    last = dve.tensor_tensor(core.x[:, 2 * b:2 * b + 2, :], bank[2 + b][0:T, :].rearrange("t (u n) -> t u n", u=2),
                                             core.x[:, 2 * b:2 * b + 2, :], ALU.add)
                chain.link(last)
                norm_statistics(dve, chain, core, mv, stats, pad, var_ready)
                dve.wait_ge(rstd_ready, 1)
                for i in range(B):
                    dve.tensor_scalar(core.x[:, i, :], core.x[:, i, :], mv[:, i, 0:1], rstd[:, i, :], ALU.subtract,
                                      ALU.mult).then_inc(out_ready, 1)

            @block.scalar
            def _(act):
                chain = Chain(act, act_chain, 1)
                chain.start(0)
                act.preload_act_table_set(EXP_LN)
                act.wait_ge(shifted_ready, 1)
                act.activation(e[:, :, :], shifted[:, :, :], ACT.Exp).then_inc(e_ready, 1)
                act.wait_ge(var_ready, 1)
                chain.link(act.activation(rstd[:, :, :], mv[:, :, 1:2], ACT.Ln))
                act.activation(rstd[:, :, :], rstd[:, :, :], ACT.Exp, scale=-0.5).then_inc(rstd_ready, 1)


def latent_attention(core, d):
    nc = core.nc
    bank = core.bank
    HALF, HI = N // 2, B // 2
    LAT = 64
    AUG = HD1 + 1
    GB = 4
    NG = H1 // GB
    with ExitStack() as whole:
        sbw = lambda name, shape: whole.enter_context(nc.sbuf_tensor("la_" + name, shape, F32))
        lat = sbw("lat", [128, N])
        qg, kg = sbw("qg", [128, KD, N]), sbw("kg", [128, KD, N])
        wv, wo, rows = sbw("wv", [LAT, D]), sbw("wo", [128, KD, D]), sbw("rows", [T, 2, D])
        sem = lambda name: core.sem("la_" + name)
        wo_loaded = sem("wo_loaded")

        with ExitStack() as ctx:
            sb = lambda name, shape: ctx.enter_context(nc.sbuf_tensor("la_" + name, shape, F32))
            w_lat, w_cont, bias = sb("w_lat", [128, KD, 2 * LAT]), sb("w_cont", [128, R1]), sb("bias", [128, 7])
            w_rope = {n: sb(n, [128, KD, R1]) for n in ("wqr", "wqr_turned", "wkr", "wkr_turned")}
            t1 = [sb(f"t1{k}", [128, HI, T]) for k in range(2)]
            t2 = [sb(f"t2{k}", [128, HI, T]) for k in range(2)]
            t3 = [sb(f"t3{k}", [128, HI, T]) for k in range(2)]
            w_loaded, lat_ready, lat_done = sem("w_loaded"), sem("lat_ready"), sem("lat_done")
            cont_ready, cont_used = sem("cont_ready"), sem("cont_used")
            rope_ready, rope_used, turned_ready, gelu_done = sem("rope_ready"), sem("rope_used"), sem("turned_ready"), sem("gelu_done")
            dve_chain = sem("dve_rope")
            B_LAT, B_QC, B_KC, B_QR, B_QT, B_KR, B_KT = range(7)

            with nc.Block() as block:
                @block.sync
                def _(sp):
                    load = lambda t, n: sp.dma_start(t, d[n].rearrange("(c p) n -> p c n", p=128)).then_inc(w_loaded, 16)
                    load(w_lat[:, :, 0:LAT], "L1_attn_wkv")
                    load(w_lat[:, :, LAT:2 * LAT], "L1_attn_wq")
                    sp.dma_start(w_cont[0:LAT, :], d["L1_attn_wkc"]).then_inc(w_loaded, 16)
                    sp.dma_start(w_cont[LAT:2 * LAT, :], d["L1_attn_wqc"]).then_inc(w_loaded, 16)
                    sp.dma_start(bias[:, :], d["la_bias"]).then_inc(w_loaded, 16)
                    load(w_rope["wqr"][:, :, :], "L1_attn_wqr")
                    load(w_rope["wqr_turned"][:, :, :], "wqr_turned")
                    load(w_rope["wkr"][:, :, :], "L1_attn_wkr")
                    load(w_rope["wkr_turned"][:, :, :], "wkr_turned")
                    sp.dma_start(wv[:, :], d["L1_attn_wv"]).then_inc(wo_loaded, 16)
                    sp.dma_start(wo[:, :, :], d["L1_attn_wo"].rearrange("(c p) n -> p c n", p=128)).then_inc(wo_loaded, 16)
                    sp.dma_start(rows[:, :, :], d["la_rows"]).then_inc(wo_loaded, 16)

                @block.tensor
                def _(pe):
                    pe.wait_ge(w_loaded, 16 * 9)
                    for s in range(2):
                        cols = slice(s * HALF, (s + 1) * HALF)
                        x = [core.xt[:, c, cols] for c in range(KD)]
                        wait_past(pe, lat_done, s)
                        accumulate(pe, bank[B_LAT][:, 0:HALF], [(w_lat[:, c, :], x[c]) for c in range(KD)]).then_inc(lat_ready, 1)
                        for n, (name, b) in enumerate((("wqr", B_QR), ("wqr_turned", B_QT), ("wkr", B_KR), ("wkr_turned", B_KT))):
                            if n % 2 == 0:
                                wait_past(pe, rope_used, 2 * (s - 1) + n // 2 + 1 if s else 0)
                            last = accumulate(pe, bank[b][:, 0:HALF], [(w_rope[name][:, c, :], x[c]) for c in range(KD)])
                            if n % 2 == 1:
                                last.then_inc(rope_ready, 1)
                        pe.wait_ge(lat_done, s + 1)
                        wait_past(pe, cont_used, s)
                        pe.matmul(bank[B_KC][:, 0:HALF], w_cont[0:LAT, :], lat[0:LAT, cols], start=True, stop=True)
                        pe.matmul(bank[B_QC][:, 0:HALF], w_cont[LAT:2 * LAT, :], lat[LAT:2 * LAT, cols],
                                  start=True, stop=True).then_inc(cont_ready, 1)

                @block.vector
                def _(dve):
                    chain = Chain(dve, dve_chain, 4)
                    chain.start(0)
                    cos, sin = (core.c(128, k, T).unsqueeze(1).broadcast_to([128, HI, T]) for k in (C_COS, C_SIN))
                    dve.wait_ge(w_loaded, 16 * 9)
                    for s in range(2):
                        for k in range(2):
                            b = B_QR + 2 * k
                            of = lambda n: bank[n][:, 0:HALF].rearrange("d (i t) -> d i t", i=HI)
                            dve.wait_ge(rope_ready, 2 * s + k + 1)
                            dve.scalar_tensor_tensor(t1[k][:, :, :], of(b), bias[:, 3 + 2 * k:4 + 2 * k], cos, ALU.add, ALU.mult)
                            last = dve.scalar_tensor_tensor(t2[k][:, :, :], of(b + 1), bias[:, 4 + 2 * k:5 + 2 * k], sin, ALU.add, ALU.mult)
                            chain.link(last)
                            dve.sem_inc(rope_used, 1)
                            wait_past(dve, gelu_done, 2 * s + k - 1)
                            dve.tensor_tensor(t3[k][:, :, :], t1[k][:, :, :], t2[k][:, :, :], ALU.add).then_inc(turned_ready, 1)

                @block.scalar
                def _(act):
                    act.preload_act_table_set("gelu_and_others")
                    act.wait_ge(w_loaded, 16 * 9)
                    for s in range(2):
                        cols = slice(s * HALF, (s + 1) * HALF)
                        act.wait_ge(lat_ready, s + 1)
                        act.activation(lat[:, cols], bank[B_LAT][:, 0:HALF], ACT.Gelu, bias=bias[:, 0:1]).then_inc(lat_done, 1)
                        act.wait_ge(cont_ready, s + 1)
                        act.activation(qg[:, 0, cols], bank[B_QC][:, 0:HALF], ACT.Gelu, bias=bias[:, 1:2])
                        act.activation(kg[:, 0, cols], bank[B_KC][:, 0:HALF], ACT.Gelu, bias=bias[:, 2:3]).then_inc(cont_used, 1)
                        for k, out in enumerate((qg, kg)):
                            act.wait_ge(turned_ready, 2 * s + k + 1)
                            act.activation(out[:, 1, cols].rearrange("d (i t) -> d i t", i=HI), t3[k][:, :, :], ACT.Gelu).then_inc(gelu_done, 1)

        with ExitStack() as ctx:
            sb = lambda name, shape: ctx.enter_context(nc.sbuf_tensor("la_" + name, shape, F32))
            pair = lambda name, shape: [sb(f"{name}{p}", shape) for p in range(2)]
            q, k_sep, lat_i = pair("q", [128, KD, T]), pair("k_sep", [128, KD, 8, T]), pair("lat_i", [LAT, T])
            v = pair("v", [T, H1, AUG])
            masked = pair("masked", [T, GB, T])
            prob = pair("prob", [T, GB, T])
            prob_t = pair("prob_t", [T, GB, T])
            top = sb("top", [T, H1])
            inv, o, ot = sb("inv", [T, H1, 1]), sb("o", [T, D]), sb("ot", [128, KD, T])
            res, normed = sb("res", [T, D]), sb("normed", [T, D])
            stats, mv, rstd, pad = sb("stats", [T, 6]), sb("mv", [T, 2]), sb("rstd", [T, 1]), sb("pad", [T, 1])
            ones_set, sep_ready, v_ready, v_copied, s_ready = sem("ones_set"), sem("sep_ready"), sem("v_ready"), sem("v_copied"), sem("s_ready")
            s_used, masked_ready, e_done, et_ready, et_copied, o_ready = (
                sem("s_used"), sem("masked_ready"), sem("e_done"), sem("et_ready"), sem("et_copied"), sem("o_ready"))
            on_ready, ot_ready, ot_copied, out_ready = sem("on_ready"), sem("ot_ready"), sem("ot_copied"), sem("out_ready")
            var_ready, rstd_ready, normed_ready, nt_ready, nt_copied = (
                sem("var_ready"), sem("rstd_ready"), sem("normed_ready"), sem("nt_ready"), sem("nt_copied"))
            dve_chain, act_chain = sem("dve"), sem("act")

            with nc.Block() as block:
                @block.gpsimd
                def _(pool):
                    def front(i, p):
                        wait_past(pool, s_ready, NG * (i - 1))
                        for c in range(KD):
                            pool.tensor_tensor(k_sep[p][:, c, :, :], kg[:, c, bass.ts(i, T)].unsqueeze(1).broadcast_to([128, 8, T]),
                                               core.c(128, C_HEAD, 8).unsqueeze(2).broadcast_to([128, 8, T]), ALU.mult)
                        wait_past(pool, v_ready, i - 1)
                        pool.tensor_copy(lat_i[p][:, :], lat[0:LAT, bass.ts(i, T)])
                        pool.tensor_copy(q[p][:, :, :], qg[:, :, bass.ts(i, T)]).then_inc(sep_ready, 1)

                    for p in range(2):
                        last = pool.memset(v[p][:, :, HD1:AUG], 1.0)
                    last.then_inc(ones_set, 1)
                    skewed(pool, front, nothing)

                @block.tensor
                def _(pe):
                    ident = core.c(128, C_ID, 128)

                    def front(i, p):
                        pe.wait_ge(sep_ready, i + 1)
                        wait_past(pe, v_copied, i)
                        pe.matmul(bank[4][0:T, 0:D], lat_i[p][:, :], wv[:, :], start=True, stop=True).then_inc(v_ready, 1)
                        for j in range(NG):
                            wait_past(pe, s_used, NG * (i - 1) + j + 1 if not isinstance(i, int) or i else 0)
                            heads = slice(j % 2 * GB, (j % 2 + 1) * GB)
                            pe.matmul(bank[j][0:T, 0:GB * T], q[p][:, j // 2, :],
                                      k_sep[p][:, j // 2, heads, :].rearrange("d h t -> d (h t)"), start=True, stop=True).then_inc(s_ready, 1)

                    def weigh(i, p, j):
                        pe.wait_ge(et_copied, NG * i + j + 1)
                        if j == 0:
                            pe.wait_ge(v_copied, i + 1)
                            wait_past(pe, nt_copied, i)
                        for hh in range(GB):
                            h = GB * j + hh
                            last = pe.matmul(bank[7][0:T, h * AUG:(h + 1) * AUG], prob_t[j % 2][:, hh, :], v[p][:, h, :],
                                             start=True, stop=True)
                        if j == NG - 1:
                            last.then_inc(o_ready, 1)

                    def back(i, p):
                        for j in range(NG):
                            pe.wait_ge(e_done, NG * i + j + 1)
                            if j >= 2:
                                pe.wait_ge(et_copied, NG * i + j - 1)
                            for hh in range(GB):
                                last = pe.transpose(bank[5 + j % 2][0:T, hh * T:(hh + 1) * T], prob[j % 2][:, hh, :], ident[0:T, 0:T])
                            last.then_inc(et_ready, 1)
                            if j > 0:
                                weigh(i, p, j - 1)
                        weigh(i, p, NG - 1)
                        pe.wait_ge(on_ready, i + 1)
                        for c in range(KD):
                            last = pe.transpose(bank[5][:, c * T:(c + 1) * T], o[:, c * 128:(c + 1) * 128], ident[0:T, 0:T])
                        last.then_inc(ot_ready, 1)
                        pe.wait_ge(ot_copied, i + 1)
                        accumulate(pe, bank[6][0:T, 0:D], [(ot[:, c, :], wo[:, c, :]) for c in range(KD)]).then_inc(out_ready, 1)
                        pe.wait_ge(normed_ready, i + 1)
                        for c in range(KD):
                            last = pe.transpose(bank[7][:, c * T:(c + 1) * T], normed[:, c * 128:(c + 1) * 128], ident[0:T, 0:T])
                        last.then_inc(nt_ready, 1)

                    pe.wait_ge(wo_loaded, 48)
                    skewed(pe, front, back)

                @block.vector
                def _(dve):
                    chain = Chain(dve, dve_chain, 2 * NG + 6)

                    def front(i, p):
                        dve.wait_ge(v_ready, i + 1)
                        wait_past(dve, o_ready, i - 1)
                        dve.tensor_tensor(v[p][:, :, 0:HD1], bank[4][0:T, 0:D].rearrange("t (h e) -> t h e", h=H1),
                                          rows[:, 0, :].rearrange("t (h e) -> t h e", h=H1), ALU.add).then_inc(v_copied, 1)

                    def back(i, p):
                        chain.start(i)
                        for j in range(NG):
                            dve.wait_ge(s_ready, NG * i + j + 1)
                            m = masked[j % 2]
                            t = top[:, GB * j:GB * (j + 1)]
                            wait_past(dve, e_done, NG * i + (j - 1 if j > 1 else 0))
                            chain.link(dve.tensor_tensor(m[:, :, :], bank[j][0:T, 0:GB * T].rearrange("t (h s) -> t h s", h=GB),
                                                         core.c(T, C_CAUSAL, T).unsqueeze(1).broadcast_to([T, GB, T]), ALU.add))
                            dve.sem_inc(s_used, 1)
                            chain.link(dve.tensor_reduce(t, m[:, :, :], AX_X, ALU.max))
                            dve.tensor_tensor(m[:, :, :], m[:, :, :], t.unsqueeze(2).broadcast_to([T, GB, T]),
                                              ALU.subtract).then_inc(masked_ready, 1)
                        dve.wait_ge(o_ready, i + 1)
                        av = bank[7][0:T, 0:H1 * AUG].rearrange("t (h e) -> t h e", h=H1)
                        chain.link(dve.reciprocal(inv[:, :, :], av[:, :, HD1:AUG]))
                        dve.tensor_tensor(o[:, :].rearrange("t (h e) -> t h e", h=H1), av[:, :, 0:HD1],
                                          inv[:, :, :].broadcast_to([T, H1, HD1]), ALU.mult).then_inc(on_ready, 1)
                        chain.link(dve.tensor_tensor(res[:, :], core.x[:, i, :], rows[:, 1, :], ALU.add))
                        dve.wait_ge(out_ready, i + 1)
                        chain.link(dve.tensor_tensor(res[:, :], bank[6][0:T, 0:D], res[:, :], ALU.add))
                        chain.link(dve.bn_stats(stats[:, :], res[:, :]))
                        dve.memset(pad[:, :], 0.0)
                        chain.link(dve.bn_aggr(mv[:, :], stats[:, :]))
                        dve.tensor_scalar(mv[:, 1:2], mv[:, 1:2], EPS, None, ALU.add).then_inc(var_ready, 1)
                        dve.wait_ge(rstd_ready, i + 1)
                        chain.link(dve.tensor_scalar(normed[:, :], res[:, :], mv[:, 0:1], rstd[:, :], ALU.subtract, ALU.mult))
                        dve.sem_inc(normed_ready, 1)
                        dve.tensor_copy(core.x[:, i, :], normed[:, :])

                    dve.wait_ge(ones_set, 1)
                    dve.wait_ge(wo_loaded, 48)
                    skewed(dve, front, back)

                @block.scalar
                def _(act):
                    chain = Chain(act, act_chain, 1)
                    act.preload_act_table_set(EXP_LN)

                    def back(i, p):
                        chain.start(i)

                        def turn(j):
                            act.wait_ge(et_ready, NG * i + j + 1)
                            act.copy(prob_t[j % 2][:, :, :], bank[5 + j % 2][0:T, 0:GB * T].rearrange("s (h t) -> s h t", h=GB)).then_inc(et_copied, 1)

                        for j in range(NG):
                            act.wait_ge(masked_ready, NG * i + j + 1)
                            act.activation(prob[j % 2][:, :, :], masked[j % 2][:, :, :], ACT.Exp, scale=HD1 ** -0.5).then_inc(e_done, 1)
                            if j > 0:
                                turn(j - 1)
                        turn(NG - 1)
                        act.wait_ge(ot_ready, i + 1)
                        act.copy(ot[:, :, :], bank[5][:, 0:KD * T].rearrange("d (c t) -> d c t", c=KD)).then_inc(ot_copied, 1)
                        act.wait_ge(var_ready, i + 1)
                        chain.link(act.activation(rstd[:, :], mv[:, 1:2], ACT.Ln))
                        act.activation(rstd[:, :], rstd[:, :], ACT.Exp, scale=-0.5).then_inc(rstd_ready, 1)
                        act.wait_ge(nt_ready, i + 1)
                        act.copy(core.xt[:, :, bass.ts(i, T)], bank[7][:, 0:KD * T].rearrange("d (c t) -> d c t", c=KD)).then_inc(nt_copied, 1)

                    skewed(act, nothing, back)


def build(nc, d, out):
    with ExitStack() as ctx:
        core = Core(nc, ctx)
        with ExitStack() as layer:
            sb = lambda name, shape: layer.enter_context(nc.sbuf_tensor(name, shape, F32))
            core.w_in = sb("w_in", [128, KD, W_IN])
            zs = sb("zs", [T, B, DI])
            dt, dta = sb("dt", [T, B, H0]), sb("dta", [T, B, H0])
            cosine, sine = sb("cosine", [T, B * H0, PAIRS]), sb("sine", [T, B * H0, PAIRS])
            project_time_and_gate(core, d, zs, dt, dta, cosine, sine)
            state_space(core, d, zs, dt, dta, cosine, sine)
        core.free_semaphores()
        cross_attention(core, d, 0)
        mixture(core, d)
        latent_attention(core, d)
        cross_attention(core, d, 1)
        low_rank_experts(core, d, out)


_AS_THEY_ARE = [
    "L0_attn_W_in", "L0_attn_W_out", "L0_xattn_Wq", "L0_xattn_Wk", "L0_xattn_Wv", "L0_xattn_Wo", "L0_ffn_Wg", "L0_ffn_W1",
    "L0_ffn_W2", "L1_attn_wq", "L1_attn_wqc", "L1_attn_wqr", "L1_attn_wkv", "L1_attn_wkr", "L1_attn_wkc", "L1_attn_wv",
    "L1_attn_wo", "L1_xattn_Wq", "L1_xattn_Wk", "L1_xattn_Wv", "L1_xattn_Wo",
]


def _layout(inputs):
    a = {n: np.ascontiguousarray(inputs[n]) for n in inputs}
    row = lambda n: np.broadcast_to(a[n].reshape(1, -1), (T, a[n].size))
    d = {n: a[n] for n in _AS_THEY_ARE}
    d["x"] = a["x"]
    d["xt"] = a["x"].reshape(N, D).T
    d["xt_items"] = a["x"].transpose(0, 2, 1)
    twice = lambda m, axis: np.concatenate([m, np.take(m, np.arange(128, DC), axis=axis)], axis=axis)
    d["ctx_t"] = np.pad(twice(a["ctx_768"].transpose(0, 2, 1), 1), ((0, 0), (0, 0), (0, SE - S)))
    for n in ("L0_xattn_Wk", "L0_xattn_Wv", "L1_xattn_Wk", "L1_xattn_Wv"):
        d[n] = twice(a[n], 0)
    d["const"] = constants()
    d["rows"] = np.concatenate([row("L0_attn_dt_bias"), row("L0_attn_A_log"), row("L0_attn_D_skip")], axis=1)
    d["norm_w"] = a["L0_attn_norm_weight"].reshape(4, 128).T
    d["L0_bo"] = a["L0_xattn_bo"].reshape(1, D)
    d["L1_bo"] = a["L1_xattn_bo"].reshape(1, D)
    turned = lambda n: np.concatenate([a[n][..., R1 // 2:], a[n][..., :R1 // 2]], axis=-1)
    d["wqr_turned"], d["wkr_turned"] = turned("L1_attn_wqr"), turned("L1_attn_wkr")
    d["la_bias"] = np.stack([
        np.concatenate([a["L1_attn_bkv"], a["L1_attn_bq"]]), a["L1_attn_bqc"], a["L1_attn_bkc"],
        a["L1_attn_bqr"], turned("L1_attn_bqr"), a["L1_attn_bkr"], turned("L1_attn_bkr")], axis=1)
    d["la_rows"] = np.stack([row("L1_attn_bv"), row("L1_attn_bo")], axis=1)
    d["base_wt"] = a["L1_ffn_base_w"].T
    d["router_wt"] = a["L1_ffn_router_w"].T
    d["lora_a"] = a["L1_ffn_lora_A"]
    d["lora_b"] = a["L1_ffn_lora_B"].reshape(E1 * RK, D)
    d["ffn_bias"] = np.concatenate([a["L1_ffn_base_b"], a["L1_ffn_router_b"], np.zeros(RK, np.float32)]).reshape(1, -1)
    return {n: np.ascontiguousarray(v) for n, v in d.items()}


def kernel(**inputs):
    import concourse.bacc as _bacc
    from concourse.bass_utils import run_bass_kernel_spmd as _run

    nc = _bacc.Bacc("TRN2", target_bir_lowering=False, num_devices=1)
    arrays = _layout({n: np.asarray(v) for n, v in inputs.items()})
    d = {n: nc.dram_tensor(f"in_{n}", v.shape, mybir.dt.from_np(v.dtype), kind="ExternalInput").ap() for n, v in arrays.items()}
    out = nc.dram_tensor("out", (B, T, D), F32, kind="ExternalOutput").ap()
    build(nc, d, out)
    r = _run(nc, [{f"in_{n}": v for n, v in arrays.items()}], core_ids=[0])
    return r.results[0]["out"]
```

```python
from contextlib import ExitStack

import numpy as np

import concourse.bass as bass
from concourse import mybir

F32 = mybir.dt.float32
F32R = mybir.dt.float32r
BF16 = mybir.dt.bfloat16
ALU = mybir.AluOpType
ACT = mybir.ActivationFunctionType
AX_X = mybir.AxisListType.X
EXP_LN = "natural_log_exp_and_others"

B, T, D = 8, 112, 256
N = B * T
S, DC = 375, 192
KD = D // 128
ST, SP_ = 3, S // 3
SE = S + 1
CB = DC - 128
EPS = 1e-5
H0, P0, NS, PAIRS = 8, 64, 64, 16
DI = H0 * P0
W_IN = 2 * DI + 2 * NS + H0
ROUND = 1.5 * 2.0 ** 23
TURN = 6.2831850
INNER = 1024
E0, F0, FM = 8, 512, 4
H1, HD1, R1 = 16, 16, 128
LAT = 64
E1, RK = 8, 8
W_LORA = D + E1 + RK

C_ID = 0
C_TRI = C_ID + 128
C_AFTER = C_TRI + T
C_CAUSAL = C_AFTER + T
C_COS = C_CAUSAL + T
C_SIN = C_COS + T
C_FREQ = C_SIN + T
C_HEAD = C_FREQ + PAIRS
C_PRIO = C_HEAD + 8
C_ONE = C_PRIO + E0
C_EPS = C_ONE + 128
C_END = C_EPS + 1

R_DTB, R_ALOG, R_DSKIP = 0, H0, 2 * H0
R_END = 3 * H0


def constants():
    c = np.zeros((128, C_END), np.float32)
    r = np.arange(T)
    c[:, C_ID:C_ID + 128] = np.eye(128)
    c[:T, C_TRI:C_TRI + T] = r[:, None] <= r[None, :]
    c[:T, C_AFTER:C_AFTER + T] = r[:, None] > r[None, :]
    c[:T, C_CAUSAL:C_CAUSAL + T] = np.where(r[None, :] > r[:, None], -1e30, 0.0)
    freq = (1.0 / np.float32(10000.0) ** (np.arange(0, R1, 2, dtype=np.float32) / np.float32(R1))).astype(np.float32)
    angle = (r.astype(np.float32)[None, :] * np.concatenate([freq, freq])[:, None]).astype(np.float32)
    c[:, C_COS:C_COS + T] = np.cos(angle)
    sign = np.where(np.arange(R1) < R1 // 2, -1.0, 1.0)
    c[:, C_SIN:C_SIN + T] = np.sin(angle) * sign[:, None]
    inv = 1.0 / np.float32(10000.0) ** (np.arange(PAIRS, dtype=np.float32) / np.float32(PAIRS))
    c[:, C_FREQ:C_FREQ + PAIRS] = inv.astype(np.float64) / (2 * np.pi)
    c[:, C_HEAD:C_HEAD + 8] = (np.arange(128) // HD1)[:, None] == np.arange(8)[None, :]
    c[:, C_PRIO:C_PRIO + E0] = E0 - np.arange(E0)
    c[:, C_ONE:C_ONE + 128] = 1.0
    c[:, C_EPS] = EPS
    return c


def accumulate(pe, out, pairs):
    last = None
    for k, (lhs, rhs) in enumerate(pairs):
        last = pe.matmul(out, lhs, rhs, start=(k == 0), stop=(k == len(pairs) - 1))
    return last


def split_products(lhs_high, lhs_low, rhs_high, rhs_low):
    return [(lhs_high, rhs_high), (lhs_high, rhs_low), (lhs_low, rhs_high)]


def exact_products(lhs, rhs):
    return [(lhs["high"], rhs["high"]), (lhs["high"], rhs["low"]), (lhs["low"], rhs["high"]),
            (lhs["rest"], rhs["rest"]), (lhs["last"], rhs["last"])]


def wait_past(eng, sem, value):
    if not isinstance(value, int) or value > 0:
        eng.wait_ge(sem, value)


class Chain:

    def __init__(self, eng, sem, links):
        self.eng, self.sem, self.links, self.item, self.done = eng, sem, links, 0, links

    def start(self, item):
        assert self.done == self.links, f"{self.sem.name}: {self.done} links"
        self.item, self.done = item, 0

    def resume(self, item, done):
        self.item, self.done = item, done

    def link(self, ins):
        self.done += 1
        ins.then_inc(self.sem, 1)
        self.eng.wait_ge(self.sem, self.item * self.links + self.done)


def skewed(eng, front, back):
    front(0, 0)
    front(1, 1)
    back(0, 0)
    with eng.Fori(0, B // 2 - 1) as j:
        front(2 * j + 2, 0)
        back(2 * j + 1, 1)
        front(2 * j + 3, 1)
        back(2 * j + 2, 0)
    back(B - 1, 1)


def overlapped(eng, round_):
    round_(-1, 1, True, False, False)
    round_(0, 0, True, True, False)
    with eng.Fori(0, B // 2 - 1) as j:
        round_(2 * j + 1, 1, True, True, True)
        round_(2 * j + 2, 0, True, True, True)
    round_(B - 1, 1, False, True, True)
    round_(B, 0, False, False, True)


def nothing(item, p):
    pass


class Core:

    def __init__(self, nc, ctx):
        self.nc = nc
        self.phase_sems = []
        sb = lambda name, shape: ctx.enter_context(nc.sbuf_tensor(name, shape, F32))
        self.x = sb("x", [T, B, D])
        self.xt = sb("xt", [128, KD, N])
        self.const = sb("const", [128, C_END])
        self.rows = sb("rows", [T, R_END])
        self.bank = [ctx.enter_context(nc.psum_tensor(f"bank{k}", [128, 512], F32)) for k in range(8)]
        self.loaded = ctx.enter_context(nc.semaphore("const_loaded"))
        self.wq, self.wk, self.wv = sb("wq", [128, KD, INNER]), sb("wk", [128, 2, INNER]), sb("wv", [128, 2, INNER])
        self.wo, self.bo = sb("wo", [128, INNER // 128, D]), sb("bo", [1, D])
        self.xw_loaded = ctx.enter_context(nc.semaphore("cross_weights_loaded"))
        self.w_lat, self.w_cont, self.la_bias = sb("w_lat", [128, KD, 2 * LAT]), sb("w_cont", [128, R1]), sb("la_bias", [128, 7])
        self.w_rope = {n: sb(n, [128, KD, R1]) for n in ("wqr", "wqr_turned", "wkr", "wkr_turned")}
        self.la_wv, self.la_wo, self.la_rows = sb("la_wv", [LAT, D]), sb("la_wo", [128, KD, D]), sb("la_rows", [T, 2, D])
        self.la_loaded, self.wo_loaded = (ctx.enter_context(nc.semaphore(n)) for n in ("la_loaded", "la_wo_loaded"))
        self.lora_w, self.lora_bias, self.lora_b = sb("lora_w", [128, KD, W_LORA]), sb("lora_bias", [1, W_LORA]), sb("lora_b", [E1 * RK, D])
        self.lora_loaded = ctx.enter_context(nc.semaphore("lora_loaded"))

    def sem(self, name):
        self.phase_sems.append(self.nc.alloc_semaphore(name=name))
        return self.phase_sems[-1]

    def free_semaphores(self):
        self.nc.clear_and_free_semaphores(self.phase_sems)
        self.phase_sems = []
        self.nc.all_engine_barrier()

    def load_cross_weights(self, sp, d, layer):
        name = f"L{layer}_xattn_W"
        sp.dma_start(self.wk[:, :, :], d[name + "k"].rearrange("(c p) n -> p c n", p=128)).then_inc(self.xw_loaded, 16)
        sp.dma_start(self.wv[:, :, :], d[name + "v"].rearrange("(c p) n -> p c n", p=128)).then_inc(self.xw_loaded, 16)
        sp.dma_start(self.wq[:, :, :], d[name + "q"].rearrange("(c p) n -> p c n", p=128)).then_inc(self.xw_loaded, 16)
        sp.dma_start(self.wo[:, :, :], d[name + "o"].rearrange("(c p) n -> p c n", p=128)).then_inc(self.xw_loaded, 16)
        sp.dma_start(self.bo[:, :], d[f"L{layer}_bo"]).then_inc(self.xw_loaded, 16)

    def load_latent_weights(self, sp, d):
        load = lambda t, n: sp.dma_start(t, d[n].rearrange("(c p) n -> p c n", p=128)).then_inc(self.la_loaded, 16)
        load(self.w_lat[:, :, 0:LAT], "L1_attn_wkv")
        load(self.w_lat[:, :, LAT:2 * LAT], "L1_attn_wq")
        sp.dma_start(self.w_cont[0:LAT, :], d["L1_attn_wkc"]).then_inc(self.la_loaded, 16)
        sp.dma_start(self.w_cont[LAT:2 * LAT, :], d["L1_attn_wqc"]).then_inc(self.la_loaded, 16)
        sp.dma_start(self.la_bias[:, :], d["la_bias"]).then_inc(self.la_loaded, 16)
        load(self.w_rope["wqr"][:, :, :], "L1_attn_wqr")
        load(self.w_rope["wqr_turned"][:, :, :], "wqr_turned")
        load(self.w_rope["wkr"][:, :, :], "L1_attn_wkr")
        load(self.w_rope["wkr_turned"][:, :, :], "wkr_turned")
        sp.dma_start(self.la_wv[:, :], d["L1_attn_wv"]).then_inc(self.wo_loaded, 16)
        sp.dma_start(self.la_wo[:, :, :], d["L1_attn_wo"].rearrange("(c p) n -> p c n", p=128)).then_inc(self.wo_loaded, 16)
        sp.dma_start(self.la_rows[:, :, :], d["la_rows"]).then_inc(self.wo_loaded, 16)

    def load_lora_weights(self, sp, d):
        w = self.lora_w
        for at, end, n in ((0, D, "base_wt"), (D, D + E1, "router_wt"), (D + E1, W_LORA, "lora_a")):
            sp.dma_start(w[:, :, at:end], d[n].rearrange("(c p) n -> p c n", p=128)).then_inc(self.lora_loaded, 16)
        sp.dma_start(self.lora_bias[:, :], d["ffn_bias"]).then_inc(self.lora_loaded, 16)
        sp.dma_start(self.lora_b[:, :], d["lora_b"]).then_inc(self.lora_loaded, 16)

    def c(self, rows, start, width):
        return self.const[0:rows, start:start + width]


def project_time_and_gate(core, d, zs, dt, dta, cosine, sine):
    nc = core.nc
    bank = core.bank
    with ExitStack() as ctx:
        sb = lambda name, shape: ctx.enter_context(nc.sbuf_tensor(name, shape, F32))
        raw = sb("dt_raw", [T, B, H0])
        mag = sb("dt_mag", [T, B, H0])
        soft = sb("dt_soft", [T, B, H0])
        rate = sb("rate", [T, H0])
        turns = sb("turns", [T, B * H0, PAIRS])
        whole = sb("whole", [T, B * H0, PAIRS])
        sin_in = sb("sin_in", [T, B * H0, PAIRS])
        cos_in = sb("cos_in", [T, B * H0, PAIRS])
        x_loaded, w_loaded = core.sem("p1_x_loaded"), core.sem("p1_w_loaded")
        dt_ready, mag_ready, soft_ready = core.sem("dt_ready"), core.sem("dt_mag_ready"), core.sem("dt_soft_ready")
        rate_ready, steps_ready = core.sem("rate_ready"), core.sem("steps_ready")
        time_ready, z_ready, z_used = core.sem("time_ready"), core.sem("z_ready"), core.sem("z_used")
        angles_ready, act_chain, dve_chain = core.sem("angles_ready"), core.sem("p1_act"), core.sem("p1_dve")
        w_out_loaded, w_scaled = core.sem("w_out_loaded"), core.sem("w_scaled")
        ZB = 4

        with nc.Block() as block:
            @block.sync
            def _(sp):
                sp.dma_start(core.xt[:, :, :], d["xt"].rearrange("(c p) n -> p c n", p=128)).then_inc(x_loaded, 16)
                sp.dma_start(core.w_in[:, :, :], d["L0_attn_W_in"].rearrange("(c p) n -> p c n", p=128)).then_inc(w_loaded, 16)
                sp.dma_start(core.const[:, :], d["const"]).then_inc(core.loaded, 16)
                sp.dma_start(core.rows[:, :], d["rows"]).then_inc(core.loaded, 16)
                for i in range(2):
                    sp.dma_start(core.xt_in[i][:, :, :], d["xt_items"][i].rearrange("(c p) n -> p c n", p=128)
                                 ).then_inc(core.item_loaded[i], 16)
                sp.dma_start(core.w_out[:, :, :], d["L0_attn_W_out"].rearrange("(c p) n -> p c n", p=128)).then_inc(w_out_loaded, 16)
                sp.dma_start(core.w_norm[:, :], d["norm_w"]).then_inc(w_out_loaded, 16)
                sp.dma_start(core.x[:, :, :], d["x"].rearrange("b t d -> t b d")).then_inc(core.state_loaded, 16)

            @block.tensor
            def _(pe):
                def z(i):
                    if i >= ZB:
                        pe.wait_ge(z_used, i - ZB + 1)
                    accumulate(pe, bank[1 + i % ZB][0:T, :], [
                        (core.xt[:, c, i * T:(i + 1) * T], core.w_in[:, c, 0:DI]) for c in range(KD)]).then_inc(z_ready, 1)

                pe.wait_ge(x_loaded, 16)
                pe.wait_ge(w_loaded, 16)
                for i in range(B):
                    last = accumulate(pe, bank[0][0:T, i * H0:(i + 1) * H0], [
                        (core.xt[:, c, i * T:(i + 1) * T], core.w_in[:, c, W_IN - H0:W_IN]) for c in range(KD)])
                last.then_inc(dt_ready, 1)
                for i in range(ZB):
                    z(i)
                pe.wait_ge(core.loaded, 32)
                pe.wait_ge(steps_ready, 1)
                pe.matmul(bank[5][0:T, 0:B * H0], core.c(T, C_TRI, T), dt[:, :, :].rearrange("t b h -> t (b h)"),
                          start=True, stop=True).then_inc(time_ready, 1)
                for i in range(ZB, B):
                    z(i)

            @block.vector
            def _(dve):
                chain = Chain(dve, dve_chain, 6)
                chain.start(0)
                row = lambda k: core.rows[:, k:k + H0].unsqueeze(1).broadcast_to([T, B, H0])
                dve.wait_ge(core.loaded, 32)
                dve.wait_ge(dt_ready, 1)
                chain.link(dve.tensor_tensor(raw[:, :, :], bank[0][0:T, 0:B * H0].rearrange("t (b h) -> t b h", b=B),
                                             row(R_DTB), ALU.add))
                dve.scalar_tensor_tensor(mag[:, :, :], raw[:, :, :], -1.0, raw[:, :, :], ALU.mult, ALU.max).then_inc(mag_ready, 1)
                dve.wait_ge(soft_ready, 1)
                chain.link(dve.scalar_tensor_tensor(dt[:, :, :], raw[:, :, :], 0.0, soft[:, :, :], ALU.max, ALU.add))
                dve.wait_ge(rate_ready, 1)
                dve.scalar_tensor_tensor(dta[:, :, :], dt[:, :, :], -1.0, rate[:, :].unsqueeze(1).broadcast_to([T, B, H0]),
                                         ALU.mult, ALU.mult).then_inc(steps_ready, 1)
                dve.wait_ge(w_out_loaded, 32)
                dve.tensor_tensor(core.w_out[:, :, :], core.w_out[:, :, :], core.w_norm[:, :].unsqueeze(2).broadcast_to([128, 4, D]),
                                  ALU.mult).then_inc(w_scaled, 1)
                dve.wait_ge(w_scaled, 1)
                dve.wait_ge(time_ready, 1)
                shape = [T, B * H0, PAIRS]
                chain.link(dve.tensor_tensor(turns[:, :, :], bank[5][0:T, 0:B * H0].unsqueeze(2).broadcast_to(shape),
                                             core.c(T, C_FREQ, PAIRS).unsqueeze(1).broadcast_to(shape), ALU.mult))
                chain.link(dve.tensor_scalar(whole[:, :, :], turns[:, :, :], ROUND, ROUND, ALU.add, ALU.subtract))
                chain.link(dve.tensor_tensor(sin_in[:, :, :], turns[:, :, :], whole[:, :, :], ALU.subtract))
                dve.tensor_scalar(cos_in[:, :, :], sin_in[:, :, :], 0.25, None, ALU.add)
                chain.link(dve.tensor_scalar(whole[:, :, :], sin_in[:, :, :], 0.25, 0.5, ALU.add, ALU.is_gt))
                dve.tensor_tensor(cos_in[:, :, :], cos_in[:, :, :], whole[:, :, :], ALU.subtract).then_inc(angles_ready, 1)

            @block.scalar
            def _(act):
                chain = Chain(act, act_chain, 1)
                chain.start(0)
                act.preload_act_table_set(EXP_LN)
                act.wait_ge(core.loaded, 32)
                act.activation(rate[:, :], core.rows[:, R_ALOG:R_ALOG + H0], ACT.Exp).then_inc(rate_ready, 1)
                act.wait_ge(mag_ready, 1)
                chain.link(act.activation(soft[:, :, :], mag[:, :, :], ACT.Exp, scale=-1.0))
                act.activation(soft[:, :, :], soft[:, :, :], ACT.Ln, bias=core.c(T, C_ONE, 1)).then_inc(soft_ready, 1)
                act.preload_act_table_set("silu_and_others")
                for i in range(B):
                    act.wait_ge(z_ready, i + 1)
                    act.activation(zs[:, i, :], bank[1 + i % ZB][0:T, :], ACT.Silu).then_inc(z_used, 1)
                act.wait_ge(angles_ready, 1)
                act.activation(sine[:, :, :], sin_in[:, :, :], ACT.Sin, scale=TURN)
                act.activation(cosine[:, :, :], cos_in[:, :, :], ACT.Sin, scale=TURN)


def state_space(core, d, zs, dt, dta, cosine, sine):
    nc = core.nc
    bank = core.bank
    with ExitStack() as ctx:
        sb = lambda name, shape: ctx.enter_context(nc.sbuf_tensor(name, shape, F32))
        pair = lambda name, shape: [sb(f"{name}{p}", shape) for p in range(2)]
        w_out, xt_in = core.w_out, core.xt_in
        bc = sb("bc", [T, 2, NS])
        rot = pair("rot", [T, 2, H0, NS])
        prod = [sb(f"prod{k}", [T, 2, H0, PAIRS]) for k in range(4)]
        xs = sb("xs", [T, DI])
        xs_dt, xs_skip = pair("xs_dt", [T, DI]), pair("xs_skip", [T, DI])
        lower = sb("lower", [T, H0, T])
        decay = pair("decay", [T, H0, T])
        rot_t = sb("rot_t", [128, 2, 4, T])
        mix = sb("mix", [T, H0, T])
        y, y2, sq = sb("y", [T, DI]), sb("y2", [T, DI]), sb("sq", [T, DI])
        y_t = sb("y_t", [128, 4, T])
        ssq, rms = sb("ssq", [T, 1]), sb("rms", [T, 1])
        res, normed = sb("res", [T, D]), sb("normed", [T, D])
        stats, mv, rstd, pad = sb("stats", [T, 6]), sb("mv", [T, 2]), sb("rstd", [T, 1]), sb("pad", [T, 1])
        sem = lambda name: core.sem("ss_" + name)
        x_loaded, state_loaded = core.item_loaded, core.state_loaded
        xs_ready, bc_ready, xs_copied, bc_copied = sem("xs_ready"), sem("bc_ready"), sem("xs_copied"), sem("bc_copied")
        lower_ready, logdecay_ready, exp_done, decay_ready = sem("lower_ready"), sem("logdecay_ready"), sem("exp_done"), sem("decay_ready")
        rot_copied, rot_ready, xdt_ready, skip_ready = sem("rot_copied"), sem("rot_ready"), sem("xdt_ready"), sem("skip_ready")
        turned, turned_copied = sem("turned"), sem("turned_copied")
        scores_ready, mix_ready, y_ready, y2_ready = sem("scores_ready"), sem("mix_ready"), sem("y_ready"), sem("y2_ready")
        yt_ready, yt_copied, rms_ready, out_ready = sem("yt_ready"), sem("yt_copied"), sem("rms_ready"), sem("out_ready")
        var_ready, rstd_ready, normed_ready, nt_ready, nt_copied = (
            sem("var_ready"), sem("rstd_ready"), sem("normed_ready"), sem("nt_ready"), sem("nt_copied"))
        front_chain, middle_chain, end_chain, act_chain = sem("dve_front"), sem("dve_middle"), sem("dve_end"), sem("act")

        with nc.Block() as block:
            @block.sync
            def _(sp):
                def load(i, p):
                    wait_past(sp, xs_ready, i - 1)
                    sp.dma_start(xt_in[p][:, :, :], d["xt_items"][i].rearrange("(c p) n -> p c n", p=128)).then_inc(x_loaded[p], 16)

                core.load_cross_weights(sp, d, 0)
                with sp.Fori(1, B // 2) as k:
                    load(2 * k, 0)
                    load(2 * k + 1, 1)

            @block.tensor
            def _(pe):
                ident = core.c(128, C_ID, 128)

                def project(i, p):
                    pe.wait_ge(x_loaded[p], 8 * i + 16 - 8 * p)
                    wait_past(pe, xs_copied, i)
                    accumulate(pe, bank[1][0:T, :], [
                        (xt_in[p][:, c, :], core.w_in[:, c, DI:2 * DI]) for c in range(KD)])
                    wait_past(pe, rot_copied, i)
                    accumulate(pe, bank[2][0:T, 0:2 * NS], [
                        (xt_in[p][:, c, :], core.w_in[:, c, 2 * DI:2 * DI + 2 * NS]) for c in range(KD)]).then_inc(xs_ready, 1)

                def log_decay(i):
                    pe.wait_ge(lower_ready, i + 1)
                    wait_past(pe, exp_done, i)
                    for h in range(H0):
                        last = pe.matmul(bank[3 + h // 4][0:T, h % 4 * T:(h % 4 + 1) * T], lower[:, h, :],
                                         core.c(T, C_TRI, T), start=True, stop=True)
                    last.then_inc(logdecay_ready, 1)

                def turn(i, p):
                    pe.wait_ge(rot_ready, i + 1)
                    pe.wait_ge(rot_copied, i + 1)
                    wait_past(pe, y2_ready, i)
                    wait_past(pe, nt_copied, i - 1)
                    for g in range(2):
                        for m in range(4):
                            last = pe.transpose(bank[5 + g][:, m * T:(m + 1) * T],
                                                rot[p][:, g, 2 * m:2 * m + 2, :].rearrange("t h n -> t (h n)"), ident[0:T, 0:T])
                    last.then_inc(turned, 1)

                def scores(i):
                    pe.wait_ge(turned_copied, 2 * i + 2)
                    wait_past(pe, yt_copied, i)
                    for h in range(H0):
                        half = slice(h % 2 * NS, (h % 2 + 1) * NS)
                        last = pe.matmul(bank[7 * (1 - h % 2)][0:T, h // 2 * T:(h // 2 + 1) * T], rot_t[half, 0, h // 2, :],
                                         rot_t[half, 1, h // 2, :], start=True, stop=True)
                    last.then_inc(scores_ready, 1)

                def weigh(i, p):
                    pe.wait_ge(mix_ready, i + 1)
                    pe.wait_ge(xdt_ready, i + 1)
                    for h in range(H0):
                        last = pe.matmul(bank[5][0:T, h * P0:(h + 1) * P0], mix[:, h, :], xs_dt[p][:, h * P0:(h + 1) * P0],
                                         start=True, stop=True)
                    last.then_inc(y_ready, 1)

                def turn_y(i):
                    pe.wait_ge(y2_ready, i + 1)
                    for m in range(4):
                        last = pe.transpose(bank[7][:, m * T:(m + 1) * T], y2[:, m * 128:(m + 1) * 128], ident[0:T, 0:T])
                    last.then_inc(yt_ready, 1)

                def out_projection(i, alone):
                    pe.wait_ge(yt_copied, i + 1)
                    if alone:
                        wait_past(pe, nt_copied, i)
                    else:
                        pe.wait_ge(turned_copied, 2 * i + 4)
                    accumulate(pe, bank[6][0:T, 0:D], [(y_t[:, m, :], w_out[:, m, :]) for m in range(4)]).then_inc(out_ready, 1)

                def turn_state(i):
                    pe.wait_ge(normed_ready, i + 1)
                    for c in range(KD):
                        last = pe.transpose(bank[6][:, c * T:(c + 1) * T], normed[:, c * 128:(c + 1) * 128], ident[0:T, 0:T])
                    last.then_inc(nt_ready, 1)

                def round_(i, p, front, middle, end):
                    if middle:
                        turn(i, p)
                    if front:
                        project(i + 1, 1 - p)
                    if end:
                        turn_y(i - 1)
                    if middle:
                        scores(i)
                    if front:
                        log_decay(i + 1)
                    if end:
                        out_projection(i - 1, not middle)
                    if middle:
                        weigh(i, p)
                    if end:
                        turn_state(i - 1)

                overlapped(pe, round_)

            @block.vector
            def _(dve):
                chain_f, chain_m, chain_e = Chain(dve, front_chain, 1), Chain(dve, middle_chain, 1), Chain(dve, end_chain, 5)
                dve.wait_ge(state_loaded, 16)

                def steps_below(i):
                    wait_past(dve, logdecay_ready, i)
                    dve.tensor_tensor(lower[:, :, :], core.c(T, C_AFTER, T).unsqueeze(1).broadcast_to([T, H0, T]),
                                      dta[:, i, :].unsqueeze(2).broadcast_to([T, H0, T]), ALU.mult).then_inc(lower_ready, 1)

                def rotate(i, p):
                    chain_f.start(i)
                    dve.wait_ge(bc_copied, i + 1)
                    wait_past(dve, turned, i - 1)
                    shape = [T, 2, H0, PAIRS]
                    c1 = cosine[:, bass.ts(i, H0), :].unsqueeze(1).broadcast_to(shape)
                    s1 = sine[:, bass.ts(i, H0), :].unsqueeze(1).broadcast_to(shape)
                    of = lambda e: bc[:, :, e:2 * PAIRS:2].unsqueeze(2).broadcast_to(shape)
                    dve.tensor_tensor(prod[0][:, :, :, :], of(0), c1, ALU.mult)
                    dve.tensor_tensor(prod[1][:, :, :, :], of(1), s1, ALU.mult)
                    dve.tensor_tensor(prod[2][:, :, :, :], of(1), c1, ALU.mult)
                    chain_f.link(dve.tensor_tensor(prod[3][:, :, :, :], of(0), s1, ALU.mult))
                    dve.tensor_tensor(rot[p][:, :, :, 0:2 * PAIRS:2], prod[0][:, :, :, :], prod[1][:, :, :, :], ALU.add)
                    dve.tensor_tensor(rot[p][:, :, :, 1:2 * PAIRS:2], prod[2][:, :, :, :], prod[3][:, :, :, :],
                                      ALU.subtract).then_inc(rot_ready, 1)

                def scale_x(i, p):
                    dve.wait_ge(xs_copied, i + 1)
                    wait_past(dve, y_ready, i - 1)
                    dve.tensor_tensor(xs_dt[p][:, :].rearrange("t (h p) -> t h p", h=H0),
                                      xs[:, :].rearrange("t (h p) -> t h p", h=H0),
                                      dt[:, i, :].unsqueeze(2).broadcast_to([T, H0, P0]), ALU.mult).then_inc(xdt_ready, 1)

                def copy_turned(i):
                    dve.wait_ge(turned, i + 1)
                    wait_past(dve, scores_ready, i)
                    dve.tensor_copy(rot_t[:, 1, :, :], bank[6][:, 0:4 * T].rearrange("n (m t) -> n m t", m=4)).then_inc(turned_copied, 1)

                def decay_scores(i, p):
                    dve.wait_ge(scores_ready, i + 1)
                    dve.wait_ge(decay_ready, i + 1)
                    wait_past(dve, y_ready, i)
                    for g in range(2):
                        last = dve.tensor_tensor(mix[:, g:H0:2, :], bank[7 * (1 - g)][0:T, 0:4 * T].rearrange("s (h t) -> s h t", h=4),
                                                 decay[p][:, g:H0:2, :], ALU.mult)
                    last.then_inc(mix_ready, 1)

                def gate(i, p):
                    chain_m.start(i)
                    dve.wait_ge(y_ready, i + 1)
                    dve.wait_ge(skip_ready, i + 1)
                    chain_m.link(dve.tensor_tensor(y[:, :], bank[5][0:T, :], xs_skip[p][:, :], ALU.add))
                    wait_past(dve, yt_ready, i)
                    wait_past(dve, rms_ready, i)
                    dve.tensor_tensor(y2[:, :], y[:, :], zs[:, i, :], ALU.mult).then_inc(y2_ready, 1)

                def residual(i):
                    chain_e.start(i)
                    dve.wait_ge(out_ready, i + 1)
                    dve.wait_ge(rms_ready, i + 1)
                    chain_e.link(dve.scalar_tensor_tensor(res[:, :], bank[6][0:T, 0:D], rms[:, :], core.x[:, i, :], ALU.mult, ALU.add))
                    chain_e.link(dve.bn_stats(stats[:, :], res[:, :]))
                    dve.memset(pad[:, :], 0.0)
                    chain_e.link(dve.bn_aggr(mv[:, :], stats[:, :]))
                    dve.tensor_scalar(mv[:, 1:2], mv[:, 1:2], EPS, None, ALU.add).then_inc(var_ready, 1)

                def normalize(i):
                    dve.wait_ge(rstd_ready, i + 1)
                    chain_e.link(dve.tensor_scalar(normed[:, :], res[:, :], mv[:, 0:1], rstd[:, :], ALU.subtract, ALU.mult))
                    dve.sem_inc(normed_ready, 1)
                    chain_e.link(dve.tensor_copy(core.x[:, i, :], normed[:, :]))

                def round_(i, p, front, middle, end):
                    if middle:
                        copy_turned(i)
                    if front:
                        steps_below(i + 1)
                    if middle:
                        decay_scores(i, p)
                    if end:
                        residual(i - 1)
                    if front:
                        rotate(i + 1, 1 - p)
                    if end:
                        normalize(i - 1)
                    if middle:
                        gate(i, p)
                    if front:
                        scale_x(i + 1, 1 - p)

                overlapped(dve, round_)

            @block.scalar
            def _(act):
                chain = Chain(act, act_chain, 4)
                act.preload_act_table_set(EXP_LN)

                def copy_turned(i):
                    act.wait_ge(turned, i + 1)
                    wait_past(act, scores_ready, i)
                    act.copy(rot_t[:, 0, :, :], bank[5][:, 0:4 * T].rearrange("n (m t) -> n m t", m=4)).then_inc(turned_copied, 1)

                def copy_projected(i, p):
                    act.wait_ge(xs_ready, i + 1)
                    wait_past(act, xdt_ready, i)
                    wait_past(act, skip_ready, i)
                    act.copy(xs[:, :], bank[1][0:T, :]).then_inc(xs_copied, 1)
                    wait_past(act, rot_ready, i)
                    act.copy(bc[:, :, :], bank[2][0:T, 0:2 * NS].rearrange("t (g n) -> t g n", g=2)).then_inc(bc_copied, 1)
                    wait_past(act, turned, i - 1)
                    for g in range(2):
                        last = act.copy(rot[p][:, g, :, 2 * PAIRS:NS], bank[2][0:T, g * NS + 2 * PAIRS:(g + 1) * NS]
                                        .unsqueeze(1).broadcast_to([T, H0, NS - 2 * PAIRS]))
                    last.then_inc(rot_copied, 1)

                def exp_decay(i, p):
                    act.wait_ge(logdecay_ready, i + 1)
                    wait_past(act, mix_ready, i - 1)
                    for g in range(2):
                        last = act.activation(decay[p][:, 4 * g:4 * g + 4, :],
                                              bank[3 + g][0:T, 0:4 * T].rearrange("s (h t) -> s h t", h=4), ACT.Exp)
                    last.then_inc(exp_done, 1)

                def copy_y(i):
                    act.wait_ge(yt_ready, i + 1)
                    wait_past(act, out_ready, i)
                    act.copy(y_t[:, :, :], bank[7][:, 0:4 * T].rearrange("n (m t) -> n m t", m=4)).then_inc(yt_copied, 1)

                def root_mean_square(i):
                    chain.start(i)
                    act.wait_ge(y2_ready, i + 1)
                    chain.link(act.activation(sq[:, :], y2[:, :], ACT.Square, accum_out=ssq[:, :]))
                    chain.link(act.activation(ssq[:, :], ssq[:, :], ACT.Ln, bias=core.c(T, C_EPS, 1), scale=1.0 / DI))
                    wait_past(act, var_ready, i)
                    act.activation(rms[:, :], ssq[:, :], ACT.Exp, scale=-0.5).then_inc(rms_ready, 1)

                def deviation(i):
                    act.wait_ge(var_ready, i + 1)
                    chain.link(act.activation(rstd[:, :], mv[:, 1:2], ACT.Ln))
                    chain.link(act.activation(rstd[:, :], rstd[:, :], ACT.Exp, scale=-0.5))
                    act.sem_inc(rstd_ready, 1)

                def copy_state(i):
                    act.wait_ge(nt_ready, i + 1)
                    act.copy(core.xt[:, :, bass.ts(i, T)], bank[6][:, 0:2 * T].rearrange("n (c t) -> n c t", c=KD)).then_inc(nt_copied, 1)

                def round_(i, p, front, middle, end):
                    if middle:
                        copy_turned(i)
                    if end:
                        root_mean_square(i - 1)
                        copy_y(i - 1)
                    if front:
                        copy_projected(i + 1, 1 - p)
                        exp_decay(i + 1, 1 - p)
                    if end:
                        deviation(i - 1)
                        copy_state(i - 1)

                overlapped(act, round_)

            @block.gpsimd
            def _(pool):
                def round_(i, p, front, middle, end):
                    if not front:
                        return
                    n, q = i + 1, 1 - p
                    pool.wait_ge(xs_copied, n + 1)
                    wait_past(pool, y2_ready, n - 1)
                    pool.tensor_tensor(xs_skip[q][:, :].rearrange("t (h p) -> t h p", h=H0),
                                       xs[:, :].rearrange("t (h p) -> t h p", h=H0),
                                       core.rows[:, R_DSKIP:R_DSKIP + H0].unsqueeze(2).broadcast_to([T, H0, P0]),
                                       ALU.mult).then_inc(skip_ready, 1)
                    pool.wait_ge(exp_done, n + 1)
                    pool.tensor_tensor(decay[q][:, :, :], decay[q][:, :, :],
                                       core.c(T, C_TRI, T).unsqueeze(1).broadcast_to([T, H0, T]), ALU.mult).then_inc(decay_ready, 1)

                overlapped(pool, round_)


def cross_attention(core, d, layer):
    nc = core.nc
    G, DH = ((16, 64), (8, 128))[layer]
    PER = 128 // DH
    SCALE = DH ** -0.5
    M = INNER // 128
    bank = core.bank
    OT_A, OT_B, OUT, NT = "ot_a", "ot_b", "out", "nt"
    fronts = [("q", 0), ("q", 1)] + [("k", m) for m in range(M)] + [("v", n) for n in range(2 * ST)]
    NF = len(fronts)
    assert NF == 16 and 2 * NF % G == 0

    TAILS = {3: ((4, 0, OT_A), (5, 1, OT_B)), 6: ((9, 3, OUT),), 10: ((14, 2, NT),)}

    def order(front, tail):
        steps = [[] for _ in range(G)]
        n = 0
        for f in range(NF):
            if front:
                steps[f * G // NF].append((n, *fronts[f]))
                n += 1
            if tail:
                for among, alone, kind in TAILS.get(f, ()):
                    steps[f * G // NF].append((among if front else alone, kind, 0))
                    n += 1
        return steps

    RSTD = 6 * G // NF + 1

    def before(i):
        if isinstance(i, int):
            return NF // 2 * min(i + 1, B) + 2 * max(i - 1, 0)
        return (NF // 2 + 2) * i + (NF // 2 - 2)

    with ExitStack() as ctx:
        sb = lambda name, shape: ctx.enter_context(nc.sbuf_tensor(f"x{layer}_{name}", shape, F32))
        sbr = lambda name, shape: ctx.enter_context(nc.sbuf_tensor(f"x{layer}_{name}", shape, F32R))
        pair = lambda name, shape: [sb(f"{name}{p}", shape) for p in range(2)]
        pair_r = lambda name, shape: [sbr(f"{name}{p}", shape) for p in range(2)]
        ctx_t = pair("ctx_t", [128, 2, SE])
        rest_high = sbr("rest_high", [128, SE])
        ctx_high, ctx_low, ctx_rest = pair_r("ctx_high", [128, SE]), pair_r("ctx_low", [128, SE]), pair_r("ctx_rest", [128, SE])
        w_high, w_low, w_rest, w_rest_low = (
            {n: sbr(f"w{n}_{part}", [rows, INNER]) for n in "kv"}
            for part, rows in (("high", 128), ("low", 128), ("rest", 128), ("rest_low", CB)))
        kt, v, qt = pair("kt", [128, M, S]), pair("v", [SP_, ST, INNER]), pair("qt", [128, M, T])
        prob, prob_t = pair("prob", [T, S]), pair("prob_t", [SP_, ST, T])
        negmax, total, inv = sb("negmax", [T, G]), sb("total", [T, G]), sb("inv", [T, G])
        o, ot = sb("o", [T, INNER]), sb("ot", [128, M, T])
        res, normed = sb("res", [T, D]), sb("normed", [T, D])
        stats, mv, rstd, pad = sb("stats", [T, 6]), sb("mv", [T, 2]), sb("rstd", [T, 1]), sb("pad", [T, 1])
        sem = lambda name: core.sem(f"x{layer}_{name}")
        ctx_loaded = [sem("ctx_loaded0"), sem("ctx_loaded1")]
        chunk_ready, chunk_used = [sem("chunk_ready0"), sem("chunk_ready1")], [sem("chunk_used0"), sem("chunk_used1")]
        s_ready, max_ready, p_ready, pt_ready, pt_copied, pv_done = (
            sem("s_ready"), sem("max_ready"), sem("p_ready"), sem("pt_ready"), sem("pt_copied"), sem("pv_done"))
        o_ready, var_ready, rstd_ready, normed_ready = sem("o_ready"), sem("var_ready"), sem("rstd_ready"), sem("normed_ready")
        dve_chain, act_chain = sem("dve"), sem("act")
        split_chain, split_done, w_rounded, w_split = sem("split_chain"), sem("split_done"), sem("w_rounded"), sem("w_split")

        def rounds(eng, round_):
            round_(-1, 1)
            round_(0, 0)
            with eng.Fori(0, B // 2 - 1) as j:
                round_(2 * j + 1, 1)
                round_(2 * j + 2, 0)
            round_(B - 1, 1)
            round_(B, 0)

        def parts(i):
            if not isinstance(i, int):
                return True, True, True
            return 0 <= i < B, i + 1 < B, i > 0

        with nc.Block() as block:
            @block.sync
            def _(sp):
                for i in range(B):
                    if i >= 2:
                        sp.wait_ge(split_done, i - 1)
                    sp.dma_start(ctx_t[i % 2][:, :, :], d["ctx_t"][i].rearrange("(c p) n -> p c n", p=128)).then_inc(ctx_loaded[i % 2], 16)
                if layer == 1:
                    core.load_lora_weights(sp, d)

            @block.gpsimd
            def _(pool):
                chain = Chain(pool, split_chain, 2)

                def split(i, p):
                    chain.start(i)
                    pool.wait_ge(ctx_loaded[p], 8 * i + 16 - 8 * p)
                    wait_past(pool, split_done, i)
                    for b in range(2):
                        wait_past(pool, chunk_ready[b], before(i - 2))
                    pool.tensor_copy(ctx_high[p][:, :], ctx_t[p][:, 0, :])
                    pool.tensor_copy(rest_high[:, :], ctx_t[p][:, 1, :])
                    chain.link(pool.tensor_copy(ctx_rest[p][0:CB, :], ctx_t[p][0:CB, 1, :]))
                    chain.link(pool.tensor_tensor(ctx_low[p][:, :], ctx_t[p][:, 0, :], ctx_high[p][:, :].bitcast(F32), ALU.subtract))
                    pool.tensor_tensor(ctx_rest[p][CB:128, :], ctx_t[p][CB:128, 1, :], rest_high[CB:128, :].bitcast(F32),
                                       ALU.subtract).then_inc(split_done, 1)

                for i in range(B):
                    split(i, i % 2)

            @block.tensor
            def _(pe):
                ident = core.c(128, C_ID, 128)
                context = lambda q, cols: dict(high=ctx_high[q][:, cols], low=ctx_low[q][:, cols], rest=ctx_rest[q][:, cols],
                                               last=ctx_rest[q][0:CB, cols])
                weights = lambda n, cols: dict(high=w_high[n][:, cols], low=w_low[n][:, cols], rest=w_rest[n][:, cols],
                                               last=w_rest_low[n][:, cols])

                def scores(i, g, p):
                    rows = slice(g % PER * DH, (g % PER + 1) * DH)
                    pe.matmul(bank[2 + g % 2][0:T, 0:S], qt[p][rows, g // PER, :], kt[p][rows, g // PER, :],
                              start=True, stop=True).then_inc(s_ready, 1)

                def weigh(i, g, p):
                    pe.wait_ge(pt_copied, i * G + g + 1)
                    if g == 0:
                        wait_past(pe, o_ready, i)
                    at = g % (G // 2) * DH
                    accumulate(pe, bank[6 + g // (G // 2)][0:T, at:at + DH], [
                        (prob_t[g % 2][:, k, :], v[p][:, k, g * DH:(g + 1) * DH]) for k in range(ST)]).then_inc(pv_done, 1)

                def chunk(i, p, n, kind, a):
                    b, q = n % 2, 1 - p
                    heads = parts(i)[0]
                    out = bank[b]
                    wait_past(pe, chunk_used[b], before(i) + n // 2)
                    if kind == "q":
                        for m in range(4):
                            last = accumulate(pe, out[:, m * T:(m + 1) * T], [
                                (core.wq[:, c, (4 * a + m) * 128:(4 * a + m + 1) * 128], core.xt[:, c, bass.ts(i + 1, T)])
                                for c in range(KD)])
                    elif kind == "k":
                        if a == 0:
                            pe.wait_ge(split_done, i + 2)
                            if not heads:
                                pe.wait_ge(w_split, 1)
                        last = accumulate(pe, out[:, 0:SE], exact_products(
                            weights("k", slice(a * 128, (a + 1) * 128)), context(q, slice(0, SE))))
                    elif kind == "v":
                        if a == 0 and not heads:
                            pe.wait_ge(w_split, 2)
                        last = accumulate(pe, out[0:SP_, :], exact_products(
                            context(q, slice(a // 2 * SP_, (a // 2 + 1) * SP_)), weights("v", slice(a % 2 * 512, (a % 2 + 1) * 512))))
                    elif kind in (OT_A, OT_B):
                        pe.wait_ge(o_ready, i)
                        for m in range(4):
                            mm = m + 4 * (kind == OT_B)
                            last = pe.transpose(out[:, m * T:(m + 1) * T], o[:, mm * 128:(mm + 1) * 128], ident[0:T, 0:T])
                    elif kind == OUT:
                        for half in range(2):
                            pe.wait_ge(chunk_used[half], before(i) + TAILS[3][half][0 if parts(i)[1] else 1] // 2 + 1)
                        last = accumulate(pe, out[0:T, 0:D], [(ot[:, m, :], core.wo[:, m, :]) for m in range(M)]
                                          + [(core.c(1, C_ONE, T), core.bo[:, :])])
                    else:
                        pe.wait_ge(normed_ready, i)
                        for c in range(KD):
                            last = pe.transpose(out[:, c * T:(c + 1) * T], normed[:, c * 128:(c + 1) * 128], ident[0:T, 0:T])
                    last.then_inc(chunk_ready[b], 1)

                def round_(i, p):
                    heads, front, tail = parts(i)
                    if heads:
                        for b in range(2):
                            pe.wait_ge(chunk_used[b], before(i))
                        scores(i, 0, p)
                        scores(i, 1, p)
                    for g, chunks in enumerate(order(front, tail)):
                        for n, kind, a in chunks:
                            chunk(i, p, n, kind, a)
                        if not heads:
                            continue
                        pe.wait_ge(p_ready, i * G + g + 1)
                        wait_past(pe, pt_copied, i * G + g - 1)
                        for k in range(ST):
                            last = pe.transpose(bank[4 + g % 2][0:SP_, k * T:(k + 1) * T], prob[g % 2][:, k * SP_:(k + 1) * SP_],
                                                ident[0:T, 0:T])
                        last.then_inc(pt_ready, 1)
                        if g + 2 < G:
                            scores(i, g + 2, p)
                        if g > 0:
                            weigh(i, g - 1, p)
                    if heads:
                        weigh(i, G - 1, p)

                pe.wait_ge(core.xw_loaded, 80 * (layer + 1))
                rounds(pe, round_)

            def empty(eng, i, p, n, kind, a, copy):
                b, q = n % 2, 1 - p
                src = bank[b]
                eng.wait_ge(chunk_ready[b], before(i) + n // 2 + 1)
                if kind == "q":
                    return copy(qt[q][:, 4 * a:4 * a + 4, :], src[:, 0:4 * T].rearrange("d (m t) -> d m t", m=4), SCALE)
                if kind == "k":
                    return copy(kt[q][:, a, :], src[:, 0:S], None)
                if kind == "v":
                    return copy(v[q][:, a // 2, a % 2 * 512:(a % 2 + 1) * 512], src[0:SP_, :], None)
                if kind in (OT_A, OT_B):
                    half = 4 * (kind == OT_B)
                    return copy(ot[:, half:half + 4, :], src[:, 0:4 * T].rearrange("d (m t) -> d m t", m=4), None)
                assert kind == NT
                return copy(core.xt[:, :, bass.ts(i - 1, T)], src[:, 0:2 * T].rearrange("d (c t) -> d c t", c=KD), None)

            @block.vector
            def _(dve):
                chain = Chain(dve, dve_chain, 6)

                def copy(out, in_, scale):
                    if scale is None:
                        return dve.tensor_copy(out, in_)
                    return dve.tensor_scalar(out, in_, scale, None, ALU.mult)

                def row_max(i, g):
                    dve.wait_ge(s_ready, i * G + g + 1)
                    dve.tensor_reduce(negmax[:, g:g + 1], bank[2 + g % 2][0:T, 0:S], AX_X, ALU.max, negate=True).then_inc(max_ready, 1)

                def round_(i, p):
                    heads, front, tail = parts(i)
                    if heads:
                        row_max(i, 0)
                    if tail:
                        chain.start(i - 1)
                        dve.wait_ge(p_ready, i * G)
                        chain.link(dve.reciprocal(inv[:, :], total[:, :]))
                        dve.wait_ge(pv_done, i * G)
                        for half in range(2):
                            w = slice(half * G // 2, (half + 1) * G // 2)
                            last = dve.tensor_tensor(o[:, half * 512:(half + 1) * 512].rearrange("t (h e) -> t h e", e=DH),
                                                     bank[6 + half][0:T, :].rearrange("t (h e) -> t h e", e=DH),
                                                     inv[:, w].unsqueeze(2).broadcast_to([T, G // 2, DH]), ALU.mult)
                        last.then_inc(o_ready, 1)
                    for g, chunks in enumerate(order(front, tail)):
                        if heads and g + 1 < G:
                            row_max(i, g + 1)
                        for n, kind, a in chunks:
                            if n % 2 == 0:
                                continue
                            if kind != OUT:
                                empty(dve, i, p, n, kind, a, copy).then_inc(chunk_used[1], 1)
                                continue
                            dve.wait_ge(chunk_ready[1], before(i) + n // 2 + 1)
                            dve.tensor_tensor(res[:, :], bank[1][0:T, 0:D], core.x[:, i - 1, :], ALU.add).then_inc(chunk_used[1], 1)
                            dve.wait_ge(chunk_used[1], before(i) + n // 2 + 1)
                            chain.link(dve.bn_stats(stats[:, :], res[:, :]))
                            dve.memset(pad[:, :], 0.0)
                            chain.link(dve.bn_aggr(mv[:, :], stats[:, :]))
                            chain.link(dve.tensor_scalar(mv[:, 1:2], mv[:, 1:2], EPS, None, ALU.add))
                            dve.sem_inc(var_ready, 1)
                        if tail and g == RSTD:
                            dve.wait_ge(rstd_ready, i)
                            chain.link(dve.tensor_scalar(normed[:, :], res[:, :], mv[:, 0:1], rstd[:, :], ALU.subtract, ALU.mult))
                            dve.sem_inc(normed_ready, 1)
                            chain.link(dve.tensor_copy(core.x[:, i - 1, :], normed[:, :]))
                        if heads:
                            dve.wait_ge(pt_ready, i * G + g + 1)
                            wait_past(dve, pv_done, i * G + g - 1)
                            dve.tensor_copy(prob_t[g % 2][:, :, :], bank[4 + g % 2][0:SP_, 0:ST * T]
                                            .rearrange("s (k t) -> s k t", k=ST)).then_inc(pt_copied, 1)

                for n, (name, w) in enumerate((("k", core.wk), ("v", core.wv))):
                    dve.wait_ge(w_rounded, n + 1)
                    dve.tensor_tensor(w_low[name][:, :], w[:, 0, :], w_high[name][:, :].bitcast(F32), ALU.subtract)
                    dve.tensor_tensor(w_rest_low[name][:, :], w[0:CB, 1, :], w_rest[name][0:CB, :].bitcast(F32),
                                      ALU.subtract).then_inc(w_split, 1)
                rounds(dve, round_)

            @block.scalar
            def _(act):
                chain = Chain(act, act_chain, 1)

                def copy(out, in_, scale):
                    if scale is None:
                        return act.copy(out, in_)
                    return act.activation(out, in_, ACT.Copy, scale=scale)

                def round_(i, p):
                    heads, front, tail = parts(i)
                    for g, chunks in enumerate(order(front, tail)):
                        if heads:
                            act.wait_ge(max_ready, i * G + g + 1)
                            wait_past(act, pt_ready, i * G + g - 1)
                            if g == 0:
                                wait_past(act, o_ready, i)
                            act.activation(prob[g % 2][:, :], bank[2 + g % 2][0:T, 0:S], ACT.Exp, bias=negmax[:, g:g + 1],
                                           accum_out=total[:, g:g + 1]).then_inc(p_ready, 1)
                        if tail and g == RSTD:
                            chain.start(i - 1)
                            act.wait_ge(var_ready, i)
                            chain.link(act.activation(rstd[:, :], mv[:, 1:2], ACT.Ln))
                            act.activation(rstd[:, :], rstd[:, :], ACT.Exp, scale=-0.5).then_inc(rstd_ready, 1)
                        for n, kind, a in chunks:
                            if n % 2 == 0:
                                empty(act, i, p, n, kind, a, copy).then_inc(chunk_used[0], 1)

                act.preload_act_table_set(EXP_LN)
                act.wait_ge(core.xw_loaded, 80 * (layer + 1))
                for name, w in (("k", core.wk), ("v", core.wv)):
                    act.copy(w_high[name][:, :], w[:, 0, :])
                    act.copy(w_rest[name][:, :], w[:, 1, :]).then_inc(w_rounded, 1)
                rounds(act, round_)


def norm_statistics(dve, chain, core, mv, stats, pad, ready):
    for i in range(B):
        dve.bn_stats(stats[:, i, :], core.x[:, i, :])
    chain.link(dve.memset(pad[:, :], 0.0))
    for i in range(B):
        dve.bn_aggr(mv[:, i, :], stats[:, i, :])
    chain.link(dve.memset(pad[:, :], 0.0))
    dve.tensor_scalar(mv[:, :, 1:2], mv[:, :, 1:2], EPS, None, ALU.add).then_inc(ready, 1)


def mixture(core, d):
    nc = core.nc
    bank = core.bank
    HALF = N // 2
    HI = B // 2
    with ExitStack() as ctx:
        sb = lambda name, shape: ctx.enter_context(nc.sbuf_tensor("moe_" + name, shape, F32))
        sbr = lambda name, shape: ctx.enter_context(nc.sbuf_tensor("moe_" + name, shape, F32R))
        pair = lambda name, shape: [sb(f"{name}{p}", shape) for p in range(2)]
        pair_r = lambda name, shape: [sbr(f"{name}{p}", shape) for p in range(2)]
        wg = sb("wg", [128, KD, E0])
        w1, w2 = pair("w1", [128, KD, F0]), pair("w2", [128, FM, D])
        xt_high, xt_low = sbr("xt_high", [128, KD, N]), sbr("xt_low", [128, KD, N])
        w1_high, w1_low = pair_r("w1_high", [128, KD, F0]), pair_r("w1_low", [128, KD, F0])
        w2_high, w2_low = pair_r("w2_high", [128, FM, D]), pair_r("w2_low", [128, FM, D])
        h_high, h_low = pair_r("h_high", [128, FM, HALF]), pair_r("h_low", [128, FM, HALF])
        r, sq = pair("r", [128, HALF]), pair("sq", [128, HALF])
        gates = {n: sb(n, [T, B, E0]) for n in ("shifted", "e", "prob", "eq", "first", "rest", "second", "both", "kept", "weight")}
        per = {n: sb(n, [T, B]) for n in ("max", "sum", "inv", "best", "pick", "sum2", "inv2")}
        stats, mv, rstd, pad = sb("stats", [T, B, 6]), sb("mv", [T, B, 2]), sb("rstd", [T, B, 1]), sb("pad", [T, 1])
        sem = lambda name: core.sem("moe_" + name)
        wg_loaded, w_loaded = sem("wg_loaded"), [sem("w_loaded0"), sem("w_loaded1")]
        logits_ready, shifted_ready, e_ready = sem("logits_ready"), sem("shifted_ready"), sem("e_ready")
        h_ready, h_used, sq_done = sem("h_ready"), sem("h_used"), sem("sq_done")
        y_ready, y_used = sem("y_ready"), sem("y_used")
        high_done, low_done, w_rounded, w_split = sem("high_done"), sem("low_done"), sem("w_rounded"), sem("w_split")
        xt_rounded, xt_split = sem("xt_rounded"), sem("xt_split")
        var_ready, rstd_ready, normed_ready, nt_ready = sem("var_ready"), sem("rstd_ready"), sem("normed_ready"), sem("nt_ready")
        dve_chain, act_chain = sem("dve"), sem("act")

        def rounds(eng, round_):
            round_(0, 0)
            with eng.Fori(0, E0 // 2 - 1) as j:
                round_(2 * j + 1, 1)
                round_(2 * j + 2, 0)
            round_(E0 - 1, 1)
            round_(E0, 0)

        def parts(e):
            return (True, True) if not isinstance(e, int) else (e < E0, e > 0)

        more = lambda e: not isinstance(e, int) or e + 1 < E0

        with nc.Block() as block:
            @block.sync
            def _(sp):
                sp.dma_start(wg[:, :, :], d["L0_ffn_Wg"].rearrange("(c p) n -> p c n", p=128)).then_inc(wg_loaded, 16)

                def load(e, p):
                    wait_past(sp, w_split, e - 1)
                    sp.dma_start(w1[p][:, :, :], d["L0_ffn_W1"][e].rearrange("(c p) n -> p c n", p=128)).then_inc(w_loaded[p], 16)
                    sp.dma_start(w2[p][:, :, :], d["L0_ffn_W2"][e].rearrange("(m p) n -> p m n", p=128)).then_inc(w_loaded[p], 16)

                load(0, 0)
                load(1, 1)
                core.load_cross_weights(sp, d, 1)
                core.load_latent_weights(sp, d)
                for e in range(2, E0):
                    load(e, e % 2)

            @block.tensor
            def _(pe):
                def hidden(e, p, half):
                    for m in range(FM):
                        c = 2 * FM * e + FM * half + m
                        wait_past(pe, h_used, c - FM + 1)
                        rows, cols = slice(m * 128, (m + 1) * 128), slice(half * HALF, (half + 1) * HALF)
                        accumulate(pe, bank[m][:, 0:HALF], [
                            pair for k in range(KD) for pair in split_products(
                                w1_high[p][:, k, rows], w1_low[p][:, k, rows], xt_high[:, k, cols], xt_low[:, k, cols])]
                        ).then_inc(h_ready, 1)

                def outputs(e, p, half):
                    pe.wait_ge(low_done, 2 * FM * e + FM * (half + 1))
                    for b in range(HI // 2):
                        pe.wait_ge(y_used, HI * e + HI // 2 * half + b + 1)
                        for u in range(2):
                            i = 2 * b + u
                            last = accumulate(pe, bank[4 + 2 * half + b][0:T, u * D:(u + 1) * D], [
                                pair for m in range(FM) for pair in split_products(
                                    h_high[half][:, m, i * T:(i + 1) * T], h_low[half][:, m, i * T:(i + 1) * T],
                                    w2_high[p][:, m, :], w2_low[p][:, m, :])])
                        last.then_inc(y_ready, 1)

                def round_(e, p):
                    own, before = parts(e)
                    if own:
                        pe.wait_ge(w_split, e + 1)
                        hidden(e, p, 0)
                    if before:
                        outputs(e - 1, 1 - p, 1)
                    if own:
                        hidden(e, p, 1)
                        outputs(e, p, 0)

                pe.wait_ge(wg_loaded, 16)
                for i in range(B):
                    last = accumulate(pe, bank[7][0:T, i * E0:(i + 1) * E0], [
                        (core.xt[:, c, i * T:(i + 1) * T], wg[:, c, :]) for c in range(KD)])
                last.then_inc(logits_ready, 1)
                pe.wait_ge(xt_split, 1)
                rounds(pe, round_)
                ident = core.c(128, C_ID, 128)
                pe.wait_ge(normed_ready, 1)
                for b in range(B // 2):
                    for u in range(2):
                        for c in range(KD):
                            at = (u * KD + c) * T
                            last = pe.transpose(bank[b][:, at:at + T], core.x[:, 2 * b + u, c * 128:(c + 1) * 128], ident[0:T, 0:T])
                    last.then_inc(nt_ready, 1)

            @block.vector
            def _(dve):
                chain = Chain(dve, dve_chain, 22)
                chain.start(0)
                link = chain.link
                g = {n: t[:, :, :] for n, t in gates.items()}
                s = {n: t[:, :] for n, t in per.items()}
                wide = lambda n: per[n][:, :].unsqueeze(2).broadcast_to([T, B, E0])
                logits = bank[7][0:T, 0:B * E0].rearrange("t (b e) -> t b e", b=B)
                prio = core.c(T, C_PRIO, E0).unsqueeze(1).broadcast_to([T, B, E0])
                tt = dve.tensor_tensor
                dve.wait_ge(xt_rounded, 1)
                dve.tensor_tensor(xt_low[:, :, :], core.xt[:, :, :], xt_high[:, :, :].bitcast(F32), ALU.subtract).then_inc(xt_split, 1)
                dve.wait_ge(w_rounded, 1)
                dve.tensor_tensor(w1_low[0][:, :, :], w1[0][:, :, :], w1_high[0][:, :, :].bitcast(F32), ALU.subtract)
                dve.tensor_tensor(w2_low[0][:, :, :], w2[0][:, :, :], w2_high[0][:, :, :].bitcast(F32), ALU.subtract).then_inc(w_split, 1)
                dve.wait_ge(logits_ready, 1)
                link(dve.tensor_reduce(s["max"], logits, AX_X, ALU.max))
                tt(g["shifted"], logits, wide("max"), ALU.subtract).then_inc(shifted_ready, 1)
                dve.wait_ge(e_ready, 1)
                link(dve.tensor_reduce(s["sum"], g["e"], AX_X, ALU.add))
                link(dve.reciprocal(s["inv"], s["sum"]))
                link(tt(g["prob"], g["e"], wide("inv"), ALU.mult))

                def pick(src, out):
                    link(dve.tensor_reduce(s["best"], g[src], AX_X, ALU.max))
                    link(tt(g["eq"], g[src], wide("best"), ALU.is_equal))
                    link(tt(g["eq"], g["eq"], prio, ALU.mult))
                    link(dve.tensor_reduce(s["pick"], g["eq"], AX_X, ALU.max))
                    link(tt(g[out], g["eq"], wide("pick"), ALU.is_equal))

                pick("prob", "first")
                link(dve.scalar_tensor_tensor(g["rest"], g["first"], -2.0, g["prob"], ALU.mult, ALU.add))
                pick("rest", "second")
                link(tt(g["both"], g["first"], g["second"], ALU.add))
                link(tt(g["kept"], g["prob"], g["both"], ALU.mult))
                link(dve.tensor_reduce(s["sum2"], g["kept"], AX_X, ALU.add))
                link(dve.tensor_scalar(s["sum2"], s["sum2"], 1e-8, None, ALU.add))
                link(dve.reciprocal(s["inv2"], s["sum2"]))
                link(tt(g["weight"], g["kept"], wide("inv2"), ALU.mult))

                def add(e, half):
                    for b in range(HI // 2):
                        n = HI * e + HI // 2 * half + b
                        dve.wait_ge(y_ready, n + 1)
                        dve.wait_ge(y_used, n + 1)
                        for u in range(2):
                            i = HI * half + 2 * b + u
                            last = dve.scalar_tensor_tensor(core.x[:, i, :], bank[4 + 2 * half + b][0:T, u * D:(u + 1) * D],
                                                            gates["weight"][:, i, bass.ds(e, 1)], core.x[:, i, :], ALU.mult, ALU.add)
                        last.then_inc(y_used, 1)

                def low(e, half):
                    for m in range(FM):
                        c = 2 * FM * e + FM * half + m
                        dve.wait_ge(sq_done, c + 1)
                        dve.wait_ge(high_done, c + 1)
                        dve.tensor_tensor(h_low[half][:, m, :], sq[m % 2][:, :], h_high[half][:, m, :].bitcast(F32),
                                          ALU.subtract).then_inc(low_done, 1)

                def split_low(e, p):
                    dve.wait_ge(w_rounded, e + 1)
                    dve.tensor_tensor(w1_low[p][:, :, :], w1[p][:, :, :], w1_high[p][:, :, :].bitcast(F32), ALU.subtract)
                    dve.tensor_tensor(w2_low[p][:, :, :], w2[p][:, :, :], w2_high[p][:, :, :].bitcast(F32),
                                      ALU.subtract).then_inc(w_split, 1)

                def round_(e, p):
                    own, before = parts(e)
                    if own:
                        low(e, 0)
                    if before:
                        add(e - 1, 1)
                    if own:
                        low(e, 1)
                        if more(e):
                            split_low(e + 1, 1 - p)
                        add(e, 0)

                dve.sem_inc(y_used, HI)
                rounds(dve, round_)
                dve.wait_ge(y_used, HI * (E0 + 1))
                norm_statistics(dve, chain, core, mv, stats, pad, var_ready)
                dve.wait_ge(rstd_ready, 1)
                for i in range(B):
                    last = dve.tensor_scalar(core.x[:, i, :], core.x[:, i, :], mv[:, i, 0:1], rstd[:, i, :], ALU.subtract, ALU.mult)
                last.then_inc(normed_ready, 1)
                for b in range(1, B // 2, 2):
                    dve.wait_ge(nt_ready, b + 1)
                    dve.tensor_copy(core.xt[:, :, 2 * b * T:2 * (b + 1) * T].rearrange("d c (u t) -> d u c t", u=2),
                                    bank[b][:, 0:4 * T].rearrange("d (u c t) -> d u c t", u=2, c=KD))

            @block.gpsimd
            def _(pool):
                def square(e, half):
                    for m in range(FM):
                        c = 2 * FM * e + FM * half + m
                        pool.wait_ge(h_used, c + 1)
                        wait_past(pool, low_done, c - 1)
                        pool.tensor_tensor(sq[m % 2][:, :], r[m % 2][:, :], r[m % 2][:, :], ALU.mult).then_inc(sq_done, 1)

                def round_(e, p):
                    if parts(e)[0]:
                        square(e, 0)
                        square(e, 1)

                rounds(pool, round_)

            @block.scalar
            def _(act):
                chain = Chain(act, act_chain, 1)
                chain.start(0)
                act.preload_act_table_set(EXP_LN)
                act.copy(xt_high[:, :, :], core.xt[:, :, :]).then_inc(xt_rounded, 1)
                act.wait_ge(w_loaded[0], 32)
                act.copy(w1_high[0][:, :, :], w1[0][:, :, :])
                act.copy(w2_high[0][:, :, :], w2[0][:, :, :]).then_inc(w_rounded, 1)
                act.wait_ge(shifted_ready, 1)
                act.activation(gates["e"][:, :, :], gates["shifted"][:, :, :], ACT.Exp).then_inc(e_ready, 1)

                def high(e, half, m):
                    c = 2 * FM * e + FM * half + m
                    act.wait_ge(h_used, c + 1)
                    act.activation(h_high[half][:, m, :], r[m % 2][:, :], ACT.Square).then_inc(high_done, 1)

                def relu(e, half):
                    for m in range(FM):
                        c = 2 * FM * e + FM * half + m
                        act.wait_ge(h_ready, c + 1)
                        wait_past(act, sq_done, c - 1)
                        wait_past(act, high_done, c - 1)
                        act.activation(r[m % 2][:, :], bank[m][:, 0:HALF], ACT.Relu).then_inc(h_used, 1)
                        if m == 0:
                            wait_past(act, y_ready, HI * (e - 1) + HI // 2 * (half + 1))
                        else:
                            high(e, half, m - 1)
                    high(e, half, FM - 1)

                def round_high(e, p):
                    act.wait_ge(w_loaded[p], 16 * e + 32 - 16 * p)
                    wait_past(act, y_ready, HI * (e - 1))
                    act.copy(w1_high[p][:, :, :], w1[p][:, :, :])
                    act.copy(w2_high[p][:, :, :], w2[p][:, :, :]).then_inc(w_rounded, 1)

                def round_(e, p):
                    if parts(e)[0]:
                        relu(e, 0)
                        relu(e, 1)
                        if more(e):
                            round_high(e + 1, 1 - p)

                rounds(act, round_)
                act.wait_ge(var_ready, 1)
                chain.link(act.activation(rstd[:, :, :], mv[:, :, 1:2], ACT.Ln))
                act.activation(rstd[:, :, :], rstd[:, :, :], ACT.Exp, scale=-0.5).then_inc(rstd_ready, 1)
                for b in range(0, B // 2, 2):
                    act.wait_ge(nt_ready, b + 1)
                    act.copy(core.xt[:, :, 2 * b * T:2 * (b + 1) * T].rearrange("d c (u t) -> d u c t", u=2),
                             bank[b][:, 0:4 * T].rearrange("d (u c t) -> d u c t", u=2, c=KD))


def low_rank_experts(core, d, out):
    nc = core.nc
    bank = core.bank
    W = W_LORA
    with ExitStack() as ctx:
        sb = lambda name, shape, dt=F32: ctx.enter_context(nc.sbuf_tensor("lora_" + name, shape, dt))
        w, bias, lora_b = core.lora_w, core.lora_bias, core.lora_b
        small = sb("small", [T, B, E1 + RK])
        shifted, e, gate = sb("shifted", [T, B, E1]), sb("e", [T, B, E1]), sb("gate", [T, B, E1], BF16)
        mid2 = sb("mid2", [T, B, RK])
        top, total, inv = sb("top", [T, B]), sb("total", [T, B]), sb("inv", [T, B])
        gm, gm_t = sb("gm", [T, B, E1, RK]), sb("gm_t", [E1 * RK, B, T])
        stats, mv, rstd, pad = sb("stats", [T, B, 6]), sb("mv", [T, B, 2]), sb("rstd", [T, B, 1]), sb("pad", [T, 1])
        sem = lambda name: core.sem("lora_" + name)
        loaded, base_ready, shifted_ready, e_ready, gm_ready = (
            core.lora_loaded, sem("base_ready"), sem("shifted_ready"), sem("e_ready"), sem("gm_ready"))
        base_used, gmt_ready, gmt_copied, low_ready = sem("base_used"), sem("gmt_ready"), sem("gmt_copied"), sem("low_ready")
        var_ready, rstd_ready, out_ready, stored = sem("var_ready"), sem("rstd_ready"), sem("out_ready"), sem("stored")
        dve_chain, act_chain = sem("dve"), sem("act")

        with nc.Block() as block:
            @block.sync
            def _(sp):
                for i in range(B):
                    sp.wait_ge(out_ready, i + 1)
                    sp.dma_start(out[i], core.x[:, i, :]).then_inc(stored, 16)
                sp.wait_ge(stored, 16 * B)

            @block.tensor
            def _(pe):
                ident = core.c(128, C_ID, 128)
                pe.wait_ge(loaded, 80)
                for i in range(B):
                    accumulate(pe, bank[i][0:T, 0:W], [(core.xt[:, c, i * T:(i + 1) * T], w[:, c, :]) for c in range(KD)]
                               + [(core.c(1, C_ONE, T), bias[:, :])]).then_inc(base_ready, 1)
                pe.wait_ge(gm_ready, 1)
                pe.wait_ge(base_used, B)
                for i in range(B):
                    last = pe.transpose(bank[i // 4][0:E1 * RK, i % 4 * T:(i % 4 + 1) * T],
                                        gm[:, i, :, :].rearrange("t e r -> t (e r)"), ident[0:T, 0:T])
                    if i % 4 == 3:
                        last.then_inc(gmt_ready, 1)
                for i in range(B):
                    if i % 4 == 0:
                        pe.wait_ge(gmt_copied, i // 4 + 1)
                    last = pe.matmul(bank[2 + i // 2][0:T, i % 2 * D:(i % 2 + 1) * D], gm_t[:, i, :], lora_b[:, :],
                                     start=True, stop=True)
                    if i % 2 == 1:
                        last.then_inc(low_ready, 1)

            @block.vector
            def _(dve):
                chain = Chain(dve, dve_chain, 9)
                chain.start(0)
                wide = lambda t: t[:, :].unsqueeze(2).broadcast_to([T, B, E1])
                logits = small[:, :, 0:E1]
                for i in range(B):
                    dve.wait_ge(base_ready, i + 1)
                    last = dve.tensor_copy(small[:, i, :], bank[i][0:T, D:W])
                chain.link(last)
                chain.link(dve.tensor_reduce(top[:, :], logits, AX_X, ALU.max))
                dve.tensor_tensor(shifted[:, :, :], logits, wide(top), ALU.subtract).then_inc(shifted_ready, 1)
                chain.link(dve.tensor_scalar(mid2[:, :, :], small[:, :, E1:E1 + RK], 2.0, None, ALU.mult))
                for i in range(B):
                    dve.tensor_tensor(core.x[:, i, :], bank[i][0:T, 0:D], core.x[:, i, :], ALU.add).then_inc(base_used, 1)
                dve.wait_ge(e_ready, 1)
                chain.link(dve.tensor_reduce(total[:, :], e[:, :, :], AX_X, ALU.add))
                chain.link(dve.reciprocal(inv[:, :], total[:, :]))
                chain.link(dve.tensor_tensor(gate[:, :, :], e[:, :, :], wide(inv), ALU.mult))
                shape = [T, B, E1, RK]
                dve.tensor_tensor(gm[:, :, :, :], gate[:, :, :].unsqueeze(3).broadcast_to(shape),
                                  mid2[:, :, :].unsqueeze(2).broadcast_to(shape), ALU.mult).then_inc(gm_ready, 1)
                for k in range(2):
                    dve.wait_ge(gmt_ready, k + 1)
                    dve.tensor_copy(gm_t[:, 4 * k:4 * k + 4, :], bank[k][0:E1 * RK, 0:4 * T].rearrange("r (i t) -> r i t", i=4)
                                    ).then_inc(gmt_copied, 1)
                for b in range(B // 2):
                    dve.wait_ge(low_ready, b + 1)
                    last = dve.tensor_tensor(core.x[:, 2 * b:2 * b + 2, :], bank[2 + b][0:T, :].rearrange("t (u n) -> t u n", u=2),
                                             core.x[:, 2 * b:2 * b + 2, :], ALU.add)
                chain.link(last)
                norm_statistics(dve, chain, core, mv, stats, pad, var_ready)
                dve.wait_ge(rstd_ready, 1)
                for i in range(B):
                    dve.tensor_scalar(core.x[:, i, :], core.x[:, i, :], mv[:, i, 0:1], rstd[:, i, :], ALU.subtract,
                                      ALU.mult).then_inc(out_ready, 1)

            @block.scalar
            def _(act):
                chain = Chain(act, act_chain, 1)
                chain.start(0)
                act.preload_act_table_set(EXP_LN)
                act.wait_ge(shifted_ready, 1)
                act.activation(e[:, :, :], shifted[:, :, :], ACT.Exp).then_inc(e_ready, 1)
                act.wait_ge(var_ready, 1)
                chain.link(act.activation(rstd[:, :, :], mv[:, :, 1:2], ACT.Ln))
                act.activation(rstd[:, :, :], rstd[:, :, :], ACT.Exp, scale=-0.5).then_inc(rstd_ready, 1)


def latent_attention(core, d):
    nc = core.nc
    bank = core.bank
    HALF, HI = N // 2, B // 2
    AUG = HD1 + 1
    GB = 4
    NG = H1 // GB
    with ExitStack() as whole:
        sbw = lambda name, shape: whole.enter_context(nc.sbuf_tensor("la_" + name, shape, F32))
        lat = sbw("lat", [128, N])
        qg, kg = sbw("qg", [128, KD, N]), sbw("kg", [128, KD, N])
        wv, wo, rows = core.la_wv, core.la_wo, core.la_rows
        sem = lambda name: core.sem("la_" + name)
        wo_loaded = core.wo_loaded

        with ExitStack() as ctx:
            sb = lambda name, shape: ctx.enter_context(nc.sbuf_tensor("la_" + name, shape, F32))
            w_lat, w_cont, bias, w_rope = core.w_lat, core.w_cont, core.la_bias, core.w_rope
            t1 = [sb(f"t1{k}", [128, HI, T]) for k in range(2)]
            t2 = [sb(f"t2{k}", [128, HI, T]) for k in range(2)]
            t3 = [sb(f"t3{k}", [128, HI, T]) for k in range(2)]
            w_loaded, lat_ready, lat_done = core.la_loaded, sem("lat_ready"), sem("lat_done")
            cont_ready, cont_used = sem("cont_ready"), sem("cont_used")
            rope_ready, rope_used, turned_ready, gelu_done = sem("rope_ready"), sem("rope_used"), sem("turned_ready"), sem("gelu_done")
            dve_chain = sem("dve_rope")
            B_LAT, B_QC, B_KC, B_QR, B_QT, B_KR, B_KT = range(7)

            with nc.Block() as block:
                @block.tensor
                def _(pe):
                    pe.wait_ge(w_loaded, 16 * 9)
                    for s in range(2):
                        cols = slice(s * HALF, (s + 1) * HALF)
                        x = [core.xt[:, c, cols] for c in range(KD)]
                        wait_past(pe, lat_done, s)
                        accumulate(pe, bank[B_LAT][:, 0:HALF], [(w_lat[:, c, :], x[c]) for c in range(KD)]).then_inc(lat_ready, 1)
                        for n, (name, b) in enumerate((("wqr", B_QR), ("wqr_turned", B_QT), ("wkr", B_KR), ("wkr_turned", B_KT))):
                            if n % 2 == 0:
                                wait_past(pe, rope_used, 2 * (s - 1) + n // 2 + 1 if s else 0)
                            last = accumulate(pe, bank[b][:, 0:HALF], [(w_rope[name][:, c, :], x[c]) for c in range(KD)])
                            if n % 2 == 1:
                                last.then_inc(rope_ready, 1)
                        pe.wait_ge(lat_done, s + 1)
                        wait_past(pe, cont_used, s)
                        pe.matmul(bank[B_KC][:, 0:HALF], w_cont[0:LAT, :], lat[0:LAT, cols], start=True, stop=True)
                        pe.matmul(bank[B_QC][:, 0:HALF], w_cont[LAT:2 * LAT, :], lat[LAT:2 * LAT, cols],
                                  start=True, stop=True).then_inc(cont_ready, 1)

                @block.vector
                def _(dve):
                    chain = Chain(dve, dve_chain, 4)
                    chain.start(0)
                    cos, sin = (core.c(128, k, T).unsqueeze(1).broadcast_to([128, HI, T]) for k in (C_COS, C_SIN))
                    dve.wait_ge(w_loaded, 16 * 9)
                    for s in range(2):
                        for k in range(2):
                            b = B_QR + 2 * k
                            of = lambda n: bank[n][:, 0:HALF].rearrange("d (i t) -> d i t", i=HI)
                            dve.wait_ge(rope_ready, 2 * s + k + 1)
                            dve.scalar_tensor_tensor(t1[k][:, :, :], of(b), bias[:, 3 + 2 * k:4 + 2 * k], cos, ALU.add, ALU.mult)
                            last = dve.scalar_tensor_tensor(t2[k][:, :, :], of(b + 1), bias[:, 4 + 2 * k:5 + 2 * k], sin, ALU.add, ALU.mult)
                            chain.link(last)
                            dve.sem_inc(rope_used, 1)
                            wait_past(dve, gelu_done, 2 * s + k - 1)
                            dve.tensor_tensor(t3[k][:, :, :], t1[k][:, :, :], t2[k][:, :, :], ALU.add).then_inc(turned_ready, 1)

                @block.scalar
                def _(act):
                    act.preload_act_table_set("gelu_and_others")
                    act.wait_ge(w_loaded, 16 * 9)
                    for s in range(2):
                        cols = slice(s * HALF, (s + 1) * HALF)
                        act.wait_ge(lat_ready, s + 1)
                        act.activation(lat[:, cols], bank[B_LAT][:, 0:HALF], ACT.Gelu, bias=bias[:, 0:1]).then_inc(lat_done, 1)
                        act.wait_ge(cont_ready, s + 1)
                        act.activation(qg[:, 0, cols], bank[B_QC][:, 0:HALF], ACT.Gelu, bias=bias[:, 1:2])
                        act.activation(kg[:, 0, cols], bank[B_KC][:, 0:HALF], ACT.Gelu, bias=bias[:, 2:3]).then_inc(cont_used, 1)
                        for k, out in enumerate((qg, kg)):
                            act.wait_ge(turned_ready, 2 * s + k + 1)
                            act.activation(out[:, 1, cols].rearrange("d (i t) -> d i t", i=HI), t3[k][:, :, :], ACT.Gelu).then_inc(gelu_done, 1)

        with ExitStack() as ctx:
            sb = lambda name, shape: ctx.enter_context(nc.sbuf_tensor("la_" + name, shape, F32))
            pair = lambda name, shape: [sb(f"{name}{p}", shape) for p in range(2)]
            q, k_sep, lat_i = pair("q", [128, KD, T]), pair("k_sep", [128, KD, 8, T]), pair("lat_i", [LAT, T])
            v = pair("v", [T, H1, AUG])
            masked = pair("masked", [T, GB, T])
            prob = pair("prob", [T, GB, T])
            prob_t = pair("prob_t", [T, GB, T])
            top = sb("top", [T, H1])
            inv, o, ot = sb("inv", [T, H1, 1]), sb("o", [T, D]), sb("ot", [128, KD, T])
            res, normed = sb("res", [T, D]), sb("normed", [T, D])
            stats, mv, rstd, pad = sb("stats", [T, 6]), sb("mv", [T, 2]), sb("rstd", [T, 1]), sb("pad", [T, 1])
            ones_set, sep_ready, v_ready, v_copied, s_ready = sem("ones_set"), sem("sep_ready"), sem("v_ready"), sem("v_copied"), sem("s_ready")
            s_used, masked_ready, e_done, et_ready, et_copied, o_ready = (
                sem("s_used"), sem("masked_ready"), sem("e_done"), sem("et_ready"), sem("et_copied"), sem("o_ready"))
            on_ready, ot_ready, ot_copied, out_ready = sem("on_ready"), sem("ot_ready"), sem("ot_copied"), sem("out_ready")
            var_ready, rstd_ready, normed_ready, nt_ready, nt_copied = (
                sem("var_ready"), sem("rstd_ready"), sem("normed_ready"), sem("nt_ready"), sem("nt_copied"))
            mask_chain, divide_chain, end_chain, act_chain = sem("dve_mask"), sem("dve_divide"), sem("dve_end"), sem("act")

            with nc.Block() as block:
                @block.gpsimd
                def _(pool):
                    def round_(n, parity, front, middle, end):
                        if not front:
                            return
                        i, p = n + 1, 1 - parity
                        wait_past(pool, s_ready, NG * (i - 1))
                        for c in range(KD):
                            pool.tensor_tensor(k_sep[p][:, c, :, :], kg[:, c, bass.ts(i, T)].unsqueeze(1).broadcast_to([128, 8, T]),
                                               core.c(128, C_HEAD, 8).unsqueeze(2).broadcast_to([128, 8, T]), ALU.mult)
                        wait_past(pool, v_ready, i - 1)
                        pool.tensor_copy(lat_i[p][:, :], lat[0:LAT, bass.ts(i, T)])
                        pool.tensor_copy(q[p][:, :, :], qg[:, :, bass.ts(i, T)]).then_inc(sep_ready, 1)

                    for p in range(2):
                        last = pool.memset(v[p][:, :, HD1:AUG], 1.0)
                    last.then_inc(ones_set, 1)
                    overlapped(pool, round_)

                @block.tensor
                def _(pe):
                    ident = core.c(128, C_ID, 128)

                    def scores(i, p, j):
                        if j == 0:
                            pe.wait_ge(sep_ready, i + 1)
                        wait_past(pe, s_used, NG * (i - 1) + j + 1 if not isinstance(i, int) or i else 0)
                        heads = slice(j % 2 * GB, (j % 2 + 1) * GB)
                        pe.matmul(bank[j][0:T, 0:GB * T], q[p][:, j // 2, :],
                                  k_sep[p][:, j // 2, heads, :].rearrange("d h t -> d (h t)"), start=True, stop=True).then_inc(s_ready, 1)

                    def values(i, p):
                        wait_past(pe, nt_copied, i - 1)
                        pe.matmul(bank[4][0:T, 0:D], lat_i[p][:, :], wv[:, :], start=True, stop=True).then_inc(v_ready, 1)

                    def turn(i, j):
                        pe.wait_ge(e_done, NG * i + j + 1)
                        wait_past(pe, et_copied, NG * i + j - 1)
                        for hh in range(GB):
                            last = pe.transpose(bank[5 + j % 2][0:T, hh * T:(hh + 1) * T], prob[j % 2][:, hh, :], ident[0:T, 0:T])
                        last.then_inc(et_ready, 1)

                    def weigh(i, p, j):
                        pe.wait_ge(et_copied, NG * i + j + 1)
                        if j == 0:
                            pe.wait_ge(v_copied, i + 1)
                            wait_past(pe, on_ready, i)
                        for hh in range(GB):
                            h = GB * j + hh
                            last = pe.matmul(bank[7][0:T, h * AUG:(h + 1) * AUG], prob_t[j % 2][:, hh, :], v[p][:, h, :],
                                             start=True, stop=True)
                        if j == NG - 1:
                            last.then_inc(o_ready, 1)

                    def turn_output(i, alone):
                        pe.wait_ge(on_ready, i + 1)
                        pe.wait_ge(v_copied, i + (1 if alone else 2))
                        wait_past(pe, nt_copied, i)
                        for c in range(KD):
                            last = pe.transpose(bank[4][:, c * T:(c + 1) * T], o[:, c * 128:(c + 1) * 128], ident[0:T, 0:T])
                        last.then_inc(ot_ready, 1)

                    def out_projection(i):
                        pe.wait_ge(ot_copied, i + 1)
                        accumulate(pe, bank[4][0:T, 0:D], [(ot[:, c, :], wo[:, c, :]) for c in range(KD)]).then_inc(out_ready, 1)

                    def turn_state(i):
                        pe.wait_ge(normed_ready, i + 1)
                        for c in range(KD):
                            last = pe.transpose(bank[4][:, c * T:(c + 1) * T], normed[:, c * 128:(c + 1) * 128], ident[0:T, 0:T])
                        last.then_inc(nt_ready, 1)

                    def round_(i, p, front, middle, end):
                        for j in range(NG):
                            if middle:
                                turn(i, j)
                            if end and j == 0:
                                turn_output(i - 1, not middle)
                            if middle and j > 0:
                                weigh(i, p, j - 1)
                            if front and j > 0:
                                scores(i + 1, 1 - p, j - 1)
                            if end and j == 2:
                                out_projection(i - 1)
                        if middle:
                            weigh(i, p, NG - 1)
                        if front:
                            scores(i + 1, 1 - p, NG - 1)
                        if end:
                            turn_state(i - 1)
                        if front:
                            values(i + 1, 1 - p)

                    pe.wait_ge(wo_loaded, 48)
                    overlapped(pe, round_)

                @block.vector
                def _(dve):
                    chain_m, chain_d, chain_e = Chain(dve, mask_chain, 2 * NG), Chain(dve, divide_chain, 1), Chain(dve, end_chain, 5)

                    def add_bias(i, p):
                        dve.wait_ge(v_ready, i + 1)
                        wait_past(dve, o_ready, i - 1)
                        dve.tensor_tensor(v[p][:, :, 0:HD1], bank[4][0:T, 0:D].rearrange("t (h e) -> t h e", h=H1),
                                          rows[:, 0, :].rearrange("t (h e) -> t h e", h=H1), ALU.add).then_inc(v_copied, 1)

                    def mask(i, j):
                        chain_m.resume(i, 2 * j)
                        dve.wait_ge(s_ready, NG * i + j + 1)
                        m = masked[j % 2]
                        t = top[:, GB * j:GB * (j + 1)]
                        wait_past(dve, e_done, NG * i + j - 1)
                        chain_m.link(dve.tensor_tensor(m[:, :, :], bank[j][0:T, 0:GB * T].rearrange("t (h s) -> t h s", h=GB),
                                                       core.c(T, C_CAUSAL, T).unsqueeze(1).broadcast_to([T, GB, T]), ALU.add))
                        dve.sem_inc(s_used, 1)
                        chain_m.link(dve.tensor_reduce(t, m[:, :, :], AX_X, ALU.max))
                        dve.tensor_tensor(m[:, :, :], m[:, :, :], t.unsqueeze(2).broadcast_to([T, GB, T]),
                                          ALU.subtract).then_inc(masked_ready, 1)

                    def divide(i):
                        dve.wait_ge(o_ready, i + 1)
                        av = bank[7][0:T, 0:H1 * AUG].rearrange("t (h e) -> t h e", h=H1)
                        chain_d.start(i)
                        chain_d.link(dve.reciprocal(inv[:, :, :], av[:, :, HD1:AUG]))
                        wait_past(dve, ot_ready, i)
                        dve.tensor_tensor(o[:, :].rearrange("t (h e) -> t h e", h=H1), av[:, :, 0:HD1],
                                          inv[:, :, :].broadcast_to([T, H1, HD1]), ALU.mult).then_inc(on_ready, 1)

                    def residual(i):
                        chain_e.start(i)
                        chain_e.link(dve.tensor_tensor(res[:, :], core.x[:, i, :], rows[:, 1, :], ALU.add))
                        dve.wait_ge(out_ready, i + 1)
                        chain_e.link(dve.tensor_tensor(res[:, :], bank[4][0:T, 0:D], res[:, :], ALU.add))
                        chain_e.link(dve.bn_stats(stats[:, :], res[:, :]))
                        dve.memset(pad[:, :], 0.0)
                        chain_e.link(dve.bn_aggr(mv[:, :], stats[:, :]))
                        dve.tensor_scalar(mv[:, 1:2], mv[:, 1:2], EPS, None, ALU.add).then_inc(var_ready, 1)

                    def normalize(i):
                        dve.wait_ge(rstd_ready, i + 1)
                        chain_e.link(dve.tensor_scalar(normed[:, :], res[:, :], mv[:, 0:1], rstd[:, :], ALU.subtract, ALU.mult))
                        dve.sem_inc(normed_ready, 1)
                        dve.tensor_copy(core.x[:, i, :], normed[:, :])

                    def round_(i, p, front, middle, end):
                        if middle:
                            add_bias(i, p)
                            mask(i, 2)
                            mask(i, 3)
                        if front:
                            mask(i + 1, 0)
                        if end:
                            residual(i - 1)
                        if middle:
                            divide(i)
                        if end:
                            normalize(i - 1)
                        if front:
                            mask(i + 1, 1)

                    dve.wait_ge(ones_set, 1)
                    dve.wait_ge(wo_loaded, 48)
                    overlapped(dve, round_)

                @block.scalar
                def _(act):
                    chain = Chain(act, act_chain, 1)
                    act.preload_act_table_set(EXP_LN)

                    def exps(i, j):
                        act.wait_ge(masked_ready, NG * i + j + 1)
                        wait_past(act, et_ready, NG * i + j - 1)
                        act.activation(prob[j % 2][:, :, :], masked[j % 2][:, :, :], ACT.Exp, scale=HD1 ** -0.5).then_inc(e_done, 1)

                    def copy_turned(i, j):
                        act.wait_ge(et_ready, NG * i + j + 1)
                        act.copy(prob_t[j % 2][:, :, :], bank[5 + j % 2][0:T, 0:GB * T].rearrange("s (h t) -> s h t", h=GB)).then_inc(et_copied, 1)

                    def copy_output(i):
                        act.wait_ge(ot_ready, i + 1)
                        wait_past(act, out_ready, i)
                        act.copy(ot[:, :, :], bank[4][:, 0:KD * T].rearrange("d (c t) -> d c t", c=KD)).then_inc(ot_copied, 1)

                    def deviation(i):
                        chain.start(i)
                        act.wait_ge(var_ready, i + 1)
                        chain.link(act.activation(rstd[:, :], mv[:, 1:2], ACT.Ln))
                        act.activation(rstd[:, :], rstd[:, :], ACT.Exp, scale=-0.5).then_inc(rstd_ready, 1)

                    def copy_state(i):
                        act.wait_ge(nt_ready, i + 1)
                        act.copy(core.xt[:, :, bass.ts(i, T)], bank[4][:, 0:KD * T].rearrange("d (c t) -> d c t", c=KD)).then_inc(nt_copied, 1)

                    def round_(i, p, front, middle, end):
                        for j in range(NG):
                            if middle and j > 0:
                                exps(i, j)
                            if end and j == 0:
                                copy_output(i - 1)
                            if middle and j > 0:
                                copy_turned(i, j - 1)
                        if middle:
                            copy_turned(i, NG - 1)
                        if front:
                            exps(i + 1, 0)
                        if end:
                            deviation(i - 1)
                            copy_state(i - 1)

                    overlapped(act, round_)


def build(nc, d, out):
    with ExitStack() as ctx:
        core = Core(nc, ctx)
        with ExitStack() as layer:
            sb = lambda name, shape: layer.enter_context(nc.sbuf_tensor(name, shape, F32))
            core.w_in = sb("w_in", [128, KD, W_IN])
            core.w_out, core.w_norm = sb("w_out", [128, 4, D]), sb("w_norm", [128, 4])
            core.xt_in = [sb("xt_in0", [128, KD, T]), sb("xt_in1", [128, KD, T])]
            core.item_loaded = [core.sem("ss_item_loaded0"), core.sem("ss_item_loaded1")]
            core.state_loaded = core.sem("ss_state_loaded")
            zs = sb("zs", [T, B, DI])
            dt, dta = sb("dt", [T, B, H0]), sb("dta", [T, B, H0])
            cosine, sine = sb("cosine", [T, B * H0, PAIRS]), sb("sine", [T, B * H0, PAIRS])
            project_time_and_gate(core, d, zs, dt, dta, cosine, sine)
            state_space(core, d, zs, dt, dta, cosine, sine)
        core.free_semaphores()
        cross_attention(core, d, 0)
        mixture(core, d)
        latent_attention(core, d)
        cross_attention(core, d, 1)
        low_rank_experts(core, d, out)


_AS_THEY_ARE = [
    "L0_attn_W_in", "L0_attn_W_out", "L0_xattn_Wq", "L0_xattn_Wk", "L0_xattn_Wv", "L0_xattn_Wo", "L0_ffn_Wg", "L0_ffn_W1",
    "L0_ffn_W2", "L1_attn_wq", "L1_attn_wqc", "L1_attn_wqr", "L1_attn_wkv", "L1_attn_wkr", "L1_attn_wkc", "L1_attn_wv",
    "L1_attn_wo", "L1_xattn_Wq", "L1_xattn_Wk", "L1_xattn_Wv", "L1_xattn_Wo",
]


def _layout(inputs):
    a = {n: np.ascontiguousarray(inputs[n]) for n in inputs}
    row = lambda n: np.broadcast_to(a[n].reshape(1, -1), (T, a[n].size))
    d = {n: a[n] for n in _AS_THEY_ARE}
    d["x"] = a["x"]
    d["xt"] = a["x"].reshape(N, D).T
    d["xt_items"] = a["x"].transpose(0, 2, 1)
    twice = lambda m, axis: np.concatenate([m, np.take(m, np.arange(128, DC), axis=axis)], axis=axis)
    d["ctx_t"] = np.pad(twice(a["ctx_768"].transpose(0, 2, 1), 1), ((0, 0), (0, 0), (0, SE - S)))
    for n in ("L0_xattn_Wk", "L0_xattn_Wv", "L1_xattn_Wk", "L1_xattn_Wv"):
        d[n] = twice(a[n], 0)
    d["const"] = constants()
    d["rows"] = np.concatenate([row("L0_attn_dt_bias"), row("L0_attn_A_log"), row("L0_attn_D_skip")], axis=1)
    d["norm_w"] = a["L0_attn_norm_weight"].reshape(4, 128).T
    d["L0_bo"] = a["L0_xattn_bo"].reshape(1, D)
    d["L1_bo"] = a["L1_xattn_bo"].reshape(1, D)
    turned = lambda n: np.concatenate([a[n][..., R1 // 2:], a[n][..., :R1 // 2]], axis=-1)
    d["wqr_turned"], d["wkr_turned"] = turned("L1_attn_wqr"), turned("L1_attn_wkr")
    d["la_bias"] = np.stack([
        np.concatenate([a["L1_attn_bkv"], a["L1_attn_bq"]]), a["L1_attn_bqc"], a["L1_attn_bkc"],
        a["L1_attn_bqr"], turned("L1_attn_bqr"), a["L1_attn_bkr"], turned("L1_attn_bkr")], axis=1)
    d["la_rows"] = np.stack([row("L1_attn_bv"), row("L1_attn_bo")], axis=1)
    d["base_wt"] = a["L1_ffn_base_w"].T
    d["router_wt"] = a["L1_ffn_router_w"].T
    d["lora_a"] = a["L1_ffn_lora_A"]
    d["lora_b"] = a["L1_ffn_lora_B"].reshape(E1 * RK, D)
    d["ffn_bias"] = np.concatenate([a["L1_ffn_base_b"], a["L1_ffn_router_b"], np.zeros(RK, np.float32)]).reshape(1, -1)
    return {n: np.ascontiguousarray(v) for n, v in d.items()}


def kernel(**inputs):
    import concourse.bacc as _bacc
    from concourse.bass_utils import run_bass_kernel_spmd as _run

    nc = _bacc.Bacc("TRN2", target_bir_lowering=False, num_devices=1)
    arrays = _layout({n: np.asarray(v) for n, v in inputs.items()})
    d = {n: nc.dram_tensor(f"in_{n}", v.shape, mybir.dt.from_np(v.dtype), kind="ExternalInput").ap() for n, v in arrays.items()}
    out = nc.dram_tensor("out", (B, T, D), F32, kind="ExternalOutput").ap()
    build(nc, d, out)
    r = _run(nc, [{f"in_{n}": v for n, v in arrays.items()}], core_ids=[0])
    return r.results[0]["out"]
```
